# Optimizing a Trainium2 kernel written in Bass

```python
import numpy as np
import jax
import jax.numpy as jnp

def _softmax(x, axis=-1):
    return jax.nn.softmax(x, axis=axis)

def _gelu(x):
    return jax.nn.gelu(x, approximate=True)

def _silu(x):
    return jax.nn.silu(x)

def _sigmoid(x):
    return jax.nn.sigmoid(x)

def _layernorm(x, axis=-1, eps=1e-05):
    m = jnp.mean(x, axis=axis, keepdims=True)
    v = jnp.var(x, axis=axis, keepdims=True)
    return (x - m) / jnp.sqrt(v + eps)

def _scatter_add(tgt, idx, src, axis=0):
    return tgt.at[idx].add(src)

def _segment_sum(src, seg, n):
    return jax.ops.segment_sum(src, seg, n)
kernel_name = 'mk_prb_d2_jaxref_r8_b4c649'

def setup_inputs(seed: int=0):
    np.random.seed(seed)
    _w = jnp.asarray

    def _L0_attn_setup():
        import jax, jax.numpy as jnp
        import numpy as np
        D_MODEL = 128
        N_HEADS = 16
        D_LATENT = 32
        HEAD_DIM = D_MODEL // N_HEADS

        def apply_rope(x):
            B, T, H, D = x.shape
            inv_freq = 1.0 / 10000.0 ** (jnp.arange(0, D, 2, dtype=jnp.float32) / D)
            t = jnp.arange(T, dtype=jnp.float32)
            freqs = t[:, None] * inv_freq[None, :]
            sin_f = jnp.sin(freqs)[None, :, None, :]
            cos_f = jnp.cos(freqs)[None, :, None, :]
            x1, x2 = jnp.split(x, 2, axis=-1)
            return jnp.concatenate([x1 * cos_f - x2 * sin_f, x1 * sin_f + x2 * cos_f], axis=-1)
        key = jax.random.key(seed)
        ks = jax.random.split(key, 10)
        B, T = (4, 512)
        s = lambda fan_in: 1.0 / np.sqrt(fan_in)
        return {'x': jax.random.normal(ks[0], (B, T, D_MODEL), dtype=jnp.float32), 'Wq': jax.random.normal(ks[1], (D_MODEL, D_MODEL), dtype=jnp.float32) * s(D_MODEL), 'bq': jnp.zeros((D_MODEL,), jnp.float32), 'Wdown': jax.random.normal(ks[2], (D_MODEL, D_LATENT), dtype=jnp.float32) * s(D_MODEL), 'bdown': jnp.zeros((D_LATENT,), jnp.float32), 'Wup': jax.random.normal(ks[3], (D_LATENT, 2 * D_MODEL), dtype=jnp.float32) * s(D_LATENT), 'bup': jnp.zeros((2 * D_MODEL,), jnp.float32), 'Wout': jax.random.normal(ks[4], (D_MODEL, D_MODEL), dtype=jnp.float32) * s(D_MODEL), 'bout': jnp.zeros((D_MODEL,), jnp.float32)}
    _L0_attn_in = _L0_attn_setup()

    def _L0_ffn_setup():
        import jax, jax.numpy as jnp
        import numpy as np
        B, S, H = (4, 256, 128)
        D = 256
        E = 8
        K = 2
        key = jax.random.key(seed)
        ks = jax.random.split(key, 8)
        w = lambda k, shape: jax.random.normal(k, shape, jnp.float32) * 0.02
        return {'hidden_states': jax.random.normal(ks[0], (B, S, H), jnp.float32), 'gate_w': w(ks[1], (H, E)), 'w_gate': w(ks[2], (E, H, D)), 'w_up': w(ks[3], (E, H, D)), 'w_down': w(ks[4], (E, D, H)), 'ws_gate': w(ks[5], (H, D)), 'ws_up': w(ks[6], (H, D)), 'ws_down': w(ks[7], (D, H))}
    _L0_ffn_in = _L0_ffn_setup()

    def _L1_attn_setup():
        import jax, jax.numpy as jnp
        import numpy as np
        EPS = 1e-05

        def _ln(x, g, b):
            m = jnp.mean(x, axis=-1, keepdims=True)
            v = jnp.mean((x - m) ** 2, axis=-1, keepdims=True)
            return (x - m) * jax.lax.rsqrt(v + EPS) * g + b

        def _forward(x, ln_attn_g, ln_attn_b, Wq, bq, Wk, bk, Wv, bv, ln_conv_g, ln_conv_b, conv_w, conv_b, ln_boom_g, ln_boom_b, Wb, bb, Wu, bu):
            B, S, D = x.shape
            K = conv_w.shape[-1]
            G = D // conv_w.shape[1]
            h = _ln(x, ln_conv_g, ln_conv_b)
            hc = jnp.transpose(h, (0, 2, 1))
            hc = jnp.pad(hc, ((0, 0), (0, 0), (K - 1, 0)))
            conv = jax.lax.conv_general_dilated(hc, conv_w, window_strides=(1,), padding='VALID', dimension_numbers=('NCH', 'OIH', 'NCH'), feature_group_count=G)
            conv = conv + conv_b[None, :, None]
            x = x + jnp.transpose(conv, (0, 2, 1))
            h = _ln(x, ln_attn_g, ln_attn_b)
            q = jnp.einsum('bsd,ed->bse', h, Wq) + bq
            k = jnp.einsum('bsd,ed->bse', h, Wk) + bk
            v = jnp.einsum('bsd,ed->bse', h, Wv) + bv
            scale = jnp.arange(1, S + 1, dtype=x.dtype)[None, :, None]
            pooled_q = jnp.cumsum(q, axis=1) / scale
            pooled_k = jnp.cumsum(pooled_q * k, axis=1) / scale
            x = x + pooled_k * v
            h = _ln(x, ln_boom_g, ln_boom_b)
            h = jax.nn.gelu(jnp.einsum('bsd,ed->bse', h, Wb) + bb, approximate=False)
            h = jnp.einsum('bse,de->bsd', h, Wu) + bu
            return x + h
        key = jax.random.key(seed)
        ks = jax.random.split(key, 8)
        B, S, D, K, G = (4, 256, 128, 4, 4)
        w = lambda k, shape: jax.random.normal(k, shape, jnp.float32) * 0.02
        return {'hidden_states': jax.random.normal(ks[0], (B, S, D), jnp.float32), 'attention_mask': jnp.ones((B, S), jnp.int32), 'ln_attn_g': jnp.ones((D,), jnp.float32), 'ln_attn_b': jnp.zeros((D,), jnp.float32), 'Wq': w(ks[1], (D, D)), 'bq': jnp.zeros((D,), jnp.float32), 'Wk': w(ks[2], (D, D)), 'bk': jnp.zeros((D,), jnp.float32), 'Wv': w(ks[3], (D, D)), 'bv': jnp.zeros((D,), jnp.float32), 'ln_conv_g': jnp.ones((D,), jnp.float32), 'ln_conv_b': jnp.zeros((D,), jnp.float32), 'conv_w': w(ks[4], (D, D // G, K)), 'conv_b': jnp.zeros((D,), jnp.float32), 'ln_boom_g': jnp.ones((D,), jnp.float32), 'ln_boom_b': jnp.zeros((D,), jnp.float32), 'Wb': w(ks[5], (4 * D, D)), 'bb': jnp.zeros((4 * D,), jnp.float32), 'Wu': w(ks[6], (D, 4 * D)), 'bu': jnp.zeros((D,), jnp.float32)}
    _L1_attn_in = _L1_attn_setup()

    def _L1_ffn_setup():
        import jax, jax.numpy as jnp
        import numpy as np
        B, S, D, E, F = (2, 128, 128, 14, 256)
        key = jax.random.key(seed)
        k0, k1, k2, k3 = jax.random.split(key, 4)
        h = jax.random.normal(k0, (B, S, D), jnp.float32)
        gate_w = jax.random.normal(k1, (E, D), jnp.float32) * 0.02
        w1 = jax.random.normal(k2, (E, D, F), jnp.float32) * (1.0 / np.sqrt(D).astype(np.float32))
        b1 = jnp.zeros((E, F), jnp.float32)
        w2 = jax.random.normal(k3, (E, F, D), jnp.float32) * (1.0 / np.sqrt(F).astype(np.float32))
        b2 = jnp.zeros((E, D), jnp.float32)
        return {'h': h, 'gate_w': gate_w, 'w1': w1, 'b1': b1, 'w2': w2, 'b2': b2}
    _L1_ffn_in = _L1_ffn_setup()
    _d = {'L0_attn_x': _L0_attn_in['x'], 'L0_attn_Wq': _L0_attn_in['Wq'], 'L0_attn_bq': _L0_attn_in['bq'], 'L0_attn_Wdown': _L0_attn_in['Wdown'], 'L0_attn_bdown': _L0_attn_in['bdown'], 'L0_attn_Wup': _L0_attn_in['Wup'], 'L0_attn_bup': _L0_attn_in['bup'], 'L0_attn_Wout': _L0_attn_in['Wout'], 'L0_attn_bout': _L0_attn_in['bout'], 'L0_ffn_gate_w': _L0_ffn_in['gate_w'], 'L0_ffn_w_gate': _L0_ffn_in['w_gate'], 'L0_ffn_w_up': _L0_ffn_in['w_up'], 'L0_ffn_w_down': _L0_ffn_in['w_down'], 'L0_ffn_ws_gate': _L0_ffn_in['ws_gate'], 'L0_ffn_ws_up': _L0_ffn_in['ws_up'], 'L0_ffn_ws_down': _L0_ffn_in['ws_down'], 'L1_attn_attention_mask': _L1_attn_in['attention_mask'], 'L1_attn_ln_attn_g': _L1_attn_in['ln_attn_g'], 'L1_attn_ln_attn_b': _L1_attn_in['ln_attn_b'], 'L1_attn_Wq': _L1_attn_in['Wq'], 'L1_attn_bq': _L1_attn_in['bq'], 'L1_attn_Wk': _L1_attn_in['Wk'], 'L1_attn_bk': _L1_attn_in['bk'], 'L1_attn_Wv': _L1_attn_in['Wv'], 'L1_attn_bv': _L1_attn_in['bv'], 'L1_attn_ln_conv_g': _L1_attn_in['ln_conv_g'], 'L1_attn_ln_conv_b': _L1_attn_in['ln_conv_b'], 'L1_attn_conv_w': _L1_attn_in['conv_w'], 'L1_attn_conv_b': _L1_attn_in['conv_b'], 'L1_attn_ln_boom_g': _L1_attn_in['ln_boom_g'], 'L1_attn_ln_boom_b': _L1_attn_in['ln_boom_b'], 'L1_attn_Wb': _L1_attn_in['Wb'], 'L1_attn_bb': _L1_attn_in['bb'], 'L1_attn_Wu': _L1_attn_in['Wu'], 'L1_attn_bu': _L1_attn_in['bu'], 'L1_ffn_gate_w': _L1_ffn_in['gate_w'], 'L1_ffn_w1': _L1_ffn_in['w1'], 'L1_ffn_b1': _L1_ffn_in['b1'], 'L1_ffn_w2': _L1_ffn_in['w2'], 'L1_ffn_b2': _L1_ffn_in['b2']}
    _x0 = _d['L0_attn_x']
    _d['L0_attn_x'] = jax.random.normal(jax.random.fold_in(jax.random.key(seed), 1), (32, 256, 128), dtype=_x0.dtype)
    del _x0
    return _d

def reference(L0_attn_x, L0_attn_Wq, L0_attn_bq, L0_attn_Wdown, L0_attn_bdown, L0_attn_Wup, L0_attn_bup, L0_attn_Wout, L0_attn_bout, L0_ffn_gate_w, L0_ffn_w_gate, L0_ffn_w_up, L0_ffn_w_down, L0_ffn_ws_gate, L0_ffn_ws_up, L0_ffn_ws_down, L1_attn_attention_mask, L1_attn_ln_attn_g, L1_attn_ln_attn_b, L1_attn_Wq, L1_attn_bq, L1_attn_Wk, L1_attn_bk, L1_attn_Wv, L1_attn_bv, L1_attn_ln_conv_g, L1_attn_ln_conv_b, L1_attn_conv_w, L1_attn_conv_b, L1_attn_ln_boom_g, L1_attn_ln_boom_b, L1_attn_Wb, L1_attn_bb, L1_attn_Wu, L1_attn_bu, L1_ffn_gate_w, L1_ffn_w1, L1_ffn_b1, L1_ffn_w2, L1_ffn_b2):

    def _L0_attn_ref(x, Wq, bq, Wdown, bdown, Wup, bup, Wout, bout):
        import jax, jax.numpy as jnp
        import numpy as np
        D_MODEL = 128
        N_HEADS = 16
        D_LATENT = 32
        HEAD_DIM = D_MODEL // N_HEADS

        def apply_rope(x):
            B, T, H, D = x.shape
            inv_freq = 1.0 / 10000.0 ** (jnp.arange(0, D, 2, dtype=jnp.float32) / D)
            t = jnp.arange(T, dtype=jnp.float32)
            freqs = t[:, None] * inv_freq[None, :]
            sin_f = jnp.sin(freqs)[None, :, None, :]
            cos_f = jnp.cos(freqs)[None, :, None, :]
            x1, x2 = jnp.split(x, 2, axis=-1)
            return jnp.concatenate([x1 * cos_f - x2 * sin_f, x1 * sin_f + x2 * cos_f], axis=-1)
        B, T, D = x.shape
        H, Dh = (N_HEADS, HEAD_DIM)
        q = x @ Wq + bq
        kv_latent = x @ Wdown + bdown
        kv = kv_latent @ Wup + bup
        q = q.reshape(B, T, H, Dh)
        kv = kv.reshape(B, T, H, 2 * Dh)
        k, v = jnp.split(kv, 2, axis=-1)
        q = apply_rope(q)
        k = apply_rope(k)
        att = jnp.einsum('bthd,btgd->bthg', q, k) / jnp.sqrt(jnp.float32(Dh))
        att = jax.nn.softmax(att, axis=-1)
        out = jnp.einsum('bthg,btgd->bthd', att, v)
        out = out.reshape(B, T, D)
        return out @ Wout + bout

    def _L0_ffn_ref(hidden_states, gate_w, w_gate, w_up, w_down, ws_gate, ws_up, ws_down):
        import jax, jax.numpy as jnp
        import numpy as np
        B, S, H = (4, 256, 128)
        D = 256
        E = 8
        K = 2
        b, s, h = hidden_states.shape
        x = hidden_states.reshape(-1, h)
        scores = jax.nn.softmax(x @ gate_w, axis=-1)
        topk_w, topk_idx = jax.lax.top_k(scores, K)
        topk_w = topk_w / (jnp.sum(topk_w, axis=-1, keepdims=True) + 1e-20)
        onehot = jax.nn.one_hot(topk_idx, E, dtype=x.dtype)
        w_per_expert = jnp.einsum('nke,nk->ne', onehot, topk_w)
        y = jnp.zeros_like(x)
        for e in range(E):
            hid = jax.nn.silu(x @ w_gate[e]) * (x @ w_up[e])
            y = y + w_per_expert[:, e:e + 1] * (hid @ w_down[e])
        shared = jax.nn.silu(x @ ws_gate) * (x @ ws_up) @ ws_down
        return (y + shared).reshape(b, s, h)

    def _L1_attn_ref(hidden_states, attention_mask, ln_attn_g, ln_attn_b, Wq, bq, Wk, bk, Wv, bv, ln_conv_g, ln_conv_b, conv_w, conv_b, ln_boom_g, ln_boom_b, Wb, bb, Wu, bu):
        import jax, jax.numpy as jnp
        import numpy as np
        EPS = 1e-05

        def _ln(x, g, b):
            m = jnp.mean(x, axis=-1, keepdims=True)
            v = jnp.mean((x - m) ** 2, axis=-1, keepdims=True)
            return (x - m) * jax.lax.rsqrt(v + EPS) * g + b

        def _forward(x, ln_attn_g, ln_attn_b, Wq, bq, Wk, bk, Wv, bv, ln_conv_g, ln_conv_b, conv_w, conv_b, ln_boom_g, ln_boom_b, Wb, bb, Wu, bu):
            B, S, D = x.shape
            K = conv_w.shape[-1]
            G = D // conv_w.shape[1]
            h = _ln(x, ln_conv_g, ln_conv_b)
            hc = jnp.transpose(h, (0, 2, 1))
            hc = jnp.pad(hc, ((0, 0), (0, 0), (K - 1, 0)))
            conv = jax.lax.conv_general_dilated(hc, conv_w, window_strides=(1,), padding='VALID', dimension_numbers=('NCH', 'OIH', 'NCH'), feature_group_count=G)
            conv = conv + conv_b[None, :, None]
            x = x + jnp.transpose(conv, (0, 2, 1))
            h = _ln(x, ln_attn_g, ln_attn_b)
            q = jnp.einsum('bsd,ed->bse', h, Wq) + bq
            k = jnp.einsum('bsd,ed->bse', h, Wk) + bk
            v = jnp.einsum('bsd,ed->bse', h, Wv) + bv
            scale = jnp.arange(1, S + 1, dtype=x.dtype)[None, :, None]
            pooled_q = jnp.cumsum(q, axis=1) / scale
            pooled_k = jnp.cumsum(pooled_q * k, axis=1) / scale
            x = x + pooled_k * v
            h = _ln(x, ln_boom_g, ln_boom_b)
            h = jax.nn.gelu(jnp.einsum('bsd,ed->bse', h, Wb) + bb, approximate=False)
            h = jnp.einsum('bse,de->bsd', h, Wu) + bu
            return x + h
        return _forward(hidden_states, ln_attn_g, ln_attn_b, Wq, bq, Wk, bk, Wv, bv, ln_conv_g, ln_conv_b, conv_w, conv_b, ln_boom_g, ln_boom_b, Wb, bb, Wu, bu)

    def _L1_ffn_ref(h, gate_w, w1, b1, w2, b2):
        import jax, jax.numpy as jnp
        import numpy as np
        B, S, D, E, F = (2, 128, 128, 14, 256)
        Bb, Ss, Dd = h.shape
        x = h.reshape(Bb * Ss, Dd)
        logits = x @ gate_w.T
        probs = jax.nn.softmax(logits, axis=-1)
        top2_p, top2_i = jax.lax.top_k(probs, 2)
        w = top2_p / jnp.maximum(top2_p.sum(-1, keepdims=True), 1e-10)
        hh = jnp.einsum('nd,edf->nef', x, w1) + b1
        hh = jax.nn.gelu(hh, approximate=False)
        all_out = jnp.einsum('nef,efd->ned', hh, w2) + b2
        n = jnp.arange(x.shape[0])
        out0 = all_out[n, top2_i[:, 0]]
        out1 = all_out[n, top2_i[:, 1]]
        moe_out = w[:, 0:1] * out0 + w[:, 1:2] * out1
        result = jnp.clip(x + moe_out, -100.0, 100.0).reshape(Bb, Ss, Dd)
        return result
    x = L0_attn_x
    xn = _layernorm(x, axis=-1)
    x = x + _L0_attn_ref(xn, L0_attn_Wq, L0_attn_bq, L0_attn_Wdown, L0_attn_bdown, L0_attn_Wup, L0_attn_bup, L0_attn_Wout, L0_attn_bout) + _L0_ffn_ref(xn, L0_ffn_gate_w, L0_ffn_w_gate, L0_ffn_w_up, L0_ffn_w_down, L0_ffn_ws_gate, L0_ffn_ws_up, L0_ffn_ws_down)
    xn = _layernorm(x, axis=-1)
    x = x + _L1_attn_ref(xn, L1_attn_attention_mask, L1_attn_ln_attn_g, L1_attn_ln_attn_b, L1_attn_Wq, L1_attn_bq, L1_attn_Wk, L1_attn_bk, L1_attn_Wv, L1_attn_bv, L1_attn_ln_conv_g, L1_attn_ln_conv_b, L1_attn_conv_w, L1_attn_conv_b, L1_attn_ln_boom_g, L1_attn_ln_boom_b, L1_attn_Wb, L1_attn_bb, L1_attn_Wu, L1_attn_bu) + _L1_ffn_ref(xn, L1_ffn_gate_w, L1_ffn_w1, L1_ffn_b1, L1_ffn_w2, L1_ffn_b2)
    return x

_drawn_inputs = setup_inputs


def setup_inputs(seed=0):
    import zlib

    import numpy as np

    out = dict(_drawn_inputs(seed))
    spreads = {'L0_attn_bq': (0.0, 0.346),
     'L0_attn_bdown': (0.0, 0.1),
     'L0_attn_bup': (0.0, 0.1),
     'L0_attn_bout': (0.0, 0.1),
     'L1_attn_ln_attn_g': (1.0, 0.6),
     'L1_attn_ln_attn_b': (0.0, 0.8),
     'L1_attn_bq': (0.0, 0.8),
     'L1_attn_bk': (0.0, 0.8),
     'L1_attn_bv': (0.0, 0.8),
     'L1_attn_ln_conv_g': (1.0, 0.6),
     'L1_attn_ln_conv_b': (0.0, 0.8),
     'L1_attn_conv_b': (0.0, 0.1),
     'L1_attn_ln_boom_g': (1.0, 0.6),
     'L1_attn_ln_boom_b': (0.0, 0.8),
     'L1_attn_bb': (0.0, 0.8),
     'L1_attn_bu': (0.0, 0.8),
     'L1_ffn_b1': (0.0, 1.825),
     'L1_ffn_b2': (0.0, 1.27)}
    factors = {'L0_ffn_gate_w': 5.014,
     'L0_ffn_w_gate': 4.576,
     'L0_ffn_w_up': 4.347,
     'L0_ffn_w_down': 4.412,
     'L0_ffn_ws_gate': 3.654,
     'L0_ffn_ws_up': 3.557,
     'L0_ffn_ws_down': 3.568,
     'L1_attn_Wq': 8.0,
     'L1_attn_Wk': 8.0,
     'L1_attn_Wv': 8.0,
     'L1_attn_Wb': 3.104,
     'L1_attn_Wu': 2.834}
    for name, (base, spread) in spreads.items():
        noise = np.random.default_rng([zlib.crc32(name.encode()), seed]).standard_normal(out[name].shape)
        drawn = base * np.exp(spread * noise) if base else spread * noise
        out[name] = jnp.asarray(drawn.astype(out[name].dtype))
    for name, factor in factors.items():
        out[name] = (out[name] * factor).astype(out[name].dtype)
    return out
```

```python
from contextlib import ExitStack

import numpy as np

import concourse.bass as bass
from concourse import mybir

FP32 = mybir.dt.float32
BF16 = mybir.dt.bfloat16
U32 = mybir.dt.uint32
ALU = mybir.AluOpType
ACT = mybir.ActivationFunctionType
AX = mybir.AxisListType

P = 128
D = 128
SEQ = 256
CHUNK = 512
TILES = CHUNK // P
SEQS = CHUNK // SEQ
H, DH = 16, 8
E0, F = 8, 256
HALVES = F // P
E1 = 14
TAPS = 4
LAT = 32
BOOM = 4
QKVG = 3 * D + E0
PART_ROWS = 65
EPS = 1e-5
SCALE = float(DH) ** -0.5

(C_GCONV, C_BCONV, C_GATTN, C_BATTN, C_GBOOM, C_BBOOM, C_BQ, C_BK, C_BV, C_BOUT, C_BU, C_BB) = range(12)
C_B1 = C_BB + BOOM
COLS = C_B1 + E1 * HALVES

S_WQ = 0
S_GATE0 = S_WQ + D
S_WOUT = S_GATE0 + E0
S_GATE1 = S_WOUT + D
S_CONV = S_GATE1 + E1
S_WQ1 = S_CONV + TAPS * D
S_WK1 = S_WQ1 + D
S_WV1 = S_WK1 + D
S_WB = S_WV1 + D
S_WU = S_WB + BOOM * D
S_ID = S_WU + BOOM * D
S_IOTA = S_ID + D
S_COUNT = S_IOTA + 16
S_END = S_COUNT + SEQ

N_WDOWN = 0
N_WUP = N_WDOWN + D
N_BDOWN = N_WUP + 2 * D
N_BUP = N_BDOWN + 1
N_BQ = N_BUP + 2 * D
N_CONVB = N_BQ + D
N_B2 = N_CONVB + D
N_END = N_B2 + D


def two_layers(nc, x, small, narrow, cols, pick0, pick1, wg0, wu0, wd0, w1, w2, out):
    tokens = x.shape[0]
    n_chunks = tokens // CHUNK
    all_tiles = tokens // P
    x_tiles = x.rearrange("(t p) d -> p t d", p=P)
    out_tiles = out.rearrange("(t p) d -> p t d", p=P)

    ctx = ExitStack()
    with ctx:
        def sb(name, shape, dt=FP32):
            return ctx.enter_context(nc.sbuf_tensor(name, shape, dt))

        def pb(name, shape, dt=FP32):
            return ctx.enter_context(nc.psum_tensor(name, shape, dt))

        def sem(name):
            return ctx.enter_context(nc.semaphore(name))

        x_all = sb("x_all", [P, all_tiles, D])
        sm = sb("sm", [P, S_END])
        nr = sb("nr", [LAT, N_END])
        cv = sb("cv", [P, COLS])
        wg0_sb = sb("wg0_sb", [P, E0 + 1, F])
        wu0_sb = sb("wu0_sb", [P, E0 + 1, F])
        wd0_sb = sb("wd0_sb", [P, E0 + 1, HALVES, D])
        w1_sb = sb("w1_sb", [P, E1, F])
        w2_sb = sb("w2_sb", [P, E1, HALVES, D])
        wqkvg = sb("wqkvg", [P, QKVG])
        bias_row = sb("bias_row", [1, 2, 512])
        bias_parts = sb("bias_parts", [PART_ROWS, 2, 512], BF16)
        ones_parts = sb("ones_parts", [PART_ROWS, P], BF16)
        mid_row = sb("mid_row", [1, 2, 512], BF16)
        ident = sm[:, S_ID:S_ID + D]
        ident_h = sb("ident_h", [P, P], BF16)
        sel0 = sb("sel0", [3 * E0, E0, P], BF16)
        sel1 = sb("sel1", [3 * E1, E1, P], BF16)
        inv_count = sb("inv_count", [P, SEQ])
        ones_f = sb("ones_f", [P, SEQ])
        neg_half = sb("neg_half", [P, TILES])
        eps = sb("eps", [P, TILES])
        idle = sb("idle", [P, 32])

        stats = sb("stats", [P, TILES, 6])
        mv = sb("mv", [P, TILES, 2])
        var_eps = sb("var_eps", [P, TILES])
        rstd = sb("rstd", [P, TILES])
        xn0 = sb("xn0", [P, TILES, D])
        xnT0 = sb("xnT0", [P, CHUNK])
        qkvg = sb("qkvg", [P, TILES, QKVG])
        prod = sb("prod", [P, H, H, DH])
        score = sb("score", [P, 2, H, H])
        prob = sb("prob", [P, 2, H, H])
        head_max = sb("head_max", [P, H])
        head_sum = sb("head_sum", [P, H])
        head_rec = sb("head_rec", [P, H])
        att = sb("att", [P, TILES, D])
        attT = sb("attT", [P, CHUNK])
        logit1 = sb("logit1", [P, TILES, E1])
        top8 = sb("top8", [P, TILES, 8])
        top8_at = sb("top8_at", [P, TILES, 8], U32)
        shift_all = sb("shift_all", [P, TILES, E1])
        shift_top = sb("shift_top", [P, TILES, 8])
        exp_all = sb("exp_all", [P, TILES, E1])
        exp_top = sb("exp_top", [P, TILES, 8])
        z_sum = sb("z_sum", [P, TILES])
        z_rec = sb("z_rec", [P, TILES])
        pair = sb("pair", [P, TILES, 2])
        pair_sum = sb("pair_sum", [P, TILES])
        pair_rec = sb("pair_rec", [P, TILES])
        pair_w = sb("pair_w", [P, TILES, 2])
        pair_at = sb("pair_at", [P, TILES, 2])
        hot = sb("hot", [P, 2, TILES, E1])
        w_tok = sb("w_tok", [P, TILES, E1])
        w_rest = sb("w_rest", [P, 2, TILES, E1])
        w_parts = sb("w_parts", [P, TILES, P], BF16)
        wT = sb("wT", [3 * E1, CHUNK], BF16)
        wT_f = sb("wT_f", [E1, CHUNK])
        xw = sb("xw", [P, CHUNK])
        silu = sb("silu", [P, 2, HALVES, CHUNK])
        hid = sb("hid", [P, HALVES, CHUNK])
        act1, hid1 = silu, hid
        sel_in = silu[:, :, :, :].rearrange("p a b n -> p (a b n)")
        sel_in0 = hid[:, :, :].rearrange("p b n -> p (b n)")
        yT = sb("yT", [P, CHUNK])
        xn1 = sb("xn1", [P, TILES, D])
        xnT1 = sb("xnT1", [P, CHUNK])
        z_tok = sb("z_tok", [P, TILES, D])
        convT = sb("convT", [P, SEQS, TAPS - 1 + SEQ])
        x2 = sb("x2", [P, TILES, D])
        hT = sb("hT", [P, CHUNK])
        qT = sb("qT", [P, CHUNK])
        scan = sb("scan", [P, CHUNK])
        pooled = sb("pooled", [P, CHUNK])
        gb = sb("gb", [P, BOOM, CHUNK])
        mlpT = sb("mlpT", [P, CHUNK])

        psY = pb("psY", [P, CHUNK])
        psE = pb("psE", [P, 4, CHUNK])
        psW = pb("psW", [P, CHUNK])
        psT = pb("psT", [P, CHUNK])
        psM = pb("psM", [P, CHUNK])
        psM_h = psM[:, 0:CHUNK // 2].bitcast(BF16)

        w_small = sem("w_small")
        w_layer0 = sem("w_layer0")
        w_layer1 = sem("w_layer1")
        x_loaded = sem("x_loaded")
        prep_pe = sem("prep_pe")
        prep_act = sem("prep_act")
        prep_dve = sem("prep_dve")
        prep_pool = sem("prep_pool")
        norm_stats = sem("norm_stats")
        norm_rstd = sem("norm_rstd")
        pool_step = sem("pool_step")
        dve_step = sem("dve_step")
        norm_out = sem("norm_out")
        psT_filled = sem("psT_filled")
        psT_read = sem("psT_read")
        qkvg_done = sem("qkvg_done")
        qkvg_read = sem("qkvg_read")
        shifted = sem("shifted")
        exped = sem("exped")
        parts_ready = sem("parts_ready")
        wT_done = sem("wT_done")
        wT_ready = sem("wT_ready")
        wb_done = sem("wb_done")
        xw_ready = sem("xw_ready")
        gate_done = sem("gate_done")
        silu_ready = sem("silu_ready")
        up_done = sem("up_done")
        hid_ready = sem("hid_ready")
        score_ready = sem("score_ready")
        prob_ready = sem("prob_ready")
        att_ready = sem("att_ready")
        y_done = sem("y_done")
        yT_ready = sem("yT_ready")
        logit_done = sem("logit_done")
        logit_read = sem("logit_read")
        conv_done = sem("conv_done")
        conv_read = sem("conv_read")
        q_done = sem("q_done")
        q_ready = sem("q_ready")
        k_done = sem("k_done")
        k_read = sem("k_read")
        v_done = sem("v_done")
        pkv_ready = sem("pkv_ready")
        boom_done = sem("boom_done")
        boom_ready = sem("boom_ready")
        mlp_done = sem("mlp_done")
        mlpT_ready = sem("mlpT_ready")
        up1_done = sem("up1_done")
        gelu_ready = sem("gelu_ready")
        hid1_ready = sem("hid1_ready")
        moe_done = sem("moe_done")
        moeT_ready = sem("moeT_ready")
        out_ready = sem("out_ready")
        out_sent = sem("out_sent")
        wTf_ready = sem("wTf_ready")
        sel_loaded = sem("sel_loaded")
        moe_tr = sem("moe_tr")

        SM_EXPERTS0 = [E0] + list(range(E0))
        NORMS = 5
        FILLS = 9
        DVE_STEPS = 62

        block = ctx.enter_context(nc.Block())

        @block.sync
        def _(sp):
            sp.dma_start(sm[:, :], small).then_inc(w_small, 16)
            sp.dma_start(nr[:, :], narrow).then_inc(w_small, 16)
            sp.dma_start(cv[:, :], cols).then_inc(w_small, 16)
            sp.dma_start(sel_in0[0:3 * E0, 0:E0 * P], pick0).then_inc(sel_loaded, 16)
            sp.dma_start(sel_in[0:3 * E1, 0:E1 * P], pick1).then_inc(sel_loaded, 16)
            sp.dma_start(x_all[:, 0:TILES, :], x_tiles[:, 0:TILES, :]).then_inc(x_loaded, 16)
            sp.dma_start(wg0_sb[:, :, :], wg0).then_inc(w_layer0, 16)
            sp.dma_start(wu0_sb[:, :, :], wu0).then_inc(w_layer0, 16)
            sp.dma_start(wd0_sb[:, :, :], wd0).then_inc(w_layer0, 16)
            sp.dma_start(w1_sb[:, :, :], w1).then_inc(w_layer1, 16)
            sp.dma_start(w2_sb[:, :, :], w2).then_inc(w_layer1, 16)
            with sp.Fori(1, n_chunks) as c:
                sp.wait_ge(x_loaded, c * 16)
                sp.dma_start(x_all[:, bass.ds(c * TILES, TILES), :],
                             x_tiles[:, bass.ds(c * TILES, TILES), :]).then_inc(x_loaded, 16)
            with sp.Fori(0, n_chunks) as c:
                sp.wait_ge(out_ready, c + 1)
                sp.dma_start(out_tiles[:, bass.ds(c * TILES, TILES), :],
                             x_all[:, bass.ds(c * TILES, TILES), :]).then_inc(out_sent, 16)
            sp.wait_ge(out_sent, 16 * n_chunks)

        @block.gpsimd
        def _(pool):
            nc.gpsimd.memset(neg_half[:, :], -0.5)
            nc.gpsimd.memset(eps[:, :], EPS)
            nc.gpsimd.memset(w_parts[:, :, :], 0.0)
            nc.gpsimd.memset(convT[:, :, 0:TAPS - 1], 0.0)
            nc.gpsimd.memset(bias_parts[:, :, :], 0.0)
            nc.gpsimd.memset(ones_parts[:, :], 1.0)
            nc.gpsimd.memset(ones_f[:, :], 1.0).then_inc(prep_pool, 1)
            pool.wait_ge(prep_pool, 1)
            with pool.Fori(0, n_chunks) as c:
                for n in range(NORMS):
                    pool.wait_ge(norm_stats, c * NORMS + n + 1)
                    nc.gpsimd.tensor_tensor(var_eps[:, :], mv[:, :, 1], eps[:, :], ALU.add).then_inc(pool_step, 1)
                    pool.wait_ge(pool_step, c * NORMS + n + 1)
                    nc.gpsimd.tensor_tensor(rstd[:, :], var_eps[:, :], neg_half[:, :], ALU.pow).then_inc(norm_rstd, 1)

        @block.tensor
        def _(pe):
            def transposes(src, c, n, ready, count):
                pe.wait_ge(ready, count)
                pe.wait_ge(psT_read, c * FILLS + n + 1)
                for t in range(TILES):
                    last = nc.tensor.transpose(psT[:, t * P:(t + 1) * P], src(t), ident)
                last.then_inc(psT_filled, 1)

            def wait_copied(c, n):
                pe.wait_ge(psT_read, c * FILLS + n + 2)

            pe.wait_ge(w_small, 48)
            nc.tensor.matmul(psM[:, 0:2 * D], nr[:, N_WDOWN:N_WDOWN + D], nr[:, N_WUP:N_WUP + 2 * D],
                             start=True, stop=True).then_inc(prep_pe, 1)
            nc.tensor.matmul(psW[0:1, 0:2 * D], nr[:, N_BDOWN:N_BDOWN + 1], nr[:, N_WUP:N_WUP + 2 * D],
                             start=True, stop=True).then_inc(prep_pe, 1)
            pe.wait_ge(prep_act, 1)
            pe.wait_ge(prep_dve, 1)

            with pe.Fori(0, n_chunks) as c:
                transposes(lambda t: xn0[:, t, :], c, 0, norm_out, c * NORMS + 1)
                wait_copied(c, 0)
                for t in range(TILES):
                    nc.tensor.matmul(psE[:, t, 0:QKVG], xnT0[:, t * P:(t + 1) * P], wqkvg[:, :],
                                     start=True, stop=False)
                    nc.tensor.matmul(psE[:, t, 0:QKVG], ones_parts[:, :], bias_parts[:, 0, 0:QKVG],
                                     start=False, stop=True).then_inc(qkvg_done, 1)

                pe.wait_ge(w_layer0, 48)
                pe.wait_ge(qkvg_read, (c + 1) * TILES)
                for j, e in enumerate(SM_EXPERTS0):
                    for f in range(HALVES):
                        if j:
                            pe.wait_ge(silu_ready, c * 18 + (j - 1) * HALVES + f + 1)
                        nc.tensor.matmul(psE[:, f, :], wg0_sb[:, e, f * P:(f + 1) * P], xnT0[:, :],
                                         start=True, stop=True).then_inc(gate_done, 1)
                    if j:
                        for f in range(HALVES):
                            pe.wait_ge(hid_ready, c * 18 + (j - 1) * HALVES + f + 1)
                            nc.tensor.matmul(psY[:, :], wd0_sb[:, SM_EXPERTS0[j - 1], f, :], hid[:, f, :],
                                             start=(j == 1 and f == 0), stop=False)
                        pe.wait_ge(xw_ready, c * E0 + j)
                    for f in range(HALVES):
                        src = xw if j else xnT0
                        nc.tensor.matmul(psE[:, 2 + f, :], wu0_sb[:, e, f * P:(f + 1) * P], src[:, :],
                                         start=True, stop=True).then_inc(up_done, 1)
                    if j == 0:
                        pe.wait_ge(parts_ready, c * 2 + 1)
                        for t in range(TILES):
                            last = nc.tensor.transpose(psM_h[0:3 * E0, t * P:(t + 1) * P],
                                                       w_parts[:, t, 0:3 * E0], ident_h[:, :])
                        last.then_inc(wT_done, 1)
                        pe.wait_ge(wT_ready, c * 2 + 1)
                    if j < E0:
                        nc.tensor.matmul(psW[:, :], sel0[:, j, :], wT[0:3 * E0, :],
                                         start=True, stop=True).then_inc(wb_done, 1)
                for f in range(HALVES):
                    pe.wait_ge(hid_ready, c * 18 + E0 * HALVES + f + 1)
                    nc.tensor.matmul(psY[:, :], wd0_sb[:, SM_EXPERTS0[E0], f, :], hid[:, f, :],
                                     start=False, stop=False)
                transposes(lambda t: att[:, t, :], c, 1, att_ready, c + 1)
                wait_copied(c, 1)
                nc.tensor.matmul(psY[:, :], sm[:, S_WOUT:S_WOUT + D], attT[:, :],
                                 start=False, stop=True).then_inc(y_done, 1)
                transposes(lambda t: yT[:, t * P:(t + 1) * P], c, 2, yT_ready, c + 1)

                transposes(lambda t: xn1[:, t, :], c, 3, norm_out, c * NORMS + 2)
                wait_copied(c, 3)
                for t in range(TILES):
                    last = nc.tensor.matmul(psW[:, t * E1:(t + 1) * E1], xnT1[:, t * P:(t + 1) * P],
                                            sm[:, S_GATE1:S_GATE1 + E1], start=True, stop=True)
                last.then_inc(logit_done, 1)
                transposes(lambda t: z_tok[:, t, :], c, 4, norm_out, c * NORMS + 3)
                pe.wait_ge(w_layer1, 32)

                def down1(j):
                    for f in range(HALVES):
                        pe.wait_ge(hid1_ready, c * E1 * HALVES + j * HALVES + f + 1)
                        nc.tensor.matmul(psY[:, :], w2_sb[:, j, f, :], hid1[:, f, :],
                                         start=(j == 0 and f == 0), stop=False)

                for j in range(E1):
                    for f in range(HALVES):
                        if j >= 2:
                            pe.wait_ge(gelu_ready, (c * E1 + j - 2) * HALVES + f + 1)
                        nc.tensor.matmul(psE[:, 2 * (j % 2) + f, :], w1_sb[:, j, f * P:(f + 1) * P],
                                         xnT1[:, :], start=True, stop=True).then_inc(up1_done, 1)
                    if j == 0:
                        pe.wait_ge(parts_ready, c * 2 + 2)
                        for t in range(TILES):
                            last = nc.tensor.transpose(psM_h[:, t * P:(t + 1) * P], w_parts[:, t, :], ident_h[:, :])
                        last.then_inc(wT_done, 1)
                        pe.wait_ge(wT_ready, c * 2 + 2)
                        for t in range(TILES):
                            last = nc.tensor.transpose(psM[0:E1, t * P:(t + 1) * P], w_tok[:, t, :], ident)
                        last.then_inc(wT_done, 1)
                        pe.wait_ge(logit_read, c + 1)
                    else:
                        down1(j - 1)
                    nc.tensor.matmul(psW[:, :], sel1[:, j, :], wT[:, :], start=True, stop=True)\
                        .then_inc(wb_done, 1)

                    if j == 1:
                        wait_copied(c, 4)
                        pe.wait_ge(wTf_ready, c + 1)
                        for t in range(TILES):
                            s, at = t // (SEQ // P), (t % (SEQ // P)) * P
                            for k in range(TAPS):
                                nc.tensor.matmul(psM[:, t * P:(t + 1) * P], convT[:, s, at + k:at + k + P],
                                                 sm[:, S_CONV + k * D:S_CONV + (k + 1) * D],
                                                 start=(k == 0), stop=False)
                            last = nc.tensor.matmul(psM[:, t * P:(t + 1) * P], ones_parts[:, :],
                                                    bias_parts[:, 1, 0:D], start=False, stop=True)
                        last.then_inc(conv_done, 1)
                    if j == 2:
                        transposes(lambda t: z_tok[:, t, :], c, 5, norm_out, c * NORMS + 4)
                    if j == 3:
                        wait_copied(c, 5)
                        pe.wait_ge(conv_read, c + 1)
                        nc.tensor.matmul(psM[:, :], sm[:, S_WQ1:S_WQ1 + D], hT[:, :],
                                         start=True, stop=True).then_inc(q_done, 1)
                        nc.tensor.matmul(psT[:, :], sm[:, S_WK1:S_WK1 + D], hT[:, :],
                                         start=True, stop=True).then_inc(k_done, 1)
                    if j == 4:
                        pe.wait_ge(q_ready, c + 1)
                        nc.tensor.matmul(psM[:, :], sm[:, S_WV1:S_WV1 + D], hT[:, :],
                                         start=True, stop=True).then_inc(v_done, 1)
                    if j == 5:
                        pe.wait_ge(k_read, c + 1)
                        transposes(lambda t: pooled[:, t * P:(t + 1) * P], c, 6, pkv_ready, c + 1)
                    if j == 6:
                        transposes(lambda t: z_tok[:, t, :], c, 7, norm_out, c * NORMS + 5)
                    if j in (7, 8):
                        wait_copied(c, 7)
                        for b, bank in ((2 * (j - 7), psM), (2 * (j - 7) + 1, psT)):
                            if b >= 2:
                                pe.wait_ge(boom_ready, c * BOOM + b - 1)
                            nc.tensor.matmul(bank[:, :], sm[:, S_WB + b * D:S_WB + (b + 1) * D], hT[:, :],
                                             start=True, stop=True).then_inc(boom_done, 1)
                    if j == 9:
                        pe.wait_ge(boom_ready, (c + 1) * BOOM)
                        for b in range(BOOM):
                            last = nc.tensor.matmul(psM[:, :], sm[:, S_WU + b * D:S_WU + (b + 1) * D],
                                                    gb[:, b, :], start=(b == 0), stop=(b == BOOM - 1))
                        last.then_inc(mlp_done, 1)
                    if j == 10:
                        transposes(lambda t: mlpT[:, t * P:(t + 1) * P], c, 8, mlpT_ready, c + 1)
                down1(E1 - 1)
                nc.tensor.matmul(psY[:, :], nr[0:E1, N_B2:N_B2 + D], wT_f[:, :], start=False, stop=True)\
                    .then_inc(moe_done, 1)
                pe.wait_ge(moeT_ready, c + 1)
                for t in range(TILES):
                    last = nc.tensor.transpose(psM[:, t * P:(t + 1) * P], yT[:, t * P:(t + 1) * P], ident)
                last.then_inc(moe_tr, 1)
                pe.wait_ge(out_ready, c + 1)

        @block.scalar
        def _(act):
            act.wait_ge(prep_pe, 1)
            nc.scalar.copy(wqkvg[:, D:3 * D], psM[:, 0:2 * D])
            nc.scalar.copy(wqkvg[:, 0:D], sm[:, S_WQ:S_WQ + D])
            nc.scalar.copy(wqkvg[:, 3 * D:QKVG], sm[:, S_GATE0:S_GATE0 + E0]).then_inc(prep_act, 1)
            act.sem_inc(psT_read, 1)

            def col(n):
                return cv[:, n:n + 1]

            def copy_out(c, n, dst, scale=None, bias=None):
                act.wait_ge(psT_filled, c * FILLS + n + 1)
                if scale is None:
                    nc.scalar.copy(dst, psT[:, :]).then_inc(psT_read, 1)
                else:
                    nc.scalar.activation(dst, psT[:, :], ACT.Identity, scale=scale, bias=bias)\
                        .then_inc(psT_read, 1)

            def route_exps(c, n, e):
                act.wait_ge(shifted, c * 2 + n)
                nc.scalar.activation(exp_all[:, :, 0:e], shift_all[:, :, 0:e], ACT.Exp)
                nc.scalar.activation(exp_top[:, :, :], shift_top[:, :, :], ACT.Exp).then_inc(exped, 1)

            with act.Fori(0, n_chunks) as c:
                copy_out(c, 0, xnT0[:, :])
                for t in range(TILES):
                    act.wait_ge(qkvg_done, c * TILES + t + 1)
                    nc.scalar.copy(qkvg[:, t, :], psE[:, t, 0:QKVG]).then_inc(qkvg_read, 1)
                route_exps(c, 1, E0)
                exp_after = {1: 0, 2: 1, 4: 2, 6: 3}
                for j in range(E0 + 1):
                    for f in range(HALVES):
                        act.wait_ge(gate_done, c * 18 + j * HALVES + f + 1)
                        nc.scalar.activation(silu[:, j % 2, f, :], psE[:, f, :], ACT.Silu).then_inc(silu_ready, 1)
                    if j == 0:
                        act.wait_ge(wT_done, c * 3 + 1)
                        nc.scalar.copy(wT[0:3 * E0, :], psM_h[0:3 * E0, :]).then_inc(wT_ready, 1)
                    if j in exp_after:
                        t = exp_after[j]
                        act.wait_ge(score_ready, c * TILES + t + 1)
                        nc.scalar.activation(prob[:, t % 2], score[:, t % 2], ACT.Exp, scale=SCALE)\
                            .then_inc(prob_ready, 1)
                copy_out(c, 1, attT[:, :])
                act.wait_ge(y_done, c + 1)
                nc.scalar.activation(yT[:, :], psY[:, :], ACT.Identity, bias=col(C_BOUT)).then_inc(yT_ready, 1)

                copy_out(c, 3, xnT1[:, :])
                act.wait_ge(psT_filled, c * FILLS + 5)
                for s in range(SEQS):
                    last = nc.scalar.activation(convT[:, s, TAPS - 1:], psT[:, s * SEQ:(s + 1) * SEQ], ACT.Identity,
                                                scale=col(C_GCONV), bias=col(C_BCONV))
                last.then_inc(psT_read, 1)
                route_exps(c, 2, E1)
                act.wait_ge(wT_done, c * 3 + 2)
                nc.scalar.copy(wT[:, :], psM_h[0:3 * E1, :]).then_inc(wT_ready, 1)
                act.wait_ge(wT_done, c * 3 + 3)
                nc.scalar.copy(wT_f[:, :], psM[0:E1, :]).then_inc(wTf_ready, 1)
                for j in range(E1):
                    for f in range(HALVES):
                        act.wait_ge(up1_done, (c * E1 + j) * HALVES + f + 1)
                        nc.scalar.activation(act1[:, j % 2, f, :], psE[:, 2 * (j % 2) + f, :], ACT.Gelu,
                                             bias=col(C_B1 + j * HALVES + f)).then_inc(gelu_ready, 1)
                    if j == 2:
                        copy_out(c, 5, hT[:, :], col(C_GATTN), col(C_BATTN))
                    if j == 3:
                        act.wait_ge(q_done, c + 1)
                        nc.scalar.activation(qT[:, :], psM[:, :], ACT.Identity, bias=col(C_BQ)).then_inc(q_ready, 1)
                    if j == 6:
                        copy_out(c, 7, hT[:, :], col(C_GBOOM), col(C_BBOOM))
                    if j in (7, 8):
                        for b, bank in ((2 * (j - 7), psM), (2 * (j - 7) + 1, psT)):
                            act.wait_ge(boom_done, c * BOOM + b + 1)
                            nc.scalar.activation(gb[:, b, :], bank[:, :], ACT.Gelu, bias=col(C_BB + b))\
                                .then_inc(boom_ready, 1)
                    if j == 9:
                        act.wait_ge(mlp_done, c + 1)
                        nc.scalar.activation(mlpT[:, :], psM[:, :], ACT.Identity, bias=col(C_BU))\
                            .then_inc(mlpT_ready, 1)
                act.wait_ge(moe_done, c + 1)
                nc.scalar.copy(yT[:, :], psY[:, :]).then_inc(moeT_ready, 1)

        @block.vector
        def _(dve):
            v = nc.vector
            steps = [0]

            def prep(ins):
                steps[0] += 1
                ins.then_inc(dve_step, 1)
                dve.wait_ge(dve_step, steps[0])

            dve.wait_ge(w_small, 48)
            dve.wait_ge(sel_loaded, 32)
            v.tensor_copy(sel0[:, :, :], sel_in0[0:3 * E0, 0:E0 * P].rearrange("p (e m) -> p e m", m=P))
            v.tensor_copy(sel1[:, :, :], sel_in[0:3 * E1, 0:E1 * P].rearrange("p (e m) -> p e m", m=P))
            v.tensor_copy(ident_h[:, :], ident)
            v.reciprocal(inv_count[:, :], sm[:, S_COUNT:S_COUNT + SEQ])
            prep(v.memset(bias_row[:, :, :], 0.0))
            dve.wait_ge(prep_pe, 2)
            dve.wait_ge(prep_pool, 1)
            v.tensor_copy(bias_row[:, 0, 0:D], nr[0:1, N_BQ:N_BQ + D])
            v.tensor_copy(bias_row[:, 1, 0:D], nr[0:1, N_CONVB:N_CONVB + D])
            prep(v.tensor_tensor(bias_row[:, 0, D:3 * D], psW[0:1, 0:2 * D], nr[0:1, N_BUP:N_BUP + 2 * D], ALU.add))
            prep(v.tensor_copy(bias_parts[0:1, :, :], bias_row[:, :, :]))
            prep(v.tensor_tensor(bias_row[:, :, :], bias_row[:, :, :], bias_parts[0:1, :, :], ALU.subtract))
            prep(v.tensor_copy(mid_row[:, :, :], bias_row[:, :, :]))
            v.tensor_copy(bias_parts[32:33, :, :], mid_row[:, :, :])
            prep(v.tensor_tensor(bias_row[:, :, :], bias_row[:, :, :], mid_row[:, :, :], ALU.subtract))
            v.tensor_copy(bias_parts[64:65, :, :], bias_row[:, :, :]).then_inc(prep_dve, 1)
            base = steps[0]

            with dve.Fori(0, n_chunks) as c:
                steps[0] = 0
                alone = [0]

                x_now = x_all[:, bass.ds(c * TILES, TILES), :]

                def wait_alone(semaphore, value):
                    dve.wait_ge(semaphore, value)
                    v.memset(idle[:, alone[0]:alone[0] + 1], 0.0)
                    alone[0] += 1

                def link(ins, alone=False):
                    steps[0] += 1
                    ins.then_inc(dve_step, 1)
                    if alone:
                        wait_alone(dve_step, c * DVE_STEPS + base + steps[0])
                    else:
                        dve.wait_ge(dve_step, c * DVE_STEPS + base + steps[0])

                def norm(n, src, dst):
                    for t in range(TILES):
                        last = v.bn_stats(stats[:, t, :], src(t))
                    link(last, alone=True)
                    for t in range(TILES):
                        last = v.bn_aggr(mv[:, t, :], stats[:, t, :])
                    last.then_inc(norm_stats, 1)
                    dve.wait_ge(norm_rstd, c * NORMS + n + 1)
                    for t in range(TILES):
                        last = v.tensor_scalar(dst[:, t, :], src(t), mv[:, t, 0:1], rstd[:, t:t + 1],
                                               ALU.subtract, ALU.mult)
                    last.then_inc(norm_out, 1)
                    wait_alone(norm_out, c * NORMS + n + 1)

                def route(n, e, logits, floor_op, floor):
                    def wide(a, k=e):
                        return a.unsqueeze(2).to_broadcast([P, TILES, k])
                    for t in range(TILES):
                        last = v.max(top8[:, t, :], logits(t))
                    link(last, alone=True)
                    for t in range(TILES):
                        v.max_index(top8_at[:, t, :], top8[:, t, :], logits(t))
                    for t in range(TILES):
                        v.tensor_scalar(shift_all[:, t, 0:e], logits(t), top8[:, t, 0:1], None, ALU.subtract)
                    v.tensor_tensor(shift_top[:, :, :], top8[:, :, :], top8[:, :, 0:1].to_broadcast([P, TILES, 8]),
                                    ALU.subtract).then_inc(shifted, 1)
                    dve.wait_ge(shifted, c * 2 + n)
                    link(v.tensor_copy(pair_at[:, :, :], top8_at[:, :, 0:2]))
                    iota = sm[:, S_IOTA:S_IOTA + e].unsqueeze(1).to_broadcast([P, TILES, e])
                    for s in range(2):
                        v.tensor_tensor(hot[:, s, :, 0:e], iota, pair_at[:, :, s:s + 1].to_broadcast([P, TILES, e]),
                                        ALU.is_equal)
                    dve.wait_ge(exped, c * 2 + n)
                    link(v.reduce_sum(z_sum[:, :], exp_all[:, :, 0:e], axis=AX.X))
                    link(v.reciprocal(z_rec[:, :], z_sum[:, :]))
                    link(v.tensor_tensor(pair[:, :, :], exp_top[:, :, 0:2], wide(z_rec[:, :], 2), ALU.mult))
                    link(v.reduce_sum(pair_sum[:, :], pair[:, :, :], axis=AX.X))
                    link(v.tensor_scalar(pair_sum[:, :], pair_sum[:, :], floor, None, floor_op))
                    link(v.reciprocal(pair_rec[:, :], pair_sum[:, :]))
                    link(v.tensor_tensor(pair_w[:, :, :], pair[:, :, :], wide(pair_rec[:, :], 2), ALU.mult))
                    for s in range(2):
                        last = v.tensor_tensor(hot[:, s, :, 0:e], hot[:, s, :, 0:e],
                                               pair_w[:, :, s:s + 1].to_broadcast([P, TILES, e]), ALU.mult)
                    link(last)
                    link(v.tensor_tensor(w_tok[:, :, 0:e], hot[:, 0, :, 0:e], hot[:, 1, :, 0:e], ALU.add))
                    link(v.tensor_copy(w_parts[:, :, 0:e], w_tok[:, :, 0:e]))
                    link(v.tensor_tensor(w_rest[:, 0, :, 0:e], w_tok[:, :, 0:e], w_parts[:, :, 0:e], ALU.subtract))
                    link(v.tensor_copy(w_parts[:, :, e:2 * e], w_rest[:, 0, :, 0:e]))
                    link(v.tensor_tensor(w_rest[:, 1, :, 0:e], w_rest[:, 0, :, 0:e], w_parts[:, :, e:2 * e],
                                         ALU.subtract))
                    v.tensor_copy(w_parts[:, :, 2 * e:3 * e], w_rest[:, 1, :, 0:e]).then_inc(parts_ready, 1)

                def scores(t):
                    q = qkvg[:, t, 0:D].rearrange("p (h d) -> p h d", d=DH).unsqueeze(2).to_broadcast([P, H, H, DH])
                    k = qkvg[:, t, D:2 * D].rearrange("p (g d) -> p g d", d=DH).unsqueeze(1).to_broadcast([P, H, H, DH])
                    link(v.tensor_tensor(prod[:, :, :, :], q, k, ALU.mult))
                    link(v.reduce_sum(score[:, t % 2], prod[:, :, :, :], axis=AX.X))
                    link(v.reduce_max(head_max[:, :], score[:, t % 2], axis=AX.X))
                    v.tensor_tensor(score[:, t % 2], score[:, t % 2],
                                    head_max[:, :].unsqueeze(2).to_broadcast([P, H, H]), ALU.subtract)\
                        .then_inc(score_ready, 1)

                def mix(t):
                    dve.wait_ge(prob_ready, c * TILES + t + 1)
                    v.reduce_sum(head_sum[:, :], prob[:, t % 2], axis=AX.X)
                    p = prob[:, t % 2].unsqueeze(2).to_broadcast([P, H, DH, H])
                    w = qkvg[:, t, 2 * D:3 * D].rearrange("p (d g) -> p d g", g=H).unsqueeze(1)\
                        .to_broadcast([P, H, DH, H])
                    prod_v = prod[:, :, :, :].rearrange("p h g d -> p (h g d)").rearrange("p (h d g) -> p h d g", d=DH, g=H)
                    link(v.tensor_tensor(prod_v, p, w, ALU.mult))
                    v.reciprocal(head_rec[:, :], head_sum[:, :])
                    link(v.reduce_sum(att[:, t, :].rearrange("p (h d) -> p h d", d=DH), prod_v, axis=AX.X))
                    out_t = att[:, t, :].rearrange("p (h d) -> p h d", d=DH)
                    last = v.tensor_tensor(out_t, out_t, head_rec[:, :].unsqueeze(2).to_broadcast([P, H, DH]), ALU.mult)
                    if t == TILES - 1:
                        last.then_inc(att_ready, 1)

                wait_alone(x_loaded, c * 16 + 16)
                norm(0, lambda t: x_all[:, bass.ds(c * TILES + t, 1), :], xn0)
                wait_alone(qkvg_read, (c + 1) * TILES)
                route(1, E0, lambda t: qkvg[:, t, 3 * D:QKVG], ALU.add, 1e-20)
                pieces = [(scores, 0), (scores, 1), (mix, 0), (scores, 2), (mix, 1), (scores, 3), (mix, 2), (mix, 3)]
                for j in range(E0 + 1):
                    for f in range(HALVES):
                        dve.wait_ge(silu_ready, c * 18 + j * HALVES + f + 1)
                        dve.wait_ge(up_done, c * 18 + j * HALVES + f + 1)
                        v.tensor_tensor(hid[:, f, :], silu[:, j % 2, f, :], psE[:, 2 + f, :], ALU.mult)\
                            .then_inc(hid_ready, 1)
                    if j < E0:
                        dve.wait_ge(wb_done, c * (E0 + E1) + j + 1)
                        v.tensor_tensor(xw[:, :], xnT0[:, :], psW[:, :], ALU.mult).then_inc(xw_ready, 1)
                        piece, t = pieces[j]
                        piece(t)

                dve.wait_ge(psT_filled, c * FILLS + 3)
                v.tensor_tensor(x_now, x_now, psT[:, :].rearrange("p (t d) -> p t d", d=D), ALU.add)\
                    .then_inc(psT_read, 1)
                wait_alone(psT_read, c * FILLS + 4)
                norm(1, lambda t: x_all[:, bass.ds(c * TILES + t, 1), :], xn1)
                norm(2, lambda t: xn1[:, t, :], z_tok)
                dve.wait_ge(logit_done, c + 1)
                v.tensor_copy(logit1[:, :, :], psW[:, 0:TILES * E1].rearrange("p (t e) -> p t e", e=E1))\
                    .then_inc(logit_read, 1)
                wait_alone(logit_read, c + 1)
                route(2, E1, lambda t: logit1[:, t, :], ALU.max, 1e-10)

                def pool_scan(src):
                    for s in range(SEQS):
                        seq = slice(s * SEQ, (s + 1) * SEQ)
                        last = v.tensor_tensor_scan(scan[:, seq], ones_f[:, :], src[:, seq], 0.0, ALU.mult, ALU.add)
                    link(last)
                    link(v.tensor_tensor(pooled[:, :].rearrange("p (s n) -> p s n", n=SEQ),
                                         scan[:, :].rearrange("p (s n) -> p s n", n=SEQ),
                                         inv_count[:, :].unsqueeze(1).to_broadcast([P, SEQS, SEQ]), ALU.mult))

                for j in range(E1):
                    for f in range(HALVES):
                        dve.wait_ge(wb_done, c * (E0 + E1) + E0 + j + 1)
                        dve.wait_ge(gelu_ready, (c * E1 + j) * HALVES + f + 1)
                        v.tensor_tensor(hid1[:, f, :], act1[:, j % 2, f, :], psW[:, :], ALU.mult)\
                            .then_inc(hid1_ready, 1)
                    if j == 1:
                        dve.wait_ge(conv_done, c + 1)
                        v.tensor_tensor(x2[:, :, :], xn1[:, :, :], psM[:, :].rearrange("p (t d) -> p t d", d=D),
                                        ALU.add).then_inc(conv_read, 1)
                        wait_alone(conv_read, c + 1)
                        norm(3, lambda t: x2[:, t, :], z_tok)
                    if j == 3:
                        dve.wait_ge(q_ready, c + 1)
                        pool_scan(qT)
                    if j == 4:
                        dve.wait_ge(k_done, c + 1)
                        v.scalar_tensor_tensor(qT[:, :], psT[:, :], cv[:, C_BK:C_BK + 1], pooled[:, :],
                                               ALU.add, ALU.mult).then_inc(k_read, 1)
                        dve.wait_ge(k_read, c + 1)
                        pool_scan(qT)
                        dve.wait_ge(v_done, c + 1)
                        v.scalar_tensor_tensor(pooled[:, :], psM[:, :], cv[:, C_BV:C_BV + 1], pooled[:, :],
                                               ALU.add, ALU.mult).then_inc(pkv_ready, 1)
                    if j == 5:
                        dve.wait_ge(psT_filled, c * FILLS + 7)
                        v.tensor_tensor(x2[:, :, :], x2[:, :, :], psT[:, :].rearrange("p (t d) -> p t d", d=D),
                                        ALU.add).then_inc(psT_read, 1)
                        wait_alone(psT_read, c * FILLS + 8)
                        norm(4, lambda t: x2[:, t, :], z_tok)
                    if j == 10:
                        dve.wait_ge(psT_filled, c * FILLS + 9)
                        v.tensor_tensor(x2[:, :, :], x2[:, :, :], psT[:, :].rearrange("p (t d) -> p t d", d=D),
                                        ALU.add).then_inc(psT_read, 1)
                        dve.wait_ge(psT_read, c * FILLS + 10)
                        link(v.tensor_tensor(x_now, x_now, x2[:, :, :], ALU.add))
                dve.wait_ge(moe_tr, c + 1)
                link(v.tensor_tensor(z_tok[:, :, :], xn1[:, :, :], psM[:, :].rearrange("p (t d) -> p t d", d=D), ALU.add))
                link(v.tensor_scalar(z_tok[:, :, :], z_tok[:, :, :], -100.0, 100.0, ALU.max, ALU.min))
                v.tensor_tensor(x_now, x_now, z_tok[:, :, :], ALU.add).then_inc(out_ready, 1)
                assert steps[0] == DVE_STEPS, steps[0]


def _packs(a):
    f32 = np.float32
    g = {k: np.asarray(v) for k, v in a.items()}
    small = np.zeros((P, S_END), f32)

    def put(at, m):
        small[:m.shape[0], at:at + m.shape[1]] = m

    put(S_WQ, g["L0_attn_Wq"])
    put(S_GATE0, g["L0_ffn_gate_w"])
    put(S_WOUT, g["L0_attn_Wout"])
    put(S_GATE1, g["L1_ffn_gate_w"].T)
    conv = g["L1_attn_conv_w"]
    width = conv.shape[1]
    for k in range(TAPS):
        for o in range(D // width):
            small[o * width:(o + 1) * width, S_CONV + k * D + o * width:S_CONV + k * D + (o + 1) * width] = \
                conv[o * width:(o + 1) * width, :, k].T
    put(S_WQ1, g["L1_attn_Wq"].T)
    put(S_WK1, g["L1_attn_Wk"].T)
    put(S_WV1, g["L1_attn_Wv"].T)
    put(S_WB, g["L1_attn_Wb"].T)
    put(S_WU, g["L1_attn_Wu"].T.reshape(BOOM, P, D).transpose(1, 0, 2).reshape(P, BOOM * D))
    put(S_ID, np.eye(P, dtype=f32))
    put(S_IOTA, np.tile(np.arange(16, dtype=f32), (P, 1)))
    put(S_COUNT, np.tile(np.arange(1, SEQ + 1, dtype=f32), (P, 1)))

    narrow = np.zeros((LAT, N_END), f32)

    def kv_order(m):
        m = m.reshape(m.shape[0], H, 2, DH)
        return np.concatenate([m[:, :, 0].reshape(-1, D), m[:, :, 1].transpose(0, 2, 1).reshape(-1, D)], axis=1)

    narrow[:, N_WDOWN:N_WDOWN + D] = g["L0_attn_Wdown"].T
    narrow[:, N_WUP:N_WUP + 2 * D] = kv_order(g["L0_attn_Wup"])
    narrow[:, N_BDOWN] = g["L0_attn_bdown"]
    narrow[0, N_BUP:N_BUP + 2 * D] = kv_order(g["L0_attn_bup"][None])[0]
    narrow[0, N_BQ:N_BQ + D] = g["L0_attn_bq"]
    narrow[0, N_CONVB:N_CONVB + D] = g["L1_attn_conv_b"]
    narrow[0:E1, N_B2:N_B2 + D] = g["L1_ffn_b2"]

    cols = np.stack(
        [g["L1_attn_" + n] for n in ("ln_conv_g", "ln_conv_b", "ln_attn_g", "ln_attn_b", "ln_boom_g", "ln_boom_b",
                                     "bq", "bk", "bv")]
        + [g["L0_attn_bout"], g["L1_attn_bu"]] + list(g["L1_attn_bb"].reshape(BOOM, P))
        + list(g["L1_ffn_b1"].reshape(E1 * HALVES, P)), axis=1)

    def with_shared(e, s):
        return np.concatenate([g[e], g[s][None]], axis=0)

    def halves(m):
        return m.reshape(m.shape[0], HALVES, P, D).transpose(2, 0, 1, 3)

    return {
        "x": g["L0_attn_x"].reshape(-1, D),
        "small": small,
        "narrow": narrow,
        "cols": cols,
        "pick0": np.repeat(np.tile(np.eye(E0, dtype=f32), (3, 1)), P, axis=1),
        "pick1": np.repeat(np.tile(np.eye(E1, dtype=f32), (3, 1)), P, axis=1),
        "wg0": with_shared("L0_ffn_w_gate", "L0_ffn_ws_gate").transpose(1, 0, 2),
        "wu0": with_shared("L0_ffn_w_up", "L0_ffn_ws_up").transpose(1, 0, 2),
        "wd0": halves(with_shared("L0_ffn_w_down", "L0_ffn_ws_down")),
        "w1": g["L1_ffn_w1"].transpose(1, 0, 2),
        "w2": halves(g["L1_ffn_w2"]),
    }


def kernel(**inputs):
    import concourse.bacc as _bacc
    from concourse.bass_utils import run_bass_kernel_spmd as _run

    shape = np.asarray(inputs["L0_attn_x"]).shape
    arrays = {k: np.ascontiguousarray(v) for k, v in _packs(inputs).items()}
    nc = _bacc.Bacc("TRN2", target_bir_lowering=False, num_devices=1)
    args = {k: nc.dram_tensor(k, a.shape, mybir.dt.from_np(a.dtype), kind="ExternalInput").ap()
            for k, a in arrays.items()}
    out = nc.dram_tensor("out", arrays["x"].shape, FP32, kind="ExternalOutput").ap()
    two_layers(nc, **args, out=out)
    r = _run(nc, [arrays], core_ids=[0])
    return r.results[0]["out"].reshape(shape)
```

```python
from contextlib import ExitStack

import numpy as np

import concourse.bass as bass
from concourse import mybir

FP32 = mybir.dt.float32
BF16 = mybir.dt.bfloat16
U32 = mybir.dt.uint32
I32 = mybir.dt.int32
ALU = mybir.AluOpType
ACT = mybir.ActivationFunctionType
AX = mybir.AxisListType

P = 128
D = 128
SEQ = 256
CHUNK = 512
TILES = CHUNK // P
SEQS = CHUNK // SEQ
TOKENS = 32 * SEQ
ALL_TILES = TOKENS // P
CHUNKS = TOKENS // CHUNK
GROUP = 16
GROUPS = ALL_TILES // GROUP
H, DH = 16, 8
E0, F = 8, 256
HALVES = F // P
E1 = 14
EXPERTS = (E0, E1)
TAPS = 4
LAT = 32
BOOM = 4
QKV = 3 * D
PART_ROWS = 65
EPS = 1e-5
ROOT_GUESS = float(0x5F3759DF)
ROOT_STEPS = 3
ROOT_LINKS = 2 + 3 * ROOT_STEPS
SCALE = float(DH) ** -0.5
BIG = 3e38

LOAD = 4
RING = 3
STEP_BLOCKS = LOAD * RING
BLOCKS = -(-(2 * ALL_TILES + E1 - 1) // STEP_BLOCKS) * STEP_BLOCKS
PASSES = BLOCKS // STEP_BLOCKS
SLOTS = BLOCKS * P
ZERO_ROWS = 8
BLOCK_PAIRS = range(2, 6)
PAIR_BLOCKS = BLOCKS // len(BLOCK_PAIRS)
assert PAIR_BLOCKS * len(BLOCK_PAIRS) == BLOCKS and PAIR_BLOCKS % STEP_BLOCKS == 0
ATT_BEATS = (1, 1, 1, 1, 1, 1, 1, 4, 2, 5)
CHAIN_BEATS = (4, 2, 6, 2, 2, 6, 6, 2, 4, 2)
LATE_MIXES = (0, 3, 6, 9, 12, 13)
assert 2 * sum(ATT_BEATS) == PAIR_BLOCKS and sum(CHAIN_BEATS) == PAIR_BLOCKS

(C_GCONV, C_BCONV, C_GATTN, C_BATTN, C_GBOOM, C_BBOOM, C_BQ, C_BK, C_BV, C_BOUT, C_BU, C_BB) = range(12)
COLS = C_BB + BOOM

S_WQ = 0
S_GATE0 = S_WQ + D
S_WOUT = S_GATE0 + E0
S_GATE1 = S_WOUT + D
S_CONV = S_GATE1 + E1
S_WQ1 = S_CONV + TAPS * D
S_WK1 = S_WQ1 + D
S_WV1 = S_WK1 + D
S_WB = S_WV1 + D
S_WU = S_WB + BOOM * D
S_ID = S_WU + BOOM * D
S_IOTA = S_ID + D
S_COUNT = S_IOTA + BLOCKS
S_BEFORE = S_COUNT + SEQ
S_END = S_BEFORE + P

N_WDOWN = 0
N_WUP = N_WDOWN + D
N_BDOWN = N_WUP + 2 * D
N_BUP = N_BDOWN + 1
N_BQ = N_BUP + 2 * D
N_CONVB = N_BQ + D
N_B12 = N_CONVB + D
N_END = N_B12 + F + D


class Links:

    def __init__(self, engine, semaphore):
        self.engine, self.semaphore = engine, semaphore
        self.base, self.start, self.count = 0, 0, 0

    def enter(self, i, per_pass):
        self.base = self.base + self.count
        self.start, self.count, self.per_pass = i * per_pass + self.base, 0, per_pass

    def leave(self, passes):
        assert self.count == self.per_pass, self.count
        self.base = self.base + passes * self.per_pass
        self.start, self.count = self.base, 0

    def mark(self, ins):
        self.count += 1
        ins.then_inc(self.semaphore, 1)

    def value(self):
        return self.start + self.count

    def link(self, ins):
        self.mark(ins)
        self.engine.wait_ge(self.semaphore, self.value())


def two_layers(nc, x, small, narrow, cols, wgu0, wd0, w1, w2, out):
    x_tiles = x.rearrange("(t p) d -> p t d", p=P)
    out_tiles = out.rearrange("(t p) d -> p t d", p=P)
    xs = nc.dram_tensor("xs", (SLOTS, D), FP32).ap()
    ys = nc.dram_tensor("ys", (SLOTS, D), FP32).ap()

    ctx = ExitStack()
    with ctx:
        def sb(name, shape, dt=FP32):
            return ctx.enter_context(nc.sbuf_tensor(name, shape, dt))

        def pb(name):
            return ctx.enter_context(nc.psum_tensor(name, [P, CHUNK], FP32))

        def sem(name):
            return ctx.enter_context(nc.semaphore(name))

        x_all = sb("x_all", [P, ALL_TILES, D])
        xn_all = sb("xn_all", [P, ALL_TILES, D])
        sm = sb("sm", [P, S_END])
        cv = sb("cv", [P, COLS])
        wgu0_sb = sb("wgu0_sb", [P, E0 + 1, 2 * F])
        wd0_sb = sb("wd0_sb", [P, E0 + 1, HALVES, D])
        w1_sb = sb("w1_sb", [P, E1, F])
        w2_sb = sb("w2_sb", [P, E1, HALVES, D])
        wqkv = sb("wqkv", [P, QKV])
        bias_parts = sb("bias_parts", [PART_ROWS, 2, QKV], BF16)
        b12_parts = sb("b12_parts", [3, E1, F + D], BF16)
        ones_h = sb("ones_h", [P, P], BF16)
        before_h = sb("before_h", [P, P], BF16)
        inv_count = sb("inv_count", [P, SEQ])
        ones_f = sb("ones_f", [P, SEQ])
        idle = sb("idle", [P, 64])
        ident = sm[:, S_ID:S_ID + D]

        w_pair = sb("w_pair", [P, 2, ALL_TILES])
        pos_u = sb("pos_u", [P, 2, ALL_TILES], U32)
        table = sb("table", [1, BLOCKS], I32)
        mv_all = sb("mv_all", [P, ALL_TILES, 2])
        mv_group = sb("mv_group", [P, GROUP, 2])
        rstd_all = sb("rstd_all", [P, ALL_TILES])
        stats = sb("stats", [P, GROUP, 6])
        var_eps = sb("var_eps", [P, ALL_TILES])
        newton = sb("newton", [P, ALL_TILES])
        few = sb("few", [P, 10, ALL_TILES])

        rings = sb("rings", [P, 2 * STEP_BLOCKS, D])
        xb = rings[:, 0:STEP_BLOCKS, :]
        yb = rings[:, STEP_BLOCKS:2 * STEP_BLOCKS, :]
        zeros = rings[:, 0:ZERO_ROWS, :]
        fresh = [rings[:, 8 + 8 * h:16 + 8 * h, :] for h in range(2)]
        assert 2 * RING * TILES <= 2 * STEP_BLOCKS
        xbT = sb("xbT", [P, 2, P])
        act_b = sb("act_b", [P, 2, F])
        hid_b = sb("hid_b", [P, 2, F])
        hT_b = sb("hT_b", [P, 2, F])

        work = sb("work", [P, 8960])

        def piece(at, shape):
            n = int(np.prod(shape))
            flat = work[:, at:at + n]
            if len(shape) == 1:
                return flat
            names = "abcd"[:len(shape)]
            return flat.rearrange("p (%s) -> p %s" % (" ".join(names), " ".join(names)),
                                  **{k: s for k, s in zip(names[1:], shape[1:])})

        xnT = [piece(0, [CHUNK]), piece(CHUNK, [CHUNK])]
        NE = ALL_TILES * E1
        lg = [piece(1024, [ALL_TILES, e]) for e in EXPERTS]
        ex = [piece(1024 + NE, [ALL_TILES, e]) for e in EXPERTS]
        rank_a = [piece(1024 + 2 * NE, [ALL_TILES, e]) for e in EXPERTS]
        hot = [[piece(1024 + (3 + s) * NE, [ALL_TILES, e]) for s in range(2)] for e in EXPERTS]
        rank_b = [piece(1024 + 5 * NE, [ALL_TILES, e]) for e in EXPERTS]
        both_h = [piece(1024 + 6 * NE, [NE // 2]).bitcast(BF16)[:, 0:ALL_TILES * e] for e in EXPERTS]
        cum = [piece(1472 + 6 * NE, [e, ALL_TILES]) for e in EXPERTS]
        total = [piece(1472 + 7 * NE, [e, ALL_TILES]) for e in EXPERTS]
        past = [piece(1024, [BLOCKS, e]) for e in EXPERTS]
        block_at = sb("block_at", [1, BLOCKS])
        int_e = sb("int_e", [P, 2, E1], I32)
        F_M1, F_I1, F_M2, F_I2, F_Z, F_P1, F_P2, F_E2, F_SUM, F_NB = range(10)
        attT = xnT[0]
        yT = xnT[0]
        x_fixed = piece(CHUNK, [TILES, D])
        qkv = [piece(1024, [TILES, QKV]), piece(2560, [TILES, QKV])]
        prod = piece(4096, [H, H, DH])
        score = piece(6144, [TILES, H, H])
        att = piece(7168, [TILES, D])
        hid = piece(7680, [HALVES, CHUNK])
        head_max = piece(8704, [2, H])
        head_sum = piece(8736, [2, H])
        head_rec = piece(8768, [2, H])
        C_SIZE = 4112
        convT = [piece(u * C_SIZE, [SEQS, TAPS - 1 + SEQ]) for u in range(2)]
        z_tok = [piece(u * C_SIZE + 520, [TILES, D]) for u in range(2)]
        x2 = [piece(u * C_SIZE + 1032, [TILES, D]) for u in range(2)]
        hT = [piece(u * C_SIZE + 1544, [CHUNK]) for u in range(2)]
        mlpT = hT
        gb = [piece(u * C_SIZE + 2056, [BOOM, CHUNK]) for u in range(2)]
        qT = [gb[u][:, 0, :] for u in range(2)]
        scan = [gb[u][:, 1, :] for u in range(2)]
        pooled = [gb[u][:, 2, :] for u in range(2)]
        ch_stats = [sb("ch_stats%d" % u, [P, TILES, 6]) for u in range(2)]
        ch_mv = sb("ch_mv", [P, 2 * TILES, 2])
        ch_rstd = sb("ch_rstd", [P, 2 * TILES])
        nr = piece(4700, [N_END])
        bias_row = piece(7400, [2, QKV])
        mid_row = piece(8200, [QKV]).bitcast(BF16).rearrange("p (a b) -> p a b", a=2)
        b12_rest = piece(6400, [F + D])
        b12_split = piece(6800, [3 * (F + D) // 2]).bitcast(BF16).rearrange("p (a b) -> p a b", a=3)

        psX, psG, psH, psD, psT, psQ0, psQ1, psY = [
            pb(n) for n in ("psX", "psG", "psH", "psD", "psT", "psQ0", "psQ1", "psY")]
        psQ = (psQ0, psQ1)
        chT = (psT, psQ0)
        chM = (psQ1, psY)

        w_small = sem("w_small")
        w_layer0 = sem("w_layer0")
        w_layer1 = sem("w_layer1")
        x_loaded = sem("x_loaded")
        prep_pe = sem("prep_pe")
        prep_act = sem("prep_act")
        prep_dve = sem("prep_dve")
        prep_pool = sem("prep_pool")
        split_ready = sem("split_ready")
        b12_loaded = sem("b12_loaded")
        zeros_ready = sem("zeros_ready")
        zeros_sent = sem("zeros_sent")
        dve_step = sem("dve_step")
        xn_done = sem("xn_done")
        xn_moved = [sem("xn_moved%d" % h) for h in range(2)]
        x_fixed_loaded = sem("x_fixed_loaded")
        nT_filled = sem("nT_filled")
        nT_copied = sem("nT_copied")
        lg_done = sem("lg_done")
        lg_copied = sem("lg_copied")
        shifted = sem("shifted")
        exped = sem("exped")
        hot_ready = sem("hot_ready")
        ranked = sem("ranked")
        routed = sem("routed")
        scattered = sem("scattered")
        xb_loaded = [sem("xb_loaded%d" % s) for s in range(RING)]
        ys_sent = [sem("ys_sent%d" % s) for s in range(RING)]
        xbT_filled = sem("xbT_filled")
        xbT_ready = sem("xbT_ready")
        gu_done = sem("gu_done")
        act_ready = sem("act_ready")
        up_b_ready = sem("up_b_ready")
        hid_b_ready = sem("hid_b_ready")
        hTb_filled = sem("hTb_filled")
        hTb_ready = sem("hTb_ready")
        dn_done = sem("dn_done")
        yb_ready = sem("yb_ready")
        gathered = [sem("gathered%d" % s) for s in range(RING)]
        mixed = sem("mixed")
        xT_filled = sem("xT_filled")
        xT_copied = sem("xT_copied")
        qkv_done = sem("qkv_done")
        qkv_copied = sem("qkv_copied")
        gate_done = sem("gate_done")
        silu_ready = sem("silu_ready")
        up_done = sem("up_done")
        hid_ready = sem("hid_ready")
        down_done = sem("down_done")
        score_ready = sem("score_ready")
        prob_ready = sem("prob_ready")
        att_done = sem("att_done")
        attT_filled = sem("attT_filled")
        attT_copied = sem("attT_copied")
        y_done = sem("y_done")
        yT_ready = sem("yT_ready")
        yT_filled = sem("yT_filled")
        y_added = sem("y_added")

        def two(name):
            return [sem("%s%d" % (name, u)) for u in range(2)]
        z_ready = two("z_ready")
        zT_filled = two("zT_filled")
        zT_copied = two("zT_copied")
        conv_done = two("conv_done")
        q_done = two("q_done")
        q_ready = two("q_ready")
        k_done = two("k_done")
        v_done = two("v_done")
        k_read = two("k_read")
        pkv_ready = two("pkv_ready")
        pkvT_filled = two("pkvT_filled")
        res_read = two("res_read")
        boom_done = two("boom_done")
        boom_ready = two("boom_ready")
        mlp_done = two("mlp_done")
        mlpT_ready = two("mlpT_ready")
        mlpT_filled = two("mlpT_filled")
        out_ready = sem("out_ready")
        out_sent = sem("out_sent")

        PAIRS = CHUNKS // 2
        LINKS_ATT = 36
        LINKS_CHAIN = 12 + 3 * ROOT_LINKS

        block = ctx.enter_context(nc.Block())

        def tile_of(a, n):
            return a[:, bass.ds(n, 1), :].squeeze(1)

        @block.sync
        def _(sp):
            for h in range(2):
                sp.sem_inc(xn_moved[h], 16)
            sp.dma_start(sm[:, :], small).then_inc(w_small, 16)
            sp.dma_start(nr[0:LAT, :], narrow).then_inc(w_small, 16)
            sp.dma_start(cv[:, :], cols).then_inc(w_small, 16)
            sp.dma_start(x_all[:, 0:8, :], x_tiles[:, 0:8, :]).then_inc(x_loaded, 16)
            with sp.Fori(1, ALL_TILES // 8) as g:
                sp.wait_ge(x_loaded, g * 16)
                sp.dma_start(x_all[:, bass.ds(g * 8, 8), :],
                             x_tiles[:, bass.ds(g * 8, 8), :]).then_inc(x_loaded, 16)
            sp.wait_ge(zeros_ready, 1)
            rows = ZERO_ROWS * P
            for n in range(SLOTS // rows):
                sp.dma_start(xs[n * rows:(n + 1) * rows, :].rearrange("(p r) d -> p r d", p=P), zeros)\
                    .then_inc(zeros_sent, 16)
            sp.dma_start(wgu0_sb[:, :, :], wgu0).then_inc(w_layer0, 16)
            sp.dma_start(wd0_sb[:, :, :], wd0).then_inc(w_layer0, 16)
            sp.dma_start(w1_sb[:, :, :], w1).then_inc(w_layer1, 16)
            sp.dma_start(w2_sb[:, :, :], w2).then_inc(w_layer1, 16)
            def move_xn(layer):
                with sp.Fori(0, GROUPS) as g:
                    for h in range(2):
                        sp.wait_ge(nT_filled, g * 4 + layer * CHUNKS + 2 * h + 2)
                        sp.dma_start(xn_all[:, bass.ds(g * GROUP + 8 * h, 8), :], fresh[h])\
                            .then_inc(xn_moved[h], 16)

            sp.wait_ge(split_ready, 1)
            for k in range(3):
                sp.dma_start(b12_parts[k:k + 1, :, :], b12_split[0:E1, k, :]).then_inc(b12_loaded, 16)

            def load(n, slot):
                rows = xs[bass.ds(n * (LOAD * P), LOAD * P), :].rearrange("(b p) d -> p b d", p=P)
                sp.dma_start(xb[:, slot * LOAD:(slot + 1) * LOAD, :], rows).then_inc(xb_loaded[slot], 16)

            for layer in range(2):
                move_xn(layer)
                sp.wait_ge(scattered, (layer + 1) * 2 * ALL_TILES * 16)
                for slot in range(RING):
                    load(slot, slot)
                with sp.Fori(0, PASSES - 1) as i:
                    for slot in range(RING):
                        sp.wait_ge(xbT_filled, i * STEP_BLOCKS + layer * BLOCKS + (slot + 1) * LOAD)
                        load(i * RING + RING + slot, slot)

            with sp.Fori(0, CHUNKS) as c:
                sp.wait_ge(out_ready, c + 1)
                sp.dma_start(out_tiles[:, bass.ds(c * TILES, TILES), :],
                             x_all[:, bass.ds(c * TILES, TILES), :]).then_inc(out_sent, 16)
            sp.wait_ge(out_sent, 16 * CHUNKS)

        @block.gpsimd
        def _(pool):
            nc.gpsimd.memset(zeros, 0.0).then_inc(zeros_ready, 1)
            nc.gpsimd.memset(bias_parts[:, :, :], 0.0)
            nc.gpsimd.memset(ones_h[:, :], 1.0)
            nc.gpsimd.memset(ones_f[:, :], 1.0).then_inc(prep_pool, 1)

            def scatter(t):
                for s in range(2):
                    pool.indirect_dma_start(xs, bass.IndirectOffsetOnAxis(ap=pos_u[:, s, t:t + 1], axis=0),
                                            xn_all[:, t, :], None).then_inc(scattered, 16)

            def gather(layer, c, half):
                if c >= RING and half == 0:
                    pool.wait_ge(mixed, layer * CHUNKS + c - RING + 1)
                for j in (2 * half, 2 * half + 1):
                    for s in range(2):
                        pool.indirect_dma_start(
                            rings[:, (c % RING * TILES + j) * 2 + s, :], None, ys,
                            bass.IndirectOffsetOnAxis(ap=pos_u[:, s, c * TILES + j:c * TILES + j + 1], axis=0))\
                            .then_inc(gathered[c % RING], 16)

            def wait_stored(layer):
                for slot in range(RING):
                    pool.wait_ge(ys_sent[slot], (layer + 1) * PASSES * 16)

            def wait_moved(layer):
                for h in range(2):
                    pool.wait_ge(xn_moved[h], ((layer + 1) * GROUPS + 1) * 16)

            pool.wait_ge(routed, 1)
            pool.wait_ge(zeros_sent, SLOTS // (ZERO_ROWS * P) * 16)
            wait_moved(0)
            for t in range(ALL_TILES):
                scatter(t)
            with pool.Fori(0, PASSES) as i:
                for k in range(STEP_BLOCKS):
                    pool.wait_ge(up_b_ready, i * STEP_BLOCKS + k + 1)
                    nc.gpsimd.tensor_tensor(hid_b[:, k % 2, :], act_b[:, k % 2, :], hid_b[:, k % 2, :], ALU.mult)\
                        .then_inc(hid_b_ready, 1)
            wait_stored(0)
            for n in range(2 * CHUNKS):
                gather(0, n // 2, n % 2)
            pool.wait_ge(routed, 2)
            wait_moved(1)
            for t in range(ALL_TILES):
                scatter(t)
            wait_stored(1)
            for n in range(2 * CHUNKS):
                gather(1, n // 2, n % 2)

        @block.tensor
        def _(pe):
            def transposes(bank, src):
                for t in range(TILES):
                    last = nc.tensor.transpose(bank[:, t * P:(t + 1) * P], src(t), ident)
                return last

            def logits(layer):
                e = EXPERTS[layer]
                gate_w = sm[:, S_GATE0:S_GATE0 + E0] if layer == 0 else sm[:, S_GATE1:S_GATE1 + E1]
                with pe.Fori(0, GROUPS) as g:
                    chunk0 = g * (GROUP // TILES) + layer * CHUNKS
                    for k in range(GROUP // TILES + 1):
                        if k < GROUP // TILES:
                            if k % 2 == 0:
                                pe.wait_ge(xn_done, (g + layer * GROUPS) * 2 + k // 2 + 1)
                            if k >= 2:
                                pe.wait_ge(nT_copied, chunk0 + k - 1)
                            transposes(psQ[k % 2], lambda t: fresh[k // 2][:, k % 2 * TILES + t, :])\
                                .then_inc(nT_filled, 1)
                        if k:
                            pe.wait_ge(nT_copied, chunk0 + k)
                            if k == 1:
                                pe.wait_ge(lg_copied, g + layer * GROUPS + 1)
                            for t in range(TILES):
                                at = ((k - 1) * TILES + t) * e
                                last = nc.tensor.matmul(psY[:, at:at + e], xnT[(k - 1) % 2][:, t * P:(t + 1) * P],
                                                        gate_w, start=True, stop=True)
                            last.then_inc(lg_done, 1)

            def ranks(layer):
                e = EXPERTS[layer]
                pe.wait_ge(hot_ready, layer + 1)
                per = min(ALL_TILES, CHUNK // e // 8 * 8)
                for h in range(ALL_TILES // per):
                    cols = slice(h * per * e, (h + 1) * per * e)
                    nc.tensor.matmul((psX, psH)[h][:, 0:per * e], before_h[:, :], both_h[layer][:, cols],
                                     start=True, stop=True)
                    last = nc.tensor.matmul((psG, psD)[h][:, 0:per * e], ones_h[:, :], both_h[layer][:, cols],
                                            start=True, stop=True)
                last.then_inc(ranked, 1)

            def block_step(layer, b, k, passes=0, first=False, stages=(0, 1, 2, 3)):
                c = b + layer * BLOCKS
                if 0 in stages:
                    if k % LOAD == 0:
                        pe.wait_ge(xb_loaded[k // LOAD], (passes + 1) * 16)
                    if not (first and k == 0 and layer == 0):
                        pe.wait_ge(xbT_ready, c)
                    nc.tensor.transpose(psX[:, 0:P], xb[:, k, :], ident).then_inc(xbT_filled, 1)
                if 1 in stages and not (first and k < 1):
                    j = (k - 1) % 2
                    e = pe.value_load(table[0:1, bass.ds(b - 1, 1)], min_val=0, max_val=EXPERTS[layer] - 1)
                    pe.wait_ge(xbT_ready, c)
                    if layer == 0:
                        if not (first and k == 1):
                            pe.wait_ge(up_b_ready, c - 1)
                        nc.tensor.matmul(psG[:, :], xbT[:, j, :], wgu0_sb[:, bass.ds(e, 1), :].squeeze(1),
                                         start=True, stop=True).then_inc(gu_done, 1)
                    else:
                        if not (first and k == 1):
                            pe.wait_ge(act_ready, b - 1)
                        nc.tensor.matmul(psG[:, 0:F], xbT[:, j, :], w1_sb[:, bass.ds(e, 1), :].squeeze(1),
                                         start=True, stop=False)
                        nc.tensor.matmul(psG[:, 0:F], ones_h[0:3, :], b12_parts[:, bass.ds(e, 1), 0:F].squeeze(1),
                                         start=False, stop=True).then_inc(gu_done, 1)
                if 2 in stages and not (first and k < 2):
                    j = (k - 2) % 2
                    if layer == 0:
                        pe.wait_ge(hid_b_ready, c - 1)
                    else:
                        pe.wait_ge(act_ready, b - 1)
                    if not (first and k == 2 and layer == 0):
                        pe.wait_ge(hTb_ready, c - 2)
                    for f in range(HALVES):
                        last = nc.tensor.transpose(psH[:, f * P:(f + 1) * P],
                                                   (hid_b, act_b)[layer][:, j, f * P:(f + 1) * P], ident)
                    last.then_inc(hTb_filled, 1)
                if 3 in stages and not (first and k < 3):
                    j = (k - 3) % 2
                    e = pe.value_load(table[0:1, bass.ds(b - 3, 1)], min_val=0, max_val=EXPERTS[layer] - 1)
                    pe.wait_ge(hTb_ready, c - 2)
                    if not (first and k == 3 and layer == 0):
                        pe.wait_ge(yb_ready, c - 3)
                    w_down = (wd0_sb, w2_sb)[layer]
                    for f in range(HALVES):
                        last = nc.tensor.matmul(psD[:, 0:D], hT_b[:, j, f * P:(f + 1) * P],
                                                w_down[:, bass.ds(e, 1), f, :].squeeze(1),
                                                start=(f == 0), stop=(layer == 0 and f == HALVES - 1))
                    if layer == 1:
                        last = nc.tensor.matmul(psD[:, 0:D], ones_h[0:3, :],
                                                b12_parts[:, bass.ds(e, 1), F:F + D].squeeze(1),
                                                start=False, stop=True)
                    last.then_inc(dn_done, 1)

            def drain(layer):
                for k, stages in ((0, (1, 2, 3)), (1, (2, 3)), (2, (3,))):
                    block_step(layer, BLOCKS + k, k, stages=stages)

            def beats(layer, pair, counts, u=0, first=False):
                def beat(n):
                    done = u * sum(counts) + sum(counts[:n])
                    for k in range(done, done + counts[n]):
                        passed = (pair - BLOCK_PAIRS[0]) * (PAIR_BLOCKS // STEP_BLOCKS) + k // STEP_BLOCKS
                        block_step(layer, (pair - BLOCK_PAIRS[0]) * PAIR_BLOCKS + k, k % STEP_BLOCKS,
                                   passed + layer * PASSES, first=first and k < STEP_BLOCKS)
                return beat

            def pre(c, beat=lambda n: None):
                beat(3)
                if not isinstance(c, int) or c >= 2:
                    pe.wait_ge(y_added, c - 1)
                pe.wait_ge(x_fixed_loaded, c * 16 + 16)
                transposes(psT, lambda t: x_fixed[:, t, :]).then_inc(xT_filled, 1)
                pe.wait_ge(xT_copied, c + 1)
                for t in range(TILES):
                    if t % 2 == 0:
                        beat(4 + t // 2)
                    if t >= 2:
                        pe.wait_ge(qkv_copied, c * TILES + t - 1)
                    elif not isinstance(c, int) or c >= 1:
                        pe.wait_ge((silu_ready, hid_ready)[t], c * HALVES)
                    nc.tensor.matmul(psQ[t % 2][:, 0:QKV], xnT[0][:, t * P:(t + 1) * P], wqkv[:, :],
                                     start=True, stop=False)
                    nc.tensor.matmul(psQ[t % 2][:, 0:QKV], ones_h[0:PART_ROWS, :], bias_parts[:, 0, :],
                                     start=False, stop=True).then_inc(qkv_done, 1)
                for f in range(HALVES):
                    beat(6 + f)
                    if f == 0:
                        pe.wait_ge(qkv_copied, c * TILES + TILES)
                    else:
                        pe.wait_ge(silu_ready, c * HALVES + f)
                    nc.tensor.matmul(psQ0[:, :], wgu0_sb[:, E0, f * P:(f + 1) * P], xnT[0][:, :],
                                     start=True, stop=True).then_inc(gate_done, 1)
                    if f:
                        beat(8)
                        pe.wait_ge(hid_ready, c * HALVES + f)
                    nc.tensor.matmul(psQ1[:, :], wgu0_sb[:, E0, F + f * P:F + (f + 1) * P], xnT[0][:, :],
                                     start=True, stop=True).then_inc(up_done, 1)

            def down(c):
                pe.wait_ge(hid_ready, c * HALVES + HALVES)
                if not isinstance(c, int) or c >= 1:
                    pe.wait_ge(yT_ready, c)
                for f in range(HALVES):
                    last = nc.tensor.matmul(psY[:, :], wd0_sb[:, E0, f, :], hid[:, f, :],
                                            start=(f == 0), stop=False)
                last.then_inc(down_done, 1)

            def post(c, beat=lambda n: None):
                beat(0)
                pe.wait_ge(att_done, c + 1)
                transposes(psT, lambda t: att[:, t, :]).then_inc(attT_filled, 1)
                beat(1)
                pe.wait_ge(attT_copied, c + 1)
                nc.tensor.matmul(psY[:, :], sm[:, S_WOUT:S_WOUT + D], attT[:, :],
                                 start=False, stop=True).then_inc(y_done, 1)
                beat(2)
                pe.wait_ge(yT_ready, c + 1)
                transposes(psT, lambda t: yT[:, t * P:(t + 1) * P]).then_inc(yT_filled, 1)

            def att_chunk(c, first=False, last=False, beat=lambda n: None):
                if not first:
                    post(c - 1, beat)
                down(c)
                if not last:
                    pre(c + 1, beat)
                beat(9)

            def chain(pair, beat=lambda n: None):
                beat(0)
                for u in range(2):
                    if not isinstance(pair, int) or pair > 0:
                        pe.wait_ge(res_read[u], pair * 2)
                    pe.wait_ge(z_ready[u], pair * 3 + 1)
                    transposes(chT[u], lambda t: z_tok[u][:, t, :]).then_inc(zT_filled[u], 1)
                beat(1)
                for u in range(2):
                    pe.wait_ge(zT_copied[u], pair * 3 + 1)
                    for t in range(TILES):
                        s, at = t // (SEQ // P), (t % (SEQ // P)) * P
                        for k in range(TAPS):
                            nc.tensor.matmul(chM[u][:, t * P:(t + 1) * P], convT[u][:, s, at + k:at + k + P],
                                             sm[:, S_CONV + k * D:S_CONV + (k + 1) * D],
                                             start=(k == 0), stop=False)
                        last = nc.tensor.matmul(chM[u][:, t * P:(t + 1) * P], ones_h[0:PART_ROWS, :],
                                                bias_parts[:, 1, 0:D], start=False, stop=True)
                    last.then_inc(conv_done[u], 1)
                beat(2)
                for u in range(2):
                    pe.wait_ge(z_ready[u], pair * 3 + 2)
                    transposes(chT[u], lambda t: z_tok[u][:, t, :]).then_inc(zT_filled[u], 1)
                beat(3)
                for u in range(2):
                    pe.wait_ge(zT_copied[u], pair * 3 + 2)
                    nc.tensor.matmul(chM[u][:, :], sm[:, S_WQ1:S_WQ1 + D], hT[u][:, :],
                                     start=True, stop=True).then_inc(q_done[u], 1)
                    nc.tensor.matmul(chT[u][:, :], sm[:, S_WK1:S_WK1 + D], hT[u][:, :],
                                     start=True, stop=True).then_inc(k_done[u], 1)
                beat(4)
                for u in range(2):
                    pe.wait_ge(q_ready[u], pair + 1)
                    nc.tensor.matmul(chM[u][:, :], sm[:, S_WV1:S_WV1 + D], hT[u][:, :],
                                     start=True, stop=True).then_inc(v_done[u], 1)
                beat(5)
                for u in range(2):
                    pe.wait_ge(k_read[u], pair + 1)
                    pe.wait_ge(pkv_ready[u], pair + 1)
                    transposes(chT[u], lambda t: pooled[u][:, t * P:(t + 1) * P]).then_inc(pkvT_filled[u], 1)
                beat(6)
                for u in range(2):
                    pe.wait_ge(res_read[u], pair * 2 + 1)
                    pe.wait_ge(z_ready[u], pair * 3 + 3)
                    transposes(chT[u], lambda t: z_tok[u][:, t, :]).then_inc(zT_filled[u], 1)
                beat(7)
                for b in range(BOOM):
                    for u in range(2):
                        if b == 0:
                            pe.wait_ge(zT_copied[u], pair * 3 + 3)
                        if b >= 2:
                            pe.wait_ge(boom_ready[u], pair * BOOM + b - 1)
                        nc.tensor.matmul((chM, chT)[b % 2][u][:, :], sm[:, S_WB + b * D:S_WB + (b + 1) * D],
                                         hT[u][:, :], start=True, stop=True).then_inc(boom_done[u], 1)
                beat(8)
                for u in range(2):
                    pe.wait_ge(boom_ready[u], pair * BOOM + BOOM)
                    for b in range(BOOM):
                        last = nc.tensor.matmul(chM[u][:, :], sm[:, S_WU + b * D:S_WU + (b + 1) * D],
                                                gb[u][:, b, :], start=(b == 0), stop=(b == BOOM - 1))
                    last.then_inc(mlp_done[u], 1)
                beat(9)
                for u in range(2):
                    pe.wait_ge(mlpT_ready[u], pair + 1)
                    transposes(chT[u], lambda t: mlpT[u][:, t * P:(t + 1) * P]).then_inc(mlpT_filled[u], 1)

            pe.wait_ge(w_small, 48)
            nc.tensor.matmul(psX[:, 0:2 * D], nr[0:LAT, N_WDOWN:N_WDOWN + D], nr[0:LAT, N_WUP:N_WUP + 2 * D],
                             start=True, stop=True).then_inc(prep_pe, 1)
            nc.tensor.matmul(psG[0:1, 0:2 * D], nr[0:LAT, N_BDOWN:N_BDOWN + 1], nr[0:LAT, N_WUP:N_WUP + 2 * D],
                             start=True, stop=True).then_inc(prep_pe, 1)

            logits(0)
            pe.wait_ge(prep_act, 1)
            pe.wait_ge(prep_dve, 1)
            ranks(0)
            pe.wait_ge(w_layer0, 32)
            pe.wait_ge(routed, 1)
            pre(0)
            for c in range(2 * BLOCK_PAIRS[0]):
                att_chunk(c, first=(c == 0))
            pair = BLOCK_PAIRS[0]
            for u in range(2):
                att_chunk(pair * 2 + u, beat=beats(0, pair, ATT_BEATS, u, first=True))
            with pe.Fori(pair + 1, BLOCK_PAIRS[-1] + 1) as pair:
                for u in range(2):
                    att_chunk(pair * 2 + u, beat=beats(0, pair, ATT_BEATS, u))
            drain(0)
            for c in range(2 * BLOCK_PAIRS[-1] + 2, CHUNKS):
                att_chunk(c, last=(c == CHUNKS - 1))
            post(CHUNKS - 1)

            logits(1)
            ranks(1)
            pe.wait_ge(routed, 2)
            chain(0)
            with pe.Fori(1, BLOCK_PAIRS[0]) as pair:
                chain(pair)
            pe.wait_ge(w_layer1, 32)
            pe.wait_ge(b12_loaded, 48)
            pair = BLOCK_PAIRS[0]
            chain(pair, beats(1, pair, CHAIN_BEATS, first=True))
            with pe.Fori(pair + 1, BLOCK_PAIRS[-1] + 1) as pair:
                chain(pair, beats(1, pair, CHAIN_BEATS))
            drain(1)
            with pe.Fori(BLOCK_PAIRS[-1] + 1, PAIRS) as pair:
                chain(pair)

        @block.scalar
        def _(act):
            def col(n):
                return cv[:, n:n + 1]

            act.sem_inc(lg_copied, 1)
            act.wait_ge(prep_pe, 1)
            nc.scalar.copy(wqkv[:, D:3 * D], psX[:, 0:2 * D])
            nc.scalar.copy(wqkv[:, 0:D], sm[:, S_WQ:S_WQ + D]).then_inc(prep_act, 1)

            def logits(layer):
                e = EXPERTS[layer]
                with act.Fori(0, GROUPS) as g:
                    chunk0 = g * (GROUP // TILES) + layer * CHUNKS
                    for k in range(GROUP // TILES):
                        act.wait_ge(nT_filled, chunk0 + k + 1)
                        if k >= 2:
                            act.wait_ge(lg_done, chunk0 + k - 1)
                        nc.scalar.copy(xnT[k % 2][:, :], psQ[k % 2][:, :]).then_inc(nT_copied, 1)
                    act.wait_ge(lg_done, chunk0 + GROUP // TILES)
                    nc.scalar.copy(lg[layer][:, bass.ds(g * GROUP, GROUP), :],
                                   psY[:, 0:GROUP * e].rearrange("p (t e) -> p t e", e=e)).then_inc(lg_copied, 1)

            def route_exps(layer):
                act.wait_ge(shifted, layer + 1)
                nc.scalar.activation(ex[layer][:, :, :], ex[layer][:, :, :], ACT.Exp)
                nc.scalar.activation(few[:, F_E2, :], few[:, F_E2, :], ACT.Exp).then_inc(exped, 1)

            def block_step(layer, b, k, first=False, stages=(0, 1, 2, 3), sent=None):
                c = b + layer * BLOCKS
                if 0 in stages:
                    act.wait_ge(xbT_filled, c + 1)
                    nc.scalar.copy(xbT[:, k % 2, :], psX[:, 0:P]).then_inc(xbT_ready, 1)
                if 1 in stages and not (first and k < 1):
                    act.wait_ge(gu_done, c)
                    if layer == 0:
                        nc.scalar.activation(act_b[:, (k - 1) % 2, :], psG[:, 0:F], ACT.Silu)
                        nc.scalar.copy(hid_b[:, (k - 1) % 2, :], psG[:, F:2 * F]).then_inc(up_b_ready, 1)
                    else:
                        nc.scalar.activation(act_b[:, (k - 1) % 2, :], psG[:, 0:F], ACT.Gelu).then_inc(act_ready, 1)
                if 2 in stages and not (first and k < 2):
                    act.wait_ge(hTb_filled, c - 1)
                    nc.scalar.copy(hT_b[:, (k - 2) % 2, :], psH[:, 0:F]).then_inc(hTb_ready, 1)
                if 3 in stages and not (first and k < 3):
                    at = (k - 3) % STEP_BLOCKS
                    slot = at // LOAD
                    if at % LOAD == 0:
                        n = sent if k >= 3 else sent - 1
                        if not (isinstance(n, int) and n == 0):
                            act.wait_ge(ys_sent[slot], n * 16)
                    act.wait_ge(dn_done, c - 2)
                    nc.scalar.copy(yb[:, at, :], psD[:, 0:D]).then_inc(yb_ready, 1)
                    if at % LOAD == LOAD - 1:
                        act.wait_ge(yb_ready, c - 2)
                        rows = ys[bass.ds((b - 3 - (LOAD - 1)) * P, LOAD * P), :].rearrange("(b p) d -> p b d", p=P)
                        act.dma_start(rows, yb[:, slot * LOAD:(slot + 1) * LOAD, :]).then_inc(ys_sent[slot], 16)

            def drain(layer):
                for k, stages in ((0, (1, 2, 3)), (1, (2, 3)), (2, (3,))):
                    block_step(layer, BLOCKS + k, k, stages=stages, sent=(layer + 1) * PASSES)

            def beats(layer, pair, counts, u=0, first=False):
                def beat(n):
                    done = u * sum(counts) + sum(counts[:n])
                    for k in range(done, done + counts[n]):
                        passed = (pair - BLOCK_PAIRS[0]) * (PAIR_BLOCKS // STEP_BLOCKS) + k // STEP_BLOCKS
                        block_step(layer, (pair - BLOCK_PAIRS[0]) * PAIR_BLOCKS + k, k % STEP_BLOCKS,
                                   first=first and k < STEP_BLOCKS, sent=passed + layer * PASSES)
                return beat

            def load_fixed(c):
                act.dma_start(x_fixed, xn_all[:, bass.ds(c * TILES, TILES), :]).then_inc(x_fixed_loaded, 16)

            def pre(c, u, beat=lambda n: None, more=True):
                beat(3)
                act.wait_ge(xT_filled, c + 1)
                nc.scalar.copy(xnT[0][:, :], psT[:, :]).then_inc(xT_copied, 1)
                if more:
                    load_fixed(c + 1)
                for t in range(TILES):
                    if t % 2 == 0:
                        beat(4 + t // 2)
                    act.wait_ge(qkv_done, c * TILES + t + 1)
                    nc.scalar.copy(qkv[u][:, t, :], psQ[t % 2][:, 0:QKV]).then_inc(qkv_copied, 1)

            def shared_silu(c, f):
                act.wait_ge(gate_done, c * HALVES + f + 1)
                nc.scalar.activation(hid[:, f, :], psQ0[:, :], ACT.Silu).then_inc(silu_ready, 1)

            def post(c, beat=lambda n: None):
                beat(0)
                act.wait_ge(attT_filled, c + 1)
                nc.scalar.copy(attT[:, :], psT[:, :]).then_inc(attT_copied, 1)
                beat(1)
                act.wait_ge(y_done, c + 1)
                nc.scalar.activation(yT[:, :], psY[:, :], ACT.Identity, bias=col(C_BOUT)).then_inc(yT_ready, 1)
                beat(2)

            def exps(c, h):
                act.wait_ge(score_ready, c * 2 + h + 1)
                s = score[:, 2 * h:2 * h + 2, :, :]
                nc.scalar.activation(s, s, ACT.Exp, scale=SCALE).then_inc(prob_ready, 1)

            def att_chunk(c, u, first=False, last=False, more=True, beat=lambda n: None):
                if not first:
                    post(c - 1, beat)
                if not last:
                    pre(c + 1, 1 - u, beat, more)
                    act.wait_ge(down_done, c + 1)
                    beat(6)
                    shared_silu(c + 1, 0)
                exps(c, 0)
                beat(7)
                if not last:
                    shared_silu(c + 1, 1)
                exps(c, 1)
                beat(8)
                beat(9)

            def chain(pair, beat=lambda n: None):
                beat(0)
                for u in range(2):
                    act.wait_ge(zT_filled[u], pair * 3 + 1)
                    for s in range(SEQS):
                        last = nc.scalar.activation(convT[u][:, s, TAPS - 1:], chT[u][:, s * SEQ:(s + 1) * SEQ],
                                                    ACT.Identity, scale=col(C_GCONV), bias=col(C_BCONV))
                    last.then_inc(zT_copied[u], 1)
                beat(1)
                beat(2)
                for u in range(2):
                    act.wait_ge(zT_filled[u], pair * 3 + 2)
                    nc.scalar.activation(hT[u][:, :], chT[u][:, :], ACT.Identity, scale=col(C_GATTN),
                                         bias=col(C_BATTN)).then_inc(zT_copied[u], 1)
                beat(3)
                for u in range(2):
                    act.wait_ge(q_done[u], pair + 1)
                    nc.scalar.activation(qT[u][:, :], chM[u][:, :], ACT.Identity, bias=col(C_BQ))\
                        .then_inc(q_ready[u], 1)
                for n in (4, 5, 6):
                    beat(n)
                for u in range(2):
                    act.wait_ge(zT_filled[u], pair * 3 + 3)
                    nc.scalar.activation(hT[u][:, :], chT[u][:, :], ACT.Identity, scale=col(C_GBOOM),
                                         bias=col(C_BBOOM)).then_inc(zT_copied[u], 1)
                beat(7)
                for b in range(BOOM):
                    for u in range(2):
                        act.wait_ge(boom_done[u], pair * BOOM + b + 1)
                        nc.scalar.activation(gb[u][:, b, :], (chM, chT)[b % 2][u][:, :], ACT.Gelu,
                                             bias=col(C_BB + b)).then_inc(boom_ready[u], 1)
                beat(8)
                for u in range(2):
                    act.wait_ge(mlp_done[u], pair + 1)
                    nc.scalar.activation(mlpT[u][:, :], chM[u][:, :], ACT.Identity, bias=col(C_BU))\
                        .then_inc(mlpT_ready[u], 1)
                beat(9)

            logits(0)
            route_exps(0)
            act.wait_ge(routed, 1)
            for h in range(2):
                act.wait_ge(xn_moved[h], (GROUPS + 1) * 16)
            load_fixed(0)
            pre(0, 0)
            for f in range(HALVES):
                shared_silu(0, f)
            for c in range(2 * BLOCK_PAIRS[0]):
                att_chunk(c, c % 2, first=(c == 0))
            pair = BLOCK_PAIRS[0]
            for u in range(2):
                att_chunk(pair * 2 + u, u, beat=beats(0, pair, ATT_BEATS, u, first=True))
            with act.Fori(pair + 1, BLOCK_PAIRS[-1] + 1) as pair:
                for u in range(2):
                    att_chunk(pair * 2 + u, u, beat=beats(0, pair, ATT_BEATS, u))
            drain(0)
            for c in range(2 * BLOCK_PAIRS[-1] + 2, CHUNKS):
                att_chunk(c, c % 2, last=(c == CHUNKS - 1), more=(c < CHUNKS - 2))
            post(CHUNKS - 1)
            logits(1)
            route_exps(1)
            act.wait_ge(routed, 2)
            chain(0)
            with act.Fori(1, BLOCK_PAIRS[0]) as pair:
                chain(pair)
            pair = BLOCK_PAIRS[0]
            chain(pair, beats(1, pair, CHAIN_BEATS, first=True))
            with act.Fori(pair + 1, BLOCK_PAIRS[-1] + 1) as pair:
                chain(pair, beats(1, pair, CHAIN_BEATS))
            drain(1)
            with act.Fori(BLOCK_PAIRS[-1] + 1, PAIRS) as pair:
                chain(pair)

        @block.vector
        def _(dve):
            v = nc.vector
            L = Links(dve, dve_step)
            alone = [0]

            def wait_alone(*waits):
                for semaphore, value in waits:
                    dve.wait_ge(semaphore, value)
                v.memset(idle[:, alone[0]:alone[0] + 1], 0.0)
                alone[0] += 1

            def link_alone(ins):
                L.mark(ins)
                wait_alone((dve_step, L.value()))

            dve.wait_ge(w_small, 48)
            v.tensor_copy(before_h[:, :], sm[:, S_BEFORE:S_BEFORE + P])
            v.reciprocal(inv_count[:, :], sm[:, S_COUNT:S_COUNT + SEQ])
            L.link(v.memset(bias_row[0:1, :, :], 0.0))
            dve.wait_ge(prep_pe, 2)
            dve.wait_ge(prep_pool, 1)
            b12 = nr[0:E1, N_B12:N_END]
            v.tensor_copy(bias_row[0:1, 0, 0:D], nr[0:1, N_BQ:N_BQ + D])
            v.tensor_copy(bias_row[0:1, 1, 0:D], nr[0:1, N_CONVB:N_CONVB + D])
            v.tensor_copy(b12_split[0:E1, 0, :], b12)
            L.link(v.tensor_tensor(bias_row[0:1, 0, D:3 * D], psG[0:1, 0:2 * D], nr[0:1, N_BUP:N_BUP + 2 * D], ALU.add))
            v.tensor_tensor(b12_rest[0:E1, :], b12, b12_split[0:E1, 0, :], ALU.subtract)
            L.link(v.tensor_copy(bias_parts[0:1, :, :], bias_row[0:1, :, :]))
            v.tensor_copy(b12_split[0:E1, 1, :], b12_rest[0:E1, :])
            L.link(v.tensor_tensor(bias_row[0:1, :, :], bias_row[0:1, :, :], bias_parts[0:1, :, :], ALU.subtract))
            v.tensor_tensor(b12_rest[0:E1, :], b12_rest[0:E1, :], b12_split[0:E1, 1, :], ALU.subtract)
            L.link(v.tensor_copy(mid_row[0:1, :, :], bias_row[0:1, :, :]))
            v.tensor_copy(b12_split[0:E1, 2, :], b12_rest[0:E1, :]).then_inc(split_ready, 1)
            v.tensor_copy(bias_parts[32:33, :, :], mid_row[0:1, :, :])
            L.link(v.tensor_tensor(bias_row[0:1, :, :], bias_row[0:1, :, :], mid_row[0:1, :, :], ALU.subtract))
            v.tensor_copy(bias_parts[64:65, :, :], bias_row[0:1, :, :]).then_inc(prep_dve, 1)

            def inverse_root(y, var, n):
                v_eps, step = var_eps[:, 0:n], newton[:, 0:n]
                L.link(v.tensor_scalar(v_eps, var, EPS, None, ALU.add))
                L.link(v.tensor_scalar(y.bitcast(I32), v_eps.bitcast(I32), -0.5, ROOT_GUESS, ALU.mult, ALU.add))
                for _ in range(ROOT_STEPS):
                    L.link(v.tensor_tensor(step, y, y, ALU.mult))
                    L.link(v.scalar_tensor_tensor(step, step, -0.5, v_eps, ALU.mult, ALU.mult))
                    L.link(v.scalar_tensor_tensor(y, step, 1.5, y, ALU.add, ALU.mult))

            def norm_all(layer):
                with dve.Fori(0, GROUPS) as g:
                    L.enter(g, 3)
                    if layer == 0:
                        wait_alone((x_loaded, g * 32 + 32))
                    for t in range(GROUP):
                        last = v.bn_stats(stats[:, t, :], tile_of(x_all, g * GROUP + t))
                    link_alone(last)
                    for t in range(GROUP):
                        last = v.bn_aggr(mv_group[:, t, :], stats[:, t, :])
                    L.link(last)
                    L.link(v.tensor_copy(mv_all[:, bass.ds(g * GROUP, GROUP), :], mv_group[:, :, :]))
                L.leave(GROUPS)
                inverse_root(rstd_all[:, :], mv_all[:, :, 1], ALL_TILES)
                with dve.Fori(0, GROUPS) as g:
                    for h in range(2):
                        dve.wait_ge(xn_moved[h], (g + layer * GROUPS + 1) * 16)
                        for t in range(8):
                            n = g * GROUP + 8 * h + t
                            last = v.tensor_scalar(fresh[h][:, t, :], tile_of(x_all, n),
                                                   mv_all[:, bass.ds(n, 1), 0:1].squeeze(1),
                                                   rstd_all[:, bass.ds(n, 1)], ALU.subtract, ALU.mult)
                        last.then_inc(xn_done, 1)

            def route(layer):
                e = EXPERTS[layer]
                logit, exp_e, ra, rb, hots = lg[layer], ex[layer], rank_a[layer], rank_b[layer], hot[layer]

                def wide(k):
                    return few[:, k, :].unsqueeze(2).to_broadcast([P, ALL_TILES, e])

                iota = sm[:, S_IOTA:S_IOTA + e].unsqueeze(1).to_broadcast([P, ALL_TILES, e])
                dve.wait_ge(lg_copied, (layer + 1) * GROUPS + 1)
                L.link(v.reduce_max(few[:, F_M1, :], logit, axis=AX.X))
                v.tensor_tensor(exp_e, logit, wide(F_M1), ALU.subtract)
                L.link(v.tensor_tensor(ra, logit, wide(F_M1), ALU.is_equal))
                L.link(v.scalar_tensor_tensor(ra, ra, -32.0, iota, ALU.mult, ALU.add))
                L.link(v.tensor_reduce(few[:, F_I1, :], ra, AX.X, ALU.min))
                L.link(v.tensor_tensor(hots[0], ra, wide(F_I1), ALU.is_equal))
                L.link(v.scalar_tensor_tensor(ra, hots[0], -BIG, logit, ALU.mult, ALU.add))
                L.link(v.reduce_max(few[:, F_M2, :], ra, axis=AX.X))
                v.tensor_tensor(few[:, F_E2, :], few[:, F_M2, :], few[:, F_M1, :], ALU.subtract).then_inc(shifted, 1)
                L.link(v.tensor_tensor(rb, ra, wide(F_M2), ALU.is_equal))
                L.link(v.scalar_tensor_tensor(rb, rb, -32.0, iota, ALU.mult, ALU.add))
                L.link(v.tensor_reduce(few[:, F_I2, :], rb, AX.X, ALU.min))
                L.link(v.tensor_tensor(hots[1], rb, wide(F_I2), ALU.is_equal))
                dve.wait_ge(b12_loaded, 48)
                v.tensor_tensor(both_h[layer].rearrange("p (t e) -> p t e", e=e), hots[0], hots[1], ALU.add)\
                    .then_inc(hot_ready, 1)

                dve.wait_ge(exped, layer + 1)
                L.link(v.reduce_sum(few[:, F_Z, :], exp_e, axis=AX.X))
                L.link(v.reciprocal(few[:, F_P1, :], few[:, F_Z, :]))
                L.link(v.tensor_tensor(few[:, F_P2, :], few[:, F_E2, :], few[:, F_P1, :], ALU.mult))
                L.link(v.tensor_tensor(few[:, F_SUM, :], few[:, F_P1, :], few[:, F_P2, :], ALU.add))
                floor, floor_op = ((1e-20, ALU.add), (1e-10, ALU.max))[layer]
                L.link(v.tensor_scalar(few[:, F_SUM, :], few[:, F_SUM, :], floor, None, floor_op))
                L.link(v.reciprocal(few[:, F_Z, :], few[:, F_SUM, :]))
                for s in range(2):
                    v.tensor_tensor(w_pair[:, s, :], few[:, F_P1 + s, :], few[:, F_Z, :], ALU.mult)

                dve.wait_ge(ranked, layer + 1)
                per = min(ALL_TILES, CHUNK // e // 8 * 8)
                halves = [(h, slice(h * per, (h + 1) * per)) for h in range(ALL_TILES // per)]
                for h, tiles in halves:
                    last = v.tensor_copy(total[layer][:, :, tiles],
                                         (psG, psD)[h][:, 0:per * e].rearrange("p (t e) -> p e t", e=e))
                L.link(last)
                for j in range(e):
                    last = v.tensor_tensor_scan(cum[layer][:, j, :], ones_f[:, 0:ALL_TILES], total[layer][:, j, :],
                                                0.0, ALU.mult, ALU.add)
                L.link(last)
                blocks_e, ends = few[:, F_NB, 0:e], few[:, F_I1, 0:e]
                L.link(v.tensor_scalar(int_e[:, 0, 0:e], cum[layer][:, :, ALL_TILES - 1], float(P - 1), None, ALU.add))
                L.link(v.tensor_scalar(int_e[:, 1, 0:e], int_e[:, 0, 0:e], P.bit_length() - 1, None,
                                       ALU.arith_shift_right))
                L.link(v.tensor_copy(blocks_e, int_e[:, 1, 0:e]))
                L.link(v.tensor_tensor_scan(ends, ones_f[:, 0:e], blocks_e, 0.0, ALU.mult, ALU.add))
                v.tensor_tensor(few[:, F_M1, 0:e], ends, blocks_e, ALU.subtract)
                L.link(v.tensor_tensor(cum[layer], cum[layer], total[layer], ALU.subtract))
                L.link(v.scalar_tensor_tensor(cum[layer], few[:, F_M1, 0:e].unsqueeze(2).to_broadcast([P, e, ALL_TILES]),
                                              float(P), cum[layer], ALU.mult, ALU.add))
                for h, tiles in halves:
                    last = v.tensor_tensor(exp_e[:, tiles, :],
                                           (psX, psH)[h][:, 0:per * e].rearrange("p (t e) -> p t e", e=e),
                                           cum[layer][:, :, tiles].rearrange("p e t -> p t e"), ALU.add)
                L.link(last)
                v.tensor_tensor(ra, hots[0], exp_e, ALU.mult)
                L.link(v.tensor_tensor(rb, hots[1], exp_e, ALU.mult))
                v.reduce_sum(few[:, F_P1, :], ra, axis=AX.X)
                L.link(v.reduce_sum(few[:, F_P2, :], rb, axis=AX.X))
                for s in range(2):
                    v.tensor_copy(pos_u[:, s, :], few[:, F_P1 + s, :])
                L.link(v.tensor_tensor(past[layer][0:1, :, :],
                                       sm[0:1, S_IOTA:S_IOTA + BLOCKS].unsqueeze(2).to_broadcast([1, BLOCKS, e]),
                                       ends[0:1, :].unsqueeze(1).to_broadcast([1, BLOCKS, e]), ALU.is_ge))
                L.link(v.reduce_sum(block_at[0:1, :], past[layer][0:1, :, :], axis=AX.X))
                v.tensor_scalar(table[:, :], block_at[0:1, :], float(e - 1), None, ALU.min).then_inc(routed, 1)

            def score_pair(c, u, h):
                for t in (2 * h, 2 * h + 1):
                    q = qkv[u][:, t, 0:D].rearrange("p (h d) -> p h d", d=DH).unsqueeze(2).to_broadcast([P, H, H, DH])
                    k = qkv[u][:, t, D:2 * D].rearrange("p (g d) -> p g d", d=DH).unsqueeze(1)\
                        .to_broadcast([P, H, H, DH])
                    L.link(v.tensor_tensor(prod, q, k, ALU.mult))
                    L.link(v.reduce_sum(score[:, t, :, :], prod, axis=AX.X))
                    if t == 0:
                        yield
                s = score[:, 2 * h:2 * h + 2, :, :]
                L.link(v.reduce_max(head_max, s, axis=AX.X))
                v.tensor_tensor(s, s, head_max.unsqueeze(3).to_broadcast([P, 2, H, H]), ALU.subtract)\
                    .then_inc(score_ready, 1)

            def mix_pair(c, u, h):
                dve.wait_ge(prob_ready, c * 2 + h + 1)
                v.reduce_sum(head_sum, score[:, 2 * h:2 * h + 2, :, :], axis=AX.X)
                prod_v = prod.rearrange("p h g d -> p (h g d)").rearrange("p (h d g) -> p h d g", d=DH, g=H)
                for t in (2 * h, 2 * h + 1):
                    p = score[:, t, :, :].unsqueeze(2).to_broadcast([P, H, DH, H])
                    w = qkv[u][:, t, 2 * D:3 * D].rearrange("p (d g) -> p d g", g=H).unsqueeze(1)\
                        .to_broadcast([P, H, DH, H])
                    L.link(v.tensor_tensor(prod_v, p, w, ALU.mult))
                    if t == 2 * h:
                        v.reciprocal(head_rec, head_sum)
                    L.link(v.reduce_sum(att[:, t, :].rearrange("p (h d) -> p h d", d=DH), prod_v, axis=AX.X))
                out_t = att[:, 2 * h:2 * h + 2, :].rearrange("p t (h d) -> p t h d", d=DH)
                last = v.tensor_tensor(out_t, out_t, head_rec.unsqueeze(3).to_broadcast([P, 2, H, DH]), ALU.mult)
                if h == 1:
                    last.then_inc(att_done, 1)

            def add_y(c):
                dve.wait_ge(yT_filled, c + 1)
                x_now = x_all[:, bass.ds(c * TILES, TILES), :]
                v.tensor_tensor(x_now, x_now, psT[:, :].rearrange("p (t d) -> p t d", d=D), ALU.add)\
                    .then_inc(y_added, 1)

            def shared_hidden(c, f):
                dve.wait_ge(silu_ready, c * HALVES + f + 1)
                dve.wait_ge(up_done, c * HALVES + f + 1)
                v.tensor_tensor(hid[:, f, :], hid[:, f, :], psQ1[:, :], ALU.mult).then_inc(hid_ready, 1)

            def att_chunk(c, u, first=False, last=False, point=lambda n: None):
                dve.wait_ge(qkv_copied, c * TILES + TILES)
                for _ in score_pair(c, u, 0):
                    if not first:
                        add_y(c - 1)
                point(0)
                for _ in score_pair(c, u, 1):
                    pass
                point(1)
                if not last:
                    shared_hidden(c + 1, 0)
                mix_pair(c, u, 0)
                point(2)
                if not last:
                    shared_hidden(c + 1, 1)
                mix_pair(c, u, 1)
                point(3)

            def add_experts(layer, c, target):
                uses = layer * (CHUNKS // RING + (1 if c % RING < CHUNKS % RING else 0)) + c // RING + 1
                dve.wait_ge(gathered[c % RING], uses * 2 * TILES * 16)
                for s in range(2):
                    for j in range(TILES):
                        n = c * TILES + j
                        last = v.scalar_tensor_tensor(target[:, n, :], rings[:, (c % RING * TILES + j) * 2 + s, :],
                                                      w_pair[:, s, n:n + 1], target[:, n, :], ALU.mult, ALU.add)
                    if s == 0:
                        L.link(last)
                last.then_inc(mixed, 1)
                dve.wait_ge(mixed, layer * CHUNKS + c + 1)

            def finish(c):
                add_experts(1, c, xn_all)
                now = slice(c * TILES, (c + 1) * TILES)
                L.link(v.tensor_scalar(xn_all[:, now, :], xn_all[:, now, :], -100.0, 100.0, ALU.max, ALU.min))
                v.tensor_tensor(x_all[:, now, :], x_all[:, now, :], xn_all[:, now, :], ALU.add).then_inc(out_ready, 1)

            def chain(pair, point=lambda n: None):
                def chunk(a, u):
                    return a[:, bass.ds((pair * 2 + u) * TILES, TILES), :]

                def statistics(src):
                    for u in range(2):
                        for t in range(TILES):
                            last = v.bn_stats(ch_stats[u][:, t, :], src(u, t))
                    link_alone(last)
                    for u in range(2):
                        for t in range(TILES):
                            last = v.bn_aggr(ch_mv[:, u * TILES + t, :], ch_stats[u][:, t, :])
                    L.link(last)
                    inverse_root(ch_rstd[:, :], ch_mv[:, :, 1], 2 * TILES)

                def apply(src):
                    for u in range(2):
                        for t in range(TILES):
                            n = u * TILES + t
                            last = v.tensor_scalar(z_tok[u][:, t, :], src(u, t), ch_mv[:, n, 0:1],
                                                   ch_rstd[:, n:n + 1], ALU.subtract, ALU.mult)
                        last.then_inc(z_ready[u], 1)

                def running_mean():
                    for u in range(2):
                        if first:
                            dve.wait_ge(q_ready[u], pair + 1)
                        for s in range(SEQS):
                            seq = slice(s * SEQ, (s + 1) * SEQ)
                            last = v.tensor_tensor_scan(scan[u][:, seq], ones_f[:, :], qT[u][:, seq], 0.0,
                                                        ALU.mult, ALU.add)
                    L.link(last)
                    for u in range(2):
                        last = v.tensor_tensor(pooled[u].rearrange("p (s n) -> p s n", n=SEQ),
                                               scan[u].rearrange("p (s n) -> p s n", n=SEQ),
                                               inv_count[:, :].unsqueeze(1).to_broadcast([P, SEQS, SEQ]), ALU.mult)
                    L.link(last)

                def xn_tile(u, t):
                    return tile_of(xn_all, (pair * 2 + u) * TILES + t)

                statistics(xn_tile)
                apply(xn_tile)
                point(0)
                for u in range(2):
                    dve.wait_ge(conv_done[u], pair + 1)
                    last = v.tensor_tensor(x2[u], chunk(xn_all, u), chM[u][:, :].rearrange("p (t d) -> p t d", d=D),
                                           ALU.add)
                link_alone(last)
                statistics(lambda u, t: x2[u][:, t, :])
                apply(lambda u, t: x2[u][:, t, :])
                point(1)
                first = True
                running_mean()
                first = False
                for u in range(2):
                    dve.wait_ge(k_done[u], pair + 1)
                    v.scalar_tensor_tensor(qT[u], chT[u][:, :], cv[:, C_BK:C_BK + 1], pooled[u],
                                           ALU.add, ALU.mult).then_inc(k_read[u], 1)
                for u in range(2):
                    dve.wait_ge(k_read[u], pair + 1)
                running_mean()
                for u in range(2):
                    dve.wait_ge(v_done[u], pair + 1)
                    v.scalar_tensor_tensor(pooled[u], chM[u][:, :], cv[:, C_BV:C_BV + 1], pooled[u],
                                           ALU.add, ALU.mult).then_inc(pkv_ready[u], 1)
                for u in range(2):
                    dve.wait_ge(pkvT_filled[u], pair + 1)
                    v.tensor_tensor(x2[u], x2[u], chT[u][:, :].rearrange("p (t d) -> p t d", d=D), ALU.add)\
                        .then_inc(res_read[u], 1)
                wait_alone((res_read[0], pair * 2 + 1), (res_read[1], pair * 2 + 1))
                statistics(lambda u, t: x2[u][:, t, :])
                apply(lambda u, t: x2[u][:, t, :])
                point(2)
                for u in range(2):
                    dve.wait_ge(mlpT_filled[u], pair + 1)
                    v.tensor_tensor(x2[u], x2[u], chT[u][:, :].rearrange("p (t d) -> p t d", d=D), ALU.add)\
                        .then_inc(res_read[u], 1)
                for u in range(2):
                    dve.wait_ge(res_read[u], pair * 2 + 2)
                    last = v.tensor_tensor(chunk(x_all, u), chunk(x_all, u), x2[u], ALU.add)
                L.link(last)

            norm_all(0)
            route(0)
            for f in range(HALVES):
                shared_hidden(0, f)
            for c in range(2 * BLOCK_PAIRS[0]):
                att_chunk(c, c % 2, first=(c == 0))
            with dve.Fori(BLOCK_PAIRS[0], BLOCK_PAIRS[-1] + 1) as pair:
                L.enter(pair + (-BLOCK_PAIRS[0]), LINKS_ATT)
                for u in range(2):
                    att_chunk(pair * 2 + u, u)
            L.leave(len(BLOCK_PAIRS))
            late, added = 2 * BLOCK_PAIRS[-1] + 2, 0
            for c in range(late, CHUNKS):
                def point(n):
                    if (c - late) * 4 + n >= 2:
                        add_experts(0, (c - late) * 4 + n - 2, x_all)
                att_chunk(c, c % 2, last=(c == CHUNKS - 1), point=point)
            add_y(CHUNKS - 1)
            dve.wait_ge(y_added, CHUNKS)
            for c in range(4 * (CHUNKS - late) - 2, CHUNKS):
                add_experts(0, c, x_all)
            wait_alone((mixed, CHUNKS))

            norm_all(1)
            route(1)
            for u in range(2):
                v.memset(convT[u][:, :, 0:TAPS - 1], 0.0)
            wait_alone((xn_moved[0], (2 * GROUPS + 1) * 16), (xn_moved[1], (2 * GROUPS + 1) * 16))
            chain(0)
            with dve.Fori(0, BLOCK_PAIRS[-1]) as i:
                L.enter(i, LINKS_CHAIN)
                chain(i + 1)
            L.leave(BLOCK_PAIRS[-1])
            done = 0
            for pair in range(BLOCK_PAIRS[-1] + 1, PAIRS):
                def point(n):
                    nonlocal done
                    upto = LATE_MIXES[(pair - BLOCK_PAIRS[-1] - 1) * 3 + n]
                    for c in range(done, upto):
                        finish(c)
                    done = upto
                chain(pair, point)
            for c in range(done, CHUNKS):
                finish(c)


def _packs(a):
    f32 = np.float32
    g = {k: np.asarray(v) for k, v in a.items()}
    small = np.zeros((P, S_END), f32)

    def put(at, m):
        small[:m.shape[0], at:at + m.shape[1]] = m

    put(S_WQ, g["L0_attn_Wq"])
    put(S_GATE0, g["L0_ffn_gate_w"])
    put(S_WOUT, g["L0_attn_Wout"])
    put(S_GATE1, g["L1_ffn_gate_w"].T)
    conv = g["L1_attn_conv_w"]
    width = conv.shape[1]
    for k in range(TAPS):
        for o in range(D // width):
            small[o * width:(o + 1) * width, S_CONV + k * D + o * width:S_CONV + k * D + (o + 1) * width] = \
                conv[o * width:(o + 1) * width, :, k].T
    put(S_WQ1, g["L1_attn_Wq"].T)
    put(S_WK1, g["L1_attn_Wk"].T)
    put(S_WV1, g["L1_attn_Wv"].T)
    put(S_WB, g["L1_attn_Wb"].T)
    put(S_WU, g["L1_attn_Wu"].T.reshape(BOOM, P, D).transpose(1, 0, 2).reshape(P, BOOM * D))
    put(S_ID, np.eye(P, dtype=f32))
    put(S_IOTA, np.tile(np.arange(BLOCKS, dtype=f32), (P, 1)))
    put(S_COUNT, np.tile(np.arange(1, SEQ + 1, dtype=f32), (P, 1)))

    put(S_BEFORE, np.triu(np.ones((P, P), f32), 1))

    narrow = np.zeros((LAT, N_END), f32)

    def kv_order(m):
        m = m.reshape(m.shape[0], H, 2, DH)
        return np.concatenate([m[:, :, 0].reshape(-1, D), m[:, :, 1].transpose(0, 2, 1).reshape(-1, D)], axis=1)

    narrow[:, N_WDOWN:N_WDOWN + D] = g["L0_attn_Wdown"].T
    narrow[:, N_WUP:N_WUP + 2 * D] = kv_order(g["L0_attn_Wup"])
    narrow[:, N_BDOWN] = g["L0_attn_bdown"]
    narrow[0, N_BUP:N_BUP + 2 * D] = kv_order(g["L0_attn_bup"][None])[0]
    narrow[0, N_BQ:N_BQ + D] = g["L0_attn_bq"]
    narrow[0, N_CONVB:N_CONVB + D] = g["L1_attn_conv_b"]
    narrow[0:E1, N_B12:N_B12 + F] = g["L1_ffn_b1"]
    narrow[0:E1, N_B12 + F:N_END] = g["L1_ffn_b2"]

    cols = np.stack(
        [g["L1_attn_" + n] for n in ("ln_conv_g", "ln_conv_b", "ln_attn_g", "ln_attn_b", "ln_boom_g", "ln_boom_b",
                                     "bq", "bk", "bv")]
        + [g["L0_attn_bout"], g["L1_attn_bu"]] + list(g["L1_attn_bb"].reshape(BOOM, P)), axis=1)

    def with_shared(e, s):
        return np.concatenate([g[e], g[s][None]], axis=0)

    def halves(m):
        return m.reshape(m.shape[0], HALVES, P, D).transpose(2, 0, 1, 3)

    return {
        "x": g["L0_attn_x"].reshape(-1, D),
        "small": small,
        "narrow": narrow,
        "cols": cols,
        "wgu0": np.concatenate([with_shared("L0_ffn_w_gate", "L0_ffn_ws_gate"),
                                with_shared("L0_ffn_w_up", "L0_ffn_ws_up")], axis=2).transpose(1, 0, 2),
        "wd0": halves(with_shared("L0_ffn_w_down", "L0_ffn_ws_down")),
        "w1": g["L1_ffn_w1"].transpose(1, 0, 2),
        "w2": halves(g["L1_ffn_w2"]),
    }


def kernel(**inputs):
    import concourse.bacc as _bacc
    from concourse.bass_utils import run_bass_kernel_spmd as _run

    shape = np.asarray(inputs["L0_attn_x"]).shape
    arrays = {k: np.ascontiguousarray(v) for k, v in _packs(inputs).items()}
    nc = _bacc.Bacc("TRN2", target_bir_lowering=False, num_devices=1)
    args = {k: nc.dram_tensor(k, a.shape, mybir.dt.from_np(a.dtype), kind="ExternalInput").ap()
            for k, a in arrays.items()}
    out = nc.dram_tensor("out", arrays["x"].shape, FP32, kind="ExternalOutput").ap()
    two_layers(nc, **args, out=out)
    r = _run(nc, [arrays], core_ids=[0])
    return r.results[0]["out"].reshape(shape)
```

```python
from contextlib import ExitStack

import numpy as np

import concourse.bass as bass
from concourse import mybir

FP32 = mybir.dt.float32
BF16 = mybir.dt.bfloat16
U32 = mybir.dt.uint32
I32 = mybir.dt.int32
ALU = mybir.AluOpType
ACT = mybir.ActivationFunctionType
AX = mybir.AxisListType

P = 128
D = 128
SEQ = 256
CHUNK = 512
TILES = CHUNK // P
SEQS = CHUNK // SEQ
TOKENS = 32 * SEQ
ALL_TILES = TOKENS // P
CHUNKS = TOKENS // CHUNK
GROUP = 16
GROUPS = ALL_TILES // GROUP
H, DH = 16, 8
E0, F = 8, 256
HALVES = F // P
E1 = 14
EXPERTS = (E0, E1)
TAPS = 4
LAT = 32
BOOM = 4
QKV = 3 * D
PART_ROWS = 65
EPS = 1e-5
ROOT_GUESS = float(0x5F3759DF)
ROOT_STEPS = 3
ROOT_LINKS = 2 + 3 * ROOT_STEPS
SCALE = float(DH) ** -0.5
BIG = 3e38

LOAD = 4
RING = (2, 3)
STEP_BLOCKS = (LOAD * RING[0], LOAD * RING[1])
BLOCKS = -(-(2 * ALL_TILES + E1 - 1) // (2 * LOAD)) * 2 * LOAD
PASSES = (BLOCKS // STEP_BLOCKS[0], BLOCKS // STEP_BLOCKS[1])
assert PASSES[0] * STEP_BLOCKS[0] == BLOCKS and PASSES[1] * STEP_BLOCKS[1] == BLOCKS
SLOTS = BLOCKS * P
ZERO_ROWS = 8
ROWS_RING = 3
BLOCK_CHUNKS = range(3, 12)
CHUNK_BLOCKS = BLOCKS // len(BLOCK_CHUNKS)
BLOCK_PAIRS = range(2, 6)
PAIR_BLOCKS = BLOCKS // len(BLOCK_PAIRS)
ATT_BEATS = (1, 1, 1, 1, 1, 1, 2, 2, 3, 3)
CHAIN_BEATS = (6, 2, 6, 2, 2, 4, 6, 2, 4, 2)
LATE_MIXES = (0, 3, 6, 9, 12, 14)
assert sum(ATT_BEATS) == CHUNK_BLOCKS and CHUNK_BLOCKS % STEP_BLOCKS[0] == 0
assert CHUNK_BLOCKS * len(BLOCK_CHUNKS) == BLOCKS
assert sum(CHAIN_BEATS) == PAIR_BLOCKS and PAIR_BLOCKS % STEP_BLOCKS[1] == 0
assert PAIR_BLOCKS * len(BLOCK_PAIRS) == BLOCKS


def earlier_uses(layer, slot):
    return layer * (PASSES[0] if slot < RING[0] else 0)


(C_GCONV, C_BCONV, C_GATTN, C_BATTN, C_GBOOM, C_BBOOM, C_BQ, C_BK, C_BV, C_BOUT, C_BU, C_ROW, C_BB) = range(13)
COLS = C_BB + BOOM

S_WQ = 0
S_GATE0 = S_WQ + D
S_WOUT = S_GATE0 + E0
S_GATE1 = S_WOUT + D
S_CONV = S_GATE1 + E1
S_WQ1 = S_CONV + TAPS * D
S_WK1 = S_WQ1 + D
S_WV1 = S_WK1 + D
S_WB = S_WV1 + D
S_WU = S_WB + BOOM * D
S_ID = S_WU + BOOM * D
S_IOTA = S_ID + D
S_COUNT = S_IOTA + BLOCKS
S_BEFORE = S_COUNT + SEQ
S_PAST = S_BEFORE + P
S_END = S_PAST + E0

N_WDOWN = 0
N_WUP = N_WDOWN + D
N_BDOWN = N_WUP + 2 * D
N_BUP = N_BDOWN + 1
N_BQ = N_BUP + 2 * D
N_CONVB = N_BQ + D
N_B12 = N_CONVB + D
N_END = N_B12 + F + D


class Links:

    def __init__(self, engine, semaphore):
        self.engine, self.semaphore = engine, semaphore
        self.base, self.start, self.count = 0, 0, 0

    def enter(self, i, per_pass):
        self.base = self.base + self.count
        self.start, self.count, self.per_pass = i * per_pass + self.base, 0, per_pass

    def leave(self, passes):
        assert self.count == self.per_pass, self.count
        self.base = self.base + passes * self.per_pass
        self.start, self.count = self.base, 0

    def mark(self, ins):
        self.count += 1
        ins.then_inc(self.semaphore, 1)

    def value(self):
        return self.start + self.count

    def link(self, ins):
        self.mark(ins)
        self.engine.wait_ge(self.semaphore, self.value())


def two_layers(nc, x, small, narrow, cols, wgu0, wd0, w1, w2, out):
    x_tiles = x.rearrange("(t p) d -> p t d", p=P)
    out_tiles = out.rearrange("(t p) d -> p t d", p=P)
    xs = nc.dram_tensor("xs", (SLOTS + E0 * P, D), FP32).ap()
    ys = nc.dram_tensor("ys", (SLOTS, D), FP32).ap()

    ctx = ExitStack()
    with ctx:
        def sb(name, shape, dt=FP32):
            return ctx.enter_context(nc.sbuf_tensor(name, shape, dt))

        def pb(name):
            return ctx.enter_context(nc.psum_tensor(name, [P, CHUNK], FP32))

        def sem(name):
            return ctx.enter_context(nc.semaphore(name))

        x_all = sb("x_all", [P, ALL_TILES, D])
        xn_all = sb("xn_all", [P, ALL_TILES, D])
        sm = sb("sm", [P, S_END])
        cv = sb("cv", [P, COLS])
        wgu0_sb = sb("wgu0_sb", [P, E0 + 1, 2 * F])
        wd0_sb = sb("wd0_sb", [P, E0 + 1, HALVES, D])
        w1_sb = sb("w1_sb", [P, E1, F])
        w2_sb = sb("w2_sb", [P, E1, HALVES, D])
        wqkv = sb("wqkv", [P, QKV])
        bias_parts = sb("bias_parts", [PART_ROWS, 2, QKV], BF16)
        b12_parts = sb("b12_parts", [3, E1, F + D], BF16)
        ones_h = sb("ones_h", [P, P], BF16)
        before_h = sb("before_h", [P, P], BF16)
        inv_count = sb("inv_count", [P, SEQ])
        ones_f = sb("ones_f", [P, SEQ])
        idle = sb("idle", [P, 64])
        ident = sm[:, S_ID:S_ID + D]

        w_pair = sb("w_pair", [P, 2, ALL_TILES])
        pos_u = sb("pos_u", [P, 2, ALL_TILES], U32)
        pad_u = sb("pad_u", [P, E0], U32)
        pad_f = sb("pad_f", [P, 3, E0])
        table = sb("table", [1, BLOCKS], I32)
        mv_group = sb("mv_group", [P, GROUP, 2])
        rstd_group = sb("rstd_group", [P, GROUP])
        stats = sb("stats", [P, GROUP, 6])
        var_eps = sb("var_eps", [P, GROUP])
        newton = sb("newton", [P, GROUP])
        few = sb("few", [P, 10, ALL_TILES])

        rings = sb("rings", [P, 2 * STEP_BLOCKS[1], D])
        xb = rings[:, 0:STEP_BLOCKS[1], :]
        yb = rings[:, STEP_BLOCKS[1]:2 * STEP_BLOCKS[1], :]
        zeros = rings[:, 0:ZERO_ROWS, :]
        fresh = [rings[:, 8 + 8 * h:16 + 8 * h, :] for h in range(2)]
        assert 2 * ROWS_RING * TILES <= 2 * STEP_BLOCKS[1]
        xbT = sb("xbT", [P, 2, P])
        act_b = sb("act_b", [P, 2, F])
        hid_b = sb("hid_b", [P, 2, F])
        hT_b = sb("hT_b", [P, 2, F])

        work = sb("work", [P, 8960])

        def piece(at, shape):
            n = int(np.prod(shape))
            flat = work[:, at:at + n]
            if len(shape) == 1:
                return flat
            names = "abcd"[:len(shape)]
            return flat.rearrange("p (%s) -> p %s" % (" ".join(names), " ".join(names)),
                                  **{k: s for k, s in zip(names[1:], shape[1:])})

        xnT = [piece(0, [CHUNK]), piece(CHUNK, [CHUNK])]
        NE = ALL_TILES * E1
        lg = [piece(1024, [ALL_TILES, e]) for e in EXPERTS]
        ex = [piece(1024 + NE, [ALL_TILES, e]) for e in EXPERTS]
        rank_a = [piece(1024 + 2 * NE, [ALL_TILES, e]) for e in EXPERTS]
        hot = [[piece(1024 + (3 + s) * NE, [ALL_TILES, e]) for s in range(2)] for e in EXPERTS]
        rank_b = [piece(1024 + 5 * NE, [ALL_TILES, e]) for e in EXPERTS]
        both_h = [piece(1024 + 6 * NE, [NE // 2]).bitcast(BF16)[:, 0:ALL_TILES * e] for e in EXPERTS]
        cum = [piece(1472 + 6 * NE, [e, ALL_TILES]) for e in EXPERTS]
        total = [piece(1472 + 7 * NE, [e, ALL_TILES]) for e in EXPERTS]
        past = [piece(1024, [BLOCKS, e]) for e in EXPERTS]
        block_at = sb("block_at", [1, BLOCKS])
        int_e = sb("int_e", [P, 2, E1], I32)
        F_M1, F_I1, F_M2, F_I2, F_Z, F_P1, F_P2, F_E2, F_SUM, F_NB = range(10)
        attT = xnT[0]
        yT = xnT[0]
        x_fixed = piece(CHUNK, [TILES, D])
        qkv = [piece(1024, [TILES, QKV]), piece(2560, [TILES, QKV])]
        prod = [piece(4096, [H, H, DH]),
                w2_sb[:, :, :, :].rearrange("p e f d -> p (e f d)")[:, 0:H * H * DH]
                .rearrange("p (h g d) -> p h g d", h=H, g=H)]
        score = piece(6144, [TILES, H, H])
        att = piece(7168, [TILES, D])
        hid = piece(7680, [HALVES, CHUNK])
        head_max = piece(8704, [2, H])
        head_sum = piece(8736, [2, H])
        head_rec = piece(8768, [2, H])
        C_SIZE = 4112
        convT = [piece(u * C_SIZE, [SEQS, TAPS - 1 + SEQ]) for u in range(2)]
        z_tok = [piece(u * C_SIZE + 520, [TILES, D]) for u in range(2)]
        x2 = [piece(u * C_SIZE + 1032, [TILES, D]) for u in range(2)]
        hT = [piece(u * C_SIZE + 1544, [CHUNK]) for u in range(2)]
        mlpT = hT
        gb = [piece(u * C_SIZE + 2056, [BOOM, CHUNK]) for u in range(2)]
        qT = [gb[u][:, 0, :] for u in range(2)]
        scan = [gb[u][:, 1, :] for u in range(2)]
        pooled = [gb[u][:, 2, :] for u in range(2)]
        ch_stats = [sb("ch_stats%d" % u, [P, TILES, 6]) for u in range(2)]
        ch_mv = sb("ch_mv", [P, 2 * TILES, 2])
        ch_rstd = sb("ch_rstd", [P, 2 * TILES])
        nr = piece(4700, [N_END])
        bias_row = piece(7400, [2, QKV])
        mid_row = piece(8200, [QKV]).bitcast(BF16).rearrange("p (a b) -> p a b", a=2)
        b12_rest = piece(6400, [F + D])
        b12_split = piece(6800, [3 * (F + D) // 2]).bitcast(BF16).rearrange("p (a b) -> p a b", a=3)

        psX, psG, psH, psD, psT, psQ0, psQ1, psY = [
            pb(n) for n in ("psX", "psG", "psH", "psD", "psT", "psQ0", "psQ1", "psY")]
        psQ = (psQ0, psQ1)
        chT = (psT, psQ0)
        chM = (psQ1, psY)

        w_small = sem("w_small")
        w_layer0 = sem("w_layer0")
        w_layer1 = sem("w_layer1")
        x_loaded = sem("x_loaded")
        prep_pe = sem("prep_pe")
        prep_act = sem("prep_act")
        prep_dve = sem("prep_dve")
        prep_pool = sem("prep_pool")
        split_ready = sem("split_ready")
        b12_loaded = sem("b12_loaded")
        zeros_ready = sem("zeros_ready")
        zeros_sent = sem("zeros_sent")
        pads_known = sem("pads_known")
        pads_sent = sem("pads_sent")
        dve_step = sem("dve_step")
        xn_done = sem("xn_done")
        xn_moved = [sem("xn_moved%d" % h) for h in range(2)]
        x_fixed_loaded = sem("x_fixed_loaded")
        nT_filled = sem("nT_filled")
        nT_copied = sem("nT_copied")
        lg_done = sem("lg_done")
        lg_copied = sem("lg_copied")
        shifted = sem("shifted")
        exped = sem("exped")
        hot_ready = sem("hot_ready")
        ranked = sem("ranked")
        placed = sem("placed")
        routed = sem("routed")
        scattered = sem("scattered")
        xb_loaded = [sem("xb_loaded%d" % s) for s in range(RING[1])]
        ys_sent = [sem("ys_sent%d" % s) for s in range(RING[1])]
        xbT_filled = sem("xbT_filled")
        xbT_ready = sem("xbT_ready")
        gu_done = sem("gu_done")
        act_ready = sem("act_ready")
        up_b_ready = sem("up_b_ready")
        hid_b_ready = sem("hid_b_ready")
        hTb_filled = sem("hTb_filled")
        hTb_ready = sem("hTb_ready")
        dn_done = sem("dn_done")
        yb_ready = sem("yb_ready")
        gathered = [sem("gathered%d" % s) for s in range(ROWS_RING)]
        mixed = sem("mixed")
        xT_filled = sem("xT_filled")
        xT_copied = sem("xT_copied")
        qkv_done = sem("qkv_done")
        qkv_copied = sem("qkv_copied")
        gate_done = sem("gate_done")
        silu_ready = sem("silu_ready")
        up_done = sem("up_done")
        hid_ready = sem("hid_ready")
        down_done = sem("down_done")
        score_ready = sem("score_ready")
        prob_ready = sem("prob_ready")
        att_done = sem("att_done")
        attT_filled = sem("attT_filled")
        attT_copied = sem("attT_copied")
        y_done = sem("y_done")
        yT_ready = sem("yT_ready")
        yT_filled = sem("yT_filled")
        y_added = sem("y_added")

        def two(name):
            return [sem("%s%d" % (name, u)) for u in range(2)]
        z_ready = two("z_ready")
        zT_filled = two("zT_filled")
        zT_copied = two("zT_copied")
        conv_done = two("conv_done")
        q_done = two("q_done")
        q_ready = two("q_ready")
        k_done = two("k_done")
        v_done = two("v_done")
        k_read = two("k_read")
        pkv_ready = two("pkv_ready")
        pkvT_filled = two("pkvT_filled")
        res_read = two("res_read")
        boom_done = two("boom_done")
        boom_ready = two("boom_ready")
        mlp_done = two("mlp_done")
        mlpT_ready = two("mlpT_ready")
        mlpT_filled = two("mlpT_filled")
        out_ready = sem("out_ready")
        out_sent = sem("out_sent")

        PAIRS = CHUNKS // 2
        LINKS_ATT = 28
        LINKS_CHAIN = 12 + 3 * ROOT_LINKS

        block = ctx.enter_context(nc.Block())

        def block_from(n, each, offset=0):
            def step_of(k, step):
                return n * each + (offset + k), n * (each // step) + (offset + k) // step, (offset + k) % step
            return step_of

        def tile_of(a, n):
            return a[:, bass.ds(n, 1), :].squeeze(1)

        @block.sync
        def _(sp):
            for h in range(2):
                sp.sem_inc(xn_moved[h], 16)
            sp.dma_start(sm[:, :], small).then_inc(w_small, 16)
            sp.dma_start(nr[0:LAT, :], narrow).then_inc(w_small, 16)
            sp.dma_start(cv[:, :], cols).then_inc(w_small, 16)
            sp.dma_start(x_all[:, 0:8, :], x_tiles[:, 0:8, :]).then_inc(x_loaded, 16)
            with sp.Fori(1, ALL_TILES // 8) as g:
                sp.wait_ge(x_loaded, g * 16)
                sp.dma_start(x_all[:, bass.ds(g * 8, 8), :],
                             x_tiles[:, bass.ds(g * 8, 8), :]).then_inc(x_loaded, 16)
            sp.wait_ge(zeros_ready, 1)
            rows = ZERO_ROWS * P
            for at in range(2 * TOKENS, SLOTS, rows):
                sp.dma_start(xs[at:at + rows, :].rearrange("(p r) d -> p r d", p=P), zeros)\
                    .then_inc(zeros_sent, 16)
            def move_xn(layer):
                with sp.Fori(0, GROUPS) as g:
                    for h in range(2):
                        sp.wait_ge(xn_done, (g + layer * GROUPS) * 2 + h + 1)
                        sp.dma_start(xn_all[:, bass.ds(g * GROUP + 8 * h, 8), :], fresh[h])\
                            .then_inc(xn_moved[h], 16)

            def load_weights():
                sp.wait_ge(split_ready, 1)
                for k in range(3):
                    sp.dma_start(b12_parts[k:k + 1, :, :], b12_split[0:E1, k, :]).then_inc(b12_loaded, 16)
                sp.dma_start(wgu0_sb[:, :, :], wgu0).then_inc(w_layer0, 16)
                sp.dma_start(wd0_sb[:, :, :], wd0).then_inc(w_layer0, 16)
                sp.dma_start(w1_sb[:, :, :], w1).then_inc(w_layer1, 16)

            def load(n, slot):
                rows = xs[bass.ds(n * (LOAD * P), LOAD * P), :].rearrange("(b p) d -> p b d", p=P)
                sp.dma_start(xb[:, slot * LOAD:(slot + 1) * LOAD, :], rows).then_inc(xb_loaded[slot], 16)

            for layer in range(2):
                move_xn(layer)
                if layer == 0:
                    load_weights()
                else:
                    sp.wait_ge(att_done, CHUNKS)
                    sp.dma_start(w2_sb[:, :, :], w2).then_inc(w_layer1, 16)
                sp.wait_ge(pads_sent, E0 * 16)
                sp.wait_ge(zeros_sent, (SLOTS - 2 * TOKENS) // (ZERO_ROWS * P) * 16)
                sp.wait_ge(scattered, (layer + 1) * 2 * ALL_TILES * 16)
                for slot in range(RING[layer]):
                    load(slot, slot)
                with sp.Fori(0, PASSES[layer] - 1) as i:
                    for slot in range(RING[layer]):
                        sp.wait_ge(xbT_filled, i * STEP_BLOCKS[layer] + layer * BLOCKS + (slot + 1) * LOAD)
                        load(i * RING[layer] + RING[layer] + slot, slot)

            with sp.Fori(0, CHUNKS) as c:
                sp.wait_ge(out_ready, c + 1)
                sp.dma_start(out_tiles[:, bass.ds(c * TILES, TILES), :],
                             x_all[:, bass.ds(c * TILES, TILES), :]).then_inc(out_sent, 16)
            sp.wait_ge(out_sent, 16 * CHUNKS)

        @block.gpsimd
        def _(pool):
            nc.gpsimd.memset(zeros, 0.0).then_inc(zeros_ready, 1)
            nc.gpsimd.memset(bias_parts[:, :, :], 0.0)
            nc.gpsimd.memset(ones_h[:, :], 1.0)
            nc.gpsimd.memset(ones_f[:, :], 1.0).then_inc(prep_pool, 1)

            def scatter(t):
                for s in range(2):
                    pool.indirect_dma_start(xs, bass.IndirectOffsetOnAxis(ap=pos_u[:, s, t:t + 1], axis=0),
                                            xn_all[:, t, :], None).then_inc(scattered, 16)

            def gather(layer, c, half):
                if c >= ROWS_RING and half == 0:
                    pool.wait_ge(mixed, layer * CHUNKS + c - ROWS_RING + 1)
                for j in (2 * half, 2 * half + 1):
                    for s in range(2):
                        pool.indirect_dma_start(
                            rings[:, (c % ROWS_RING * TILES + j) * 2 + s, :], None, ys,
                            bass.IndirectOffsetOnAxis(ap=pos_u[:, s, c * TILES + j:c * TILES + j + 1], axis=0))\
                            .then_inc(gathered[c % ROWS_RING], 16)

            def wait_stored(layer):
                for slot in range(RING[layer]):
                    pool.wait_ge(ys_sent[slot], (earlier_uses(layer, slot) + PASSES[layer]) * 16)

            def wait_moved(layer):
                for h in range(2):
                    pool.wait_ge(xn_moved[h], ((layer + 1) * GROUPS + 1) * 16)

            pool.wait_ge(zeros_ready, 1)
            pool.wait_ge(pads_known, 1)
            for e in range(E0):
                pool.indirect_dma_start(xs, bass.IndirectOffsetOnAxis(ap=pad_u[:, e:e + 1], axis=0),
                                        zeros[:, 0, :], None).then_inc(pads_sent, 16)
            pool.wait_ge(placed, 1)
            wait_moved(0)
            for t in range(ALL_TILES):
                scatter(t)
            with pool.Fori(0, PASSES[0]) as i:
                for k in range(STEP_BLOCKS[0]):
                    pool.wait_ge(up_b_ready, i * STEP_BLOCKS[0] + k + 1)
                    nc.gpsimd.tensor_tensor(hid_b[:, k % 2, :], act_b[:, k % 2, :], hid_b[:, k % 2, :], ALU.mult)\
                        .then_inc(hid_b_ready, 1)
            wait_stored(0)
            for n in range(2 * CHUNKS):
                gather(0, n // 2, n % 2)
            pool.wait_ge(placed, 2)
            wait_moved(1)
            for t in range(ALL_TILES):
                scatter(t)
            wait_stored(1)
            for n in range(2 * CHUNKS):
                gather(1, n // 2, n % 2)

        @block.tensor
        def _(pe):
            def transposes(bank, src):
                for t in range(TILES):
                    last = nc.tensor.transpose(bank[:, t * P:(t + 1) * P], src(t), ident)
                return last

            def logits(layer):
                e = EXPERTS[layer]
                gate_w = sm[:, S_GATE0:S_GATE0 + E0] if layer == 0 else sm[:, S_GATE1:S_GATE1 + E1]
                with pe.Fori(0, GROUPS) as g:
                    chunk0 = g * (GROUP // TILES) + layer * CHUNKS
                    for k in range(GROUP // TILES + 1):
                        if k < GROUP // TILES:
                            if k % 2 == 0:
                                pe.wait_ge(xn_done, (g + layer * GROUPS) * 2 + k // 2 + 1)
                            if k >= 2:
                                pe.wait_ge(nT_copied, chunk0 + k - 1)
                            transposes(psQ[k % 2], lambda t: fresh[k // 2][:, k % 2 * TILES + t, :])\
                                .then_inc(nT_filled, 1)
                        if k:
                            pe.wait_ge(nT_copied, chunk0 + k)
                            if k == 1:
                                pe.wait_ge(lg_copied, g + layer * GROUPS + 1)
                            for t in range(TILES):
                                at = ((k - 1) * TILES + t) * e
                                last = nc.tensor.matmul(psY[:, at:at + e], xnT[(k - 1) % 2][:, t * P:(t + 1) * P],
                                                        gate_w, start=True, stop=True)
                            last.then_inc(lg_done, 1)

            def ranks(layer):
                e = EXPERTS[layer]
                pe.wait_ge(hot_ready, layer + 1)
                per = min(ALL_TILES, CHUNK // e // 8 * 8)
                for h in range(ALL_TILES // per):
                    cols = slice(h * per * e, (h + 1) * per * e)
                    nc.tensor.matmul((psX, psH)[h][:, 0:per * e], before_h[:, :], both_h[layer][:, cols],
                                     start=True, stop=True)
                    last = nc.tensor.matmul((psG, psD)[h][:, 0:per * e], ones_h[:, :], both_h[layer][:, cols],
                                            start=True, stop=True)
                last.then_inc(ranked, 1)

            def block_step(layer, b, k, passes=0, first=False, stages=(0, 1, 2, 3), held=None, n=0):
                c = b + layer * BLOCKS
                if 1 in stages and not (first and k < 1):
                    e_up = pe.value_load(table[0:1, bass.ds(b - 1, 1)], min_val=0, max_val=EXPERTS[layer] - 1)
                    if held is not None:
                        held[n] = e_up
                if held is not None and n - 2 in held:
                    e_down = held.pop(n - 2)
                elif 3 in stages and not (first and k < 3):
                    e_down = pe.value_load(table[0:1, bass.ds(b - 3, 1)], min_val=0, max_val=EXPERTS[layer] - 1)
                if 0 in stages:
                    if k % LOAD == 0:
                        slot = k // LOAD
                        pe.wait_ge(xb_loaded[slot], (passes + earlier_uses(layer, slot) + 1) * 16)
                    if not (first and k == 0 and layer == 0):
                        pe.wait_ge(xbT_ready, c)
                    nc.tensor.transpose(psX[:, 0:P], xb[:, k, :], ident).then_inc(xbT_filled, 1)
                if 1 in stages and not (first and k < 1):
                    j = (k - 1) % 2
                    pe.wait_ge(xbT_ready, c)
                    if layer == 0:
                        if not (first and k == 1):
                            pe.wait_ge(up_b_ready, c - 1)
                        nc.tensor.matmul(psG[:, :], xbT[:, j, :], wgu0_sb[:, bass.ds(e_up, 1), :].squeeze(1),
                                         start=True, stop=True).then_inc(gu_done, 1)
                    else:
                        if not (first and k == 1):
                            pe.wait_ge(act_ready, b - 1)
                        nc.tensor.matmul(psG[:, 0:F], xbT[:, j, :], w1_sb[:, bass.ds(e_up, 1), :].squeeze(1),
                                         start=True, stop=False)
                        nc.tensor.matmul(psG[:, 0:F], ones_h[0:3, :], b12_parts[:, bass.ds(e_up, 1), 0:F].squeeze(1),
                                         start=False, stop=True).then_inc(gu_done, 1)
                if 2 in stages and not (first and k < 2):
                    j = (k - 2) % 2
                    if layer == 0:
                        pe.wait_ge(hid_b_ready, c - 1)
                    else:
                        pe.wait_ge(act_ready, b - 1)
                    if not (first and k == 2 and layer == 0):
                        pe.wait_ge(hTb_ready, c - 2)
                    for f in range(HALVES):
                        last = nc.tensor.transpose(psH[:, f * P:(f + 1) * P],
                                                   (hid_b, act_b)[layer][:, j, f * P:(f + 1) * P], ident)
                    last.then_inc(hTb_filled, 1)
                if 3 in stages and not (first and k < 3):
                    j = (k - 3) % 2
                    pe.wait_ge(hTb_ready, c - 2)
                    if not (first and k == 3 and layer == 0):
                        pe.wait_ge(yb_ready, c - 3)
                    w_down = (wd0_sb, w2_sb)[layer]
                    for f in range(HALVES):
                        last = nc.tensor.matmul(psD[:, 0:D], hT_b[:, j, f * P:(f + 1) * P],
                                                w_down[:, bass.ds(e_down, 1), f, :].squeeze(1),
                                                start=(f == 0), stop=(layer == 0 and f == HALVES - 1))
                    if layer == 1:
                        last = nc.tensor.matmul(psD[:, 0:D], ones_h[0:3, :],
                                                b12_parts[:, bass.ds(e_down, 1), F:F + D].squeeze(1),
                                                start=False, stop=True)
                    last.then_inc(dn_done, 1)

            def drain(layer):
                for k, stages in ((0, (1, 2, 3)), (1, (2, 3)), (2, (3,))):
                    block_step(layer, BLOCKS + k, k, stages=stages)

            def beats(layer, counts, b0, first=False):
                step, held = STEP_BLOCKS[layer], {}

                def beat(n):
                    done = sum(counts[:n])
                    for k in range(done, done + counts[n]):
                        b, passes, at = b0(k, step)
                        block_step(layer, b, at, passes, first=first and k < step, held=held, n=k)
                return beat

            def pre(c, beat=lambda n: None):
                beat(3)
                pe.wait_ge(x_fixed_loaded, c * 16 + 16)
                transposes(psT, lambda t: x_fixed[:, t, :]).then_inc(xT_filled, 1)
                pe.wait_ge(xT_copied, c + 1)
                for t in range(TILES):
                    if t % 2 == 0:
                        beat(4 + t // 2)
                    if t >= 2:
                        pe.wait_ge(qkv_copied, c * TILES + t - 1)
                    elif not isinstance(c, int) or c >= 1:
                        pe.wait_ge((silu_ready, hid_ready)[t], c * HALVES)
                    if t == 1 and (not isinstance(c, int) or c >= 2):
                        pe.wait_ge(y_added, c - 1)
                    nc.tensor.matmul(psQ[t % 2][:, 0:QKV], xnT[0][:, t * P:(t + 1) * P], wqkv[:, :],
                                     start=True, stop=False)
                    nc.tensor.matmul(psQ[t % 2][:, 0:QKV], ones_h[0:PART_ROWS, :], bias_parts[:, 0, :],
                                     start=False, stop=True).then_inc(qkv_done, 1)
                for f in range(HALVES):
                    beat(6 + f)
                    if f == 0:
                        pe.wait_ge(qkv_copied, c * TILES + TILES)
                    else:
                        pe.wait_ge(silu_ready, c * HALVES + f)
                    nc.tensor.matmul(psQ0[:, :], wgu0_sb[:, E0, f * P:(f + 1) * P], xnT[0][:, :],
                                     start=True, stop=True).then_inc(gate_done, 1)
                    if f:
                        beat(8)
                        pe.wait_ge(hid_ready, c * HALVES + f)
                    nc.tensor.matmul(psQ1[:, :], wgu0_sb[:, E0, F + f * P:F + (f + 1) * P], xnT[0][:, :],
                                     start=True, stop=True).then_inc(up_done, 1)

            def down(c):
                pe.wait_ge(hid_ready, c * HALVES + HALVES)
                if not isinstance(c, int) or c >= 1:
                    pe.wait_ge(yT_ready, c)
                for f in range(HALVES):
                    last = nc.tensor.matmul(psY[:, :], wd0_sb[:, E0, f, :], hid[:, f, :],
                                            start=(f == 0), stop=False)
                last.then_inc(down_done, 1)

            def post(c, beat=lambda n: None):
                beat(0)
                pe.wait_ge(att_done, c + 1)
                transposes(psT, lambda t: att[:, t, :]).then_inc(attT_filled, 1)
                beat(1)
                pe.wait_ge(attT_copied, c + 1)
                nc.tensor.matmul(psY[:, :], sm[:, S_WOUT:S_WOUT + D], attT[:, :],
                                 start=False, stop=True).then_inc(y_done, 1)
                beat(2)
                pe.wait_ge(yT_ready, c + 1)
                pe.wait_ge(hid_ready, min(c + 2, CHUNKS) * HALVES if isinstance(c, int) else c * HALVES + 2 * HALVES)
                transposes(psQ1, lambda t: yT[:, t * P:(t + 1) * P]).then_inc(yT_filled, 1)

            def att_chunk(c, first=False, last=False, beat=lambda n: None):
                if not first:
                    post(c - 1, beat)
                down(c)
                if not last:
                    pre(c + 1, beat)
                beat(9)

            def chain(pair, beat=lambda n: None):
                beat(0)
                for u in range(2):
                    if not isinstance(pair, int) or pair > 0:
                        pe.wait_ge(res_read[u], pair * 2)
                    pe.wait_ge(z_ready[u], pair * 3 + 1)
                    transposes(chT[u], lambda t: z_tok[u][:, t, :]).then_inc(zT_filled[u], 1)
                beat(1)
                for u in range(2):
                    pe.wait_ge(zT_copied[u], pair * 3 + 1)
                    for t in range(TILES):
                        s, at = t // (SEQ // P), (t % (SEQ // P)) * P
                        for k in range(TAPS):
                            nc.tensor.matmul(chM[u][:, t * P:(t + 1) * P], convT[u][:, s, at + k:at + k + P],
                                             sm[:, S_CONV + k * D:S_CONV + (k + 1) * D],
                                             start=(k == 0), stop=False)
                        last = nc.tensor.matmul(chM[u][:, t * P:(t + 1) * P], ones_h[0:PART_ROWS, :],
                                                bias_parts[:, 1, 0:D], start=False, stop=True)
                    last.then_inc(conv_done[u], 1)
                beat(2)
                for u in range(2):
                    pe.wait_ge(z_ready[u], pair * 3 + 2)
                    transposes(chT[u], lambda t: z_tok[u][:, t, :]).then_inc(zT_filled[u], 1)
                beat(3)
                for u in range(2):
                    pe.wait_ge(zT_copied[u], pair * 3 + 2)
                    nc.tensor.matmul(chM[u][:, :], sm[:, S_WQ1:S_WQ1 + D], hT[u][:, :],
                                     start=True, stop=True).then_inc(q_done[u], 1)
                    nc.tensor.matmul(chT[u][:, :], sm[:, S_WK1:S_WK1 + D], hT[u][:, :],
                                     start=True, stop=True).then_inc(k_done[u], 1)
                beat(4)
                for u in range(2):
                    pe.wait_ge(q_ready[u], pair + 1)
                    nc.tensor.matmul(chM[u][:, :], sm[:, S_WV1:S_WV1 + D], hT[u][:, :],
                                     start=True, stop=True).then_inc(v_done[u], 1)
                beat(5)
                for u in range(2):
                    pe.wait_ge(k_read[u], pair + 1)
                    pe.wait_ge(pkv_ready[u], pair + 1)
                    transposes(chT[u], lambda t: pooled[u][:, t * P:(t + 1) * P]).then_inc(pkvT_filled[u], 1)
                beat(6)
                for u in range(2):
                    pe.wait_ge(res_read[u], pair * 2 + 1)
                    pe.wait_ge(z_ready[u], pair * 3 + 3)
                    transposes(chT[u], lambda t: z_tok[u][:, t, :]).then_inc(zT_filled[u], 1)
                beat(7)
                for b in range(BOOM):
                    for u in range(2):
                        if b == 0:
                            pe.wait_ge(zT_copied[u], pair * 3 + 3)
                        if b >= 2:
                            pe.wait_ge(boom_ready[u], pair * BOOM + b - 1)
                        nc.tensor.matmul((chM, chT)[b % 2][u][:, :], sm[:, S_WB + b * D:S_WB + (b + 1) * D],
                                         hT[u][:, :], start=True, stop=True).then_inc(boom_done[u], 1)
                beat(8)
                for u in range(2):
                    pe.wait_ge(boom_ready[u], pair * BOOM + BOOM)
                    for b in range(BOOM):
                        last = nc.tensor.matmul(chM[u][:, :], sm[:, S_WU + b * D:S_WU + (b + 1) * D],
                                                gb[u][:, b, :], start=(b == 0), stop=(b == BOOM - 1))
                    last.then_inc(mlp_done[u], 1)
                beat(9)
                for u in range(2):
                    pe.wait_ge(mlpT_ready[u], pair + 1)
                    transposes(chT[u], lambda t: mlpT[u][:, t * P:(t + 1) * P]).then_inc(mlpT_filled[u], 1)

            pe.sem_inc(nT_filled, GROUP // TILES)
            pe.wait_ge(w_small, 48)
            nc.tensor.matmul(psX[:, 0:2 * D], nr[0:LAT, N_WDOWN:N_WDOWN + D], nr[0:LAT, N_WUP:N_WUP + 2 * D],
                             start=True, stop=True).then_inc(prep_pe, 1)
            nc.tensor.matmul(psG[0:1, 0:2 * D], nr[0:LAT, N_BDOWN:N_BDOWN + 1], nr[0:LAT, N_WUP:N_WUP + 2 * D],
                             start=True, stop=True).then_inc(prep_pe, 1)

            logits(0)
            pe.wait_ge(prep_act, 1)
            pe.wait_ge(prep_dve, 1)
            ranks(0)
            pe.wait_ge(w_layer0, 32)
            pre(0)
            pe.wait_ge(routed, 1)
            for c in range(BLOCK_CHUNKS[0]):
                att_chunk(c, first=(c == 0))
            att_chunk(BLOCK_CHUNKS[0], beat=beats(0, ATT_BEATS, block_from(0, CHUNK_BLOCKS), first=True))
            with pe.Fori(BLOCK_CHUNKS[1] // 2, BLOCK_CHUNKS[-1] // 2 + 1) as pair:
                for u in range(2):
                    att_chunk(pair * 2 + u, beat=beats(0, ATT_BEATS, block_from(
                        pair, 2 * CHUNK_BLOCKS, (u - BLOCK_CHUNKS[0]) * CHUNK_BLOCKS)))
            drain(0)
            for c in range(BLOCK_CHUNKS[-1] + 1, CHUNKS):
                att_chunk(c, last=(c == CHUNKS - 1))
            post(CHUNKS - 1)

            logits(1)
            ranks(1)
            pe.wait_ge(routed, 2)
            chain(0)
            with pe.Fori(1, BLOCK_PAIRS[0]) as pair:
                chain(pair)
            pe.wait_ge(w_layer1, 32)
            pe.wait_ge(b12_loaded, 48)
            pair = BLOCK_PAIRS[0]
            chain(pair, beats(1, CHAIN_BEATS, block_from(0, PAIR_BLOCKS), first=True))
            with pe.Fori(pair + 1, BLOCK_PAIRS[-1] + 1) as pair:
                chain(pair, beats(1, CHAIN_BEATS, block_from(pair, PAIR_BLOCKS, -BLOCK_PAIRS[0] * PAIR_BLOCKS)))
            drain(1)
            with pe.Fori(BLOCK_PAIRS[-1] + 1, PAIRS) as pair:
                chain(pair)

        @block.scalar
        def _(act):
            def col(n):
                return cv[:, n:n + 1]

            act.sem_inc(lg_copied, 1)
            act.wait_ge(prep_pe, 1)
            nc.scalar.copy(wqkv[:, D:3 * D], psX[:, 0:2 * D])
            nc.scalar.copy(wqkv[:, 0:D], sm[:, S_WQ:S_WQ + D]).then_inc(prep_act, 1)

            def logits(layer):
                e = EXPERTS[layer]
                with act.Fori(0, GROUPS) as g:
                    chunk0 = g * (GROUP // TILES) + layer * CHUNKS
                    for k in range(GROUP // TILES):
                        act.wait_ge(nT_filled, chunk0 + k + 5)
                        if k >= 2:
                            act.wait_ge(lg_done, chunk0 + k - 1)
                        nc.scalar.copy(xnT[k % 2][:, :], psQ[k % 2][:, :]).then_inc(nT_copied, 1)
                    act.wait_ge(lg_done, chunk0 + GROUP // TILES)
                    nc.scalar.copy(lg[layer][:, bass.ds(g * GROUP, GROUP), :],
                                   psY[:, 0:GROUP * e].rearrange("p (t e) -> p t e", e=e)).then_inc(lg_copied, 1)

            def route_exps(layer):
                act.wait_ge(shifted, layer + 1)
                nc.scalar.activation(ex[layer][:, :, :], ex[layer][:, :, :], ACT.Exp)
                nc.scalar.activation(few[:, F_E2, :], few[:, F_E2, :], ACT.Exp).then_inc(exped, 1)

            def block_step(layer, b, k, first=False, stages=(0, 1, 2, 3), sent=None):
                c = b + layer * BLOCKS
                if 0 in stages:
                    act.wait_ge(xbT_filled, c + 1)
                    nc.scalar.copy(xbT[:, k % 2, :], psX[:, 0:P]).then_inc(xbT_ready, 1)
                if 1 in stages and not (first and k < 1):
                    act.wait_ge(gu_done, c)
                    if layer == 0:
                        nc.scalar.activation(act_b[:, (k - 1) % 2, :], psG[:, 0:F], ACT.Silu)
                        nc.scalar.copy(hid_b[:, (k - 1) % 2, :], psG[:, F:2 * F]).then_inc(up_b_ready, 1)
                    else:
                        nc.scalar.activation(act_b[:, (k - 1) % 2, :], psG[:, 0:F], ACT.Gelu).then_inc(act_ready, 1)
                if 2 in stages and not (first and k < 2):
                    act.wait_ge(hTb_filled, c - 1)
                    nc.scalar.copy(hT_b[:, (k - 2) % 2, :], psH[:, 0:F]).then_inc(hTb_ready, 1)
                if 3 in stages and not (first and k < 3):
                    at = (k - 3) % STEP_BLOCKS[layer]
                    slot = at // LOAD
                    if at % LOAD == 0:
                        n = (sent if k >= 3 else sent - 1) + earlier_uses(layer, slot)
                        if not (isinstance(n, int) and n == 0):
                            act.wait_ge(ys_sent[slot], n * 16)
                    act.wait_ge(dn_done, c - 2)
                    nc.scalar.copy(yb[:, at, :], psD[:, 0:D]).then_inc(yb_ready, 1)
                    if at % LOAD == LOAD - 1:
                        act.wait_ge(yb_ready, c - 2)
                        rows = ys[bass.ds((b - 3 - (LOAD - 1)) * P, LOAD * P), :].rearrange("(b p) d -> p b d", p=P)
                        act.dma_start(rows, yb[:, slot * LOAD:(slot + 1) * LOAD, :]).then_inc(ys_sent[slot], 16)

            def drain(layer):
                for k, stages in ((0, (1, 2, 3)), (1, (2, 3)), (2, (3,))):
                    block_step(layer, BLOCKS + k, k, stages=stages, sent=PASSES[layer])

            def beats(layer, counts, b0, first=False):
                step = STEP_BLOCKS[layer]

                def beat(n):
                    done = sum(counts[:n])
                    for k in range(done, done + counts[n]):
                        b, passes, at = b0(k, step)
                        block_step(layer, b, at, first=first and k < step, sent=passes)
                return beat

            def load_fixed(c):
                act.dma_start(x_fixed, xn_all[:, bass.ds(c * TILES, TILES), :]).then_inc(x_fixed_loaded, 16)

            def pre(c, u, beat=lambda n: None, more=True, between=None):
                beat(3)
                act.wait_ge(xT_filled, c + 1)
                nc.scalar.copy(xnT[0][:, :], psT[:, :]).then_inc(xT_copied, 1)
                if more:
                    load_fixed(c + 1)
                for t in range(TILES):
                    if t == 0 and between:
                        between()
                    if t % 2 == 0:
                        beat(4 + t // 2)
                    act.wait_ge(qkv_done, c * TILES + t + 1)
                    nc.scalar.copy(qkv[u][:, t, :], psQ[t % 2][:, 0:QKV]).then_inc(qkv_copied, 1)

            def shared_silu(c, f):
                act.wait_ge(gate_done, c * HALVES + f + 1)
                nc.scalar.activation(hid[:, f, :], psQ0[:, :], ACT.Silu).then_inc(silu_ready, 1)

            def post(c, beat=lambda n: None):
                beat(0)
                act.wait_ge(attT_filled, c + 1)
                nc.scalar.copy(attT[:, :], psT[:, :]).then_inc(attT_copied, 1)
                beat(1)
                act.wait_ge(y_done, c + 1)
                nc.scalar.activation(yT[:, :], psY[:, :], ACT.Identity, bias=col(C_BOUT)).then_inc(yT_ready, 1)
                beat(2)

            def exps(c, h):
                act.wait_ge(score_ready, c * 2 + h + 1)
                s = score[:, 2 * h:2 * h + 2, :, :]
                nc.scalar.activation(s, s, ACT.Exp, scale=SCALE).then_inc(prob_ready, 1)

            def att_chunk(c, u, first=False, last=False, more=True, beat=lambda n: None):
                if not first:
                    post(c - 1, beat)
                if not last:
                    pre(c + 1, 1 - u, beat, more, between=lambda: exps(c, 0))
                    act.wait_ge(down_done, c + 1)
                    beat(6)
                    shared_silu(c + 1, 0)
                else:
                    exps(c, 0)
                exps(c, 1)
                beat(7)
                if not last:
                    shared_silu(c + 1, 1)
                beat(8)
                beat(9)

            def chain(pair, beat=lambda n: None):
                beat(0)
                for u in range(2):
                    act.wait_ge(zT_filled[u], pair * 3 + 1)
                    for s in range(SEQS):
                        last = nc.scalar.activation(convT[u][:, s, TAPS - 1:], chT[u][:, s * SEQ:(s + 1) * SEQ],
                                                    ACT.Identity, scale=col(C_GCONV), bias=col(C_BCONV))
                    last.then_inc(zT_copied[u], 1)
                beat(1)
                beat(2)
                for u in range(2):
                    act.wait_ge(zT_filled[u], pair * 3 + 2)
                    nc.scalar.activation(hT[u][:, :], chT[u][:, :], ACT.Identity, scale=col(C_GATTN),
                                         bias=col(C_BATTN)).then_inc(zT_copied[u], 1)
                beat(3)
                for u in range(2):
                    act.wait_ge(q_done[u], pair + 1)
                    nc.scalar.activation(qT[u][:, :], chM[u][:, :], ACT.Identity, bias=col(C_BQ))\
                        .then_inc(q_ready[u], 1)
                for n in (4, 5, 6):
                    beat(n)
                for u in range(2):
                    act.wait_ge(zT_filled[u], pair * 3 + 3)
                    nc.scalar.activation(hT[u][:, :], chT[u][:, :], ACT.Identity, scale=col(C_GBOOM),
                                         bias=col(C_BBOOM)).then_inc(zT_copied[u], 1)
                beat(7)
                for b in range(BOOM):
                    for u in range(2):
                        act.wait_ge(boom_done[u], pair * BOOM + b + 1)
                        nc.scalar.activation(gb[u][:, b, :], (chM, chT)[b % 2][u][:, :], ACT.Gelu,
                                             bias=col(C_BB + b)).then_inc(boom_ready[u], 1)
                beat(8)
                for u in range(2):
                    act.wait_ge(mlp_done[u], pair + 1)
                    nc.scalar.activation(mlpT[u][:, :], chM[u][:, :], ACT.Identity, bias=col(C_BU))\
                        .then_inc(mlpT_ready[u], 1)
                beat(9)

            logits(0)
            route_exps(0)
            for h in range(2):
                act.wait_ge(xn_moved[h], (GROUPS + 1) * 16)
            load_fixed(0)
            pre(0, 0, between=lambda: act.wait_ge(routed, 1))
            for f in range(HALVES):
                shared_silu(0, f)
            for c in range(BLOCK_CHUNKS[0]):
                att_chunk(c, c % 2, first=(c == 0))
            att_chunk(BLOCK_CHUNKS[0], 1, beat=beats(0, ATT_BEATS, block_from(0, CHUNK_BLOCKS), first=True))
            with act.Fori(BLOCK_CHUNKS[1] // 2, BLOCK_CHUNKS[-1] // 2 + 1) as pair:
                for u in range(2):
                    att_chunk(pair * 2 + u, u, beat=beats(0, ATT_BEATS, block_from(
                        pair, 2 * CHUNK_BLOCKS, (u - BLOCK_CHUNKS[0]) * CHUNK_BLOCKS)))
            drain(0)
            for c in range(BLOCK_CHUNKS[-1] + 1, CHUNKS):
                att_chunk(c, c % 2, last=(c == CHUNKS - 1), more=(c < CHUNKS - 2))
            post(CHUNKS - 1)
            logits(1)
            route_exps(1)
            act.wait_ge(routed, 2)
            chain(0)
            with act.Fori(1, BLOCK_PAIRS[0]) as pair:
                chain(pair)
            pair = BLOCK_PAIRS[0]
            chain(pair, beats(1, CHAIN_BEATS, block_from(0, PAIR_BLOCKS), first=True))
            with act.Fori(pair + 1, BLOCK_PAIRS[-1] + 1) as pair:
                chain(pair, beats(1, CHAIN_BEATS, block_from(pair, PAIR_BLOCKS, -BLOCK_PAIRS[0] * PAIR_BLOCKS)))
            drain(1)
            with act.Fori(BLOCK_PAIRS[-1] + 1, PAIRS) as pair:
                chain(pair)

        @block.vector
        def _(dve):
            v = nc.vector
            L = Links(dve, dve_step)
            alone = [0]

            def wait_alone(*waits):
                for semaphore, value in waits:
                    dve.wait_ge(semaphore, value)
                v.memset(idle[:, alone[0]:alone[0] + 1], 0.0)
                alone[0] += 1

            def link_alone(ins):
                L.mark(ins)
                wait_alone((dve_step, L.value()))

            dve.wait_ge(w_small, 48)
            v.tensor_copy(before_h[:, :], sm[:, S_BEFORE:S_BEFORE + P])
            v.reciprocal(inv_count[:, :], sm[:, S_COUNT:S_COUNT + SEQ])
            L.link(v.memset(bias_row[0:1, :, :], 0.0))
            dve.wait_ge(prep_pe, 2)
            dve.wait_ge(prep_pool, 1)
            b12 = nr[0:E1, N_B12:N_END]
            v.tensor_copy(bias_row[0:1, 0, 0:D], nr[0:1, N_BQ:N_BQ + D])
            v.tensor_copy(bias_row[0:1, 1, 0:D], nr[0:1, N_CONVB:N_CONVB + D])
            v.tensor_copy(b12_split[0:E1, 0, :], b12)
            L.link(v.tensor_tensor(bias_row[0:1, 0, D:3 * D], psG[0:1, 0:2 * D], nr[0:1, N_BUP:N_BUP + 2 * D], ALU.add))
            v.tensor_tensor(b12_rest[0:E1, :], b12, b12_split[0:E1, 0, :], ALU.subtract)
            L.link(v.tensor_copy(bias_parts[0:1, :, :], bias_row[0:1, :, :]))
            v.tensor_copy(b12_split[0:E1, 1, :], b12_rest[0:E1, :])
            L.link(v.tensor_tensor(bias_row[0:1, :, :], bias_row[0:1, :, :], bias_parts[0:1, :, :], ALU.subtract))
            v.tensor_tensor(b12_rest[0:E1, :], b12_rest[0:E1, :], b12_split[0:E1, 1, :], ALU.subtract)
            L.link(v.tensor_copy(mid_row[0:1, :, :], bias_row[0:1, :, :]))
            v.tensor_copy(b12_split[0:E1, 2, :], b12_rest[0:E1, :]).then_inc(split_ready, 1)
            v.tensor_copy(bias_parts[32:33, :, :], mid_row[0:1, :, :])
            L.link(v.tensor_tensor(bias_row[0:1, :, :], bias_row[0:1, :, :], mid_row[0:1, :, :], ALU.subtract))
            v.tensor_copy(bias_parts[64:65, :, :], bias_row[0:1, :, :]).then_inc(prep_dve, 1)

            def inverse_root(y, var, n):
                v_eps, step = var_eps[:, 0:n], newton[:, 0:n]
                L.link(v.tensor_scalar(v_eps, var, EPS, None, ALU.add))
                L.link(v.tensor_scalar(y.bitcast(I32), v_eps.bitcast(I32), -0.5, ROOT_GUESS, ALU.mult, ALU.add))
                for _ in range(ROOT_STEPS):
                    L.link(v.tensor_tensor(step, y, y, ALU.mult))
                    L.link(v.scalar_tensor_tensor(step, step, -0.5, v_eps, ALU.mult, ALU.mult))
                    L.link(v.scalar_tensor_tensor(y, step, 1.5, y, ALU.add, ALU.mult))

            def norm_all(layer):
                with dve.Fori(0, GROUPS) as g:
                    L.enter(g, 2 + ROOT_LINKS)
                    if layer == 0:
                        wait_alone((x_loaded, g * 32 + 32))
                    for t in range(GROUP):
                        last = v.bn_stats(stats[:, t, :], tile_of(x_all, g * GROUP + t))
                    link_alone(last)
                    for t in range(GROUP):
                        last = v.bn_aggr(mv_group[:, t, :], stats[:, t, :])
                    L.link(last)
                    inverse_root(rstd_group[:, :], mv_group[:, :, 1], GROUP)
                    for h in range(2):
                        dve.wait_ge(xn_moved[h], (g + layer * GROUPS + 1) * 16)
                        dve.wait_ge(nT_filled, (g + layer * GROUPS) * (GROUP // TILES) + 2 * h + 2)
                        for t in range(8):
                            n = 8 * h + t
                            last = v.tensor_scalar(fresh[h][:, t, :], tile_of(x_all, g * GROUP + n),
                                                   mv_group[:, n, 0:1], rstd_group[:, n:n + 1],
                                                   ALU.subtract, ALU.mult)
                        last.then_inc(xn_done, 1)
                L.leave(GROUPS)

            def route(layer):
                e = EXPERTS[layer]
                logit, exp_e, ra, rb, hots = lg[layer], ex[layer], rank_a[layer], rank_b[layer], hot[layer]

                def wide(k):
                    return few[:, k, :].unsqueeze(2).to_broadcast([P, ALL_TILES, e])

                iota = sm[:, S_IOTA:S_IOTA + e].unsqueeze(1).to_broadcast([P, ALL_TILES, e])
                dve.wait_ge(lg_copied, (layer + 1) * GROUPS + 1)
                L.link(v.reduce_max(few[:, F_M1, :], logit, axis=AX.X))
                v.tensor_tensor(exp_e, logit, wide(F_M1), ALU.subtract)
                L.link(v.tensor_tensor(ra, logit, wide(F_M1), ALU.is_equal))
                L.link(v.scalar_tensor_tensor(ra, ra, -32.0, iota, ALU.mult, ALU.add))
                L.link(v.tensor_reduce(few[:, F_I1, :], ra, AX.X, ALU.min))
                L.link(v.tensor_tensor(hots[0], ra, wide(F_I1), ALU.is_equal))
                L.link(v.scalar_tensor_tensor(ra, hots[0], -BIG, logit, ALU.mult, ALU.add))
                L.link(v.reduce_max(few[:, F_M2, :], ra, axis=AX.X))
                v.tensor_tensor(few[:, F_E2, :], few[:, F_M2, :], few[:, F_M1, :], ALU.subtract).then_inc(shifted, 1)
                L.link(v.tensor_tensor(rb, ra, wide(F_M2), ALU.is_equal))
                L.link(v.scalar_tensor_tensor(rb, rb, -32.0, iota, ALU.mult, ALU.add))
                L.link(v.tensor_reduce(few[:, F_I2, :], rb, AX.X, ALU.min))
                L.link(v.tensor_tensor(hots[1], rb, wide(F_I2), ALU.is_equal))
                dve.wait_ge(b12_loaded, 48)
                v.tensor_tensor(both_h[layer].rearrange("p (t e) -> p t e", e=e), hots[0], hots[1], ALU.add)\
                    .then_inc(hot_ready, 1)

                dve.wait_ge(ranked, layer + 1)
                per = min(ALL_TILES, CHUNK // e // 8 * 8)
                halves = [(h, slice(h * per, (h + 1) * per)) for h in range(ALL_TILES // per)]
                for h, tiles in halves:
                    last = v.tensor_copy(total[layer][:, :, tiles],
                                         (psG, psD)[h][:, 0:per * e].rearrange("p (t e) -> p e t", e=e))
                L.link(last)
                for j in range(e):
                    last = v.tensor_tensor_scan(cum[layer][:, j, :], ones_f[:, 0:ALL_TILES], total[layer][:, j, :],
                                                0.0, ALU.mult, ALU.add)
                L.link(last)
                blocks_e, ends = few[:, F_NB, 0:e], few[:, F_I1, 0:e]
                L.link(v.tensor_scalar(int_e[:, 0, 0:e], cum[layer][:, :, ALL_TILES - 1], float(P - 1), None, ALU.add))
                L.link(v.tensor_scalar(int_e[:, 1, 0:e], int_e[:, 0, 0:e], P.bit_length() - 1, None,
                                       ALU.arith_shift_right))
                L.link(v.tensor_copy(blocks_e, int_e[:, 1, 0:e]))
                L.link(v.tensor_tensor_scan(ends, ones_f[:, 0:e], blocks_e, 0.0, ALU.mult, ALU.add))
                v.tensor_tensor(few[:, F_M1, 0:e], ends, blocks_e, ALU.subtract)
                L.link(v.tensor_tensor(cum[layer], cum[layer], total[layer], ALU.subtract))
                L.link(v.scalar_tensor_tensor(cum[layer], few[:, F_M1, 0:e].unsqueeze(2).to_broadcast([P, e, ALL_TILES]),
                                              float(P), cum[layer], ALU.mult, ALU.add))
                if layer == 0:
                    own, over, by = pad_f[:, 0, :], pad_f[:, 1, :], pad_f[:, 2, :]
                    L.link(v.scalar_tensor_tensor(own, cum[layer][:, :, ALL_TILES - 1], cv[:, C_ROW:C_ROW + 1],
                                                  total[layer][:, :, ALL_TILES - 1], ALU.add, ALU.add))
                    v.tensor_tensor(by, sm[:, S_PAST:S_PAST + E0], own, ALU.subtract)
                    L.link(v.scalar_tensor_tensor(over, ends, float(P), own, ALU.mult, ALU.is_le))
                    L.link(v.tensor_tensor(by, by, over, ALU.mult))
                    v.tensor_tensor(pad_u[:, :], own, by, ALU.add).then_inc(pads_known, 1)
                for h, tiles in halves:
                    last = v.tensor_tensor(logit[:, tiles, :],
                                           (psX, psH)[h][:, 0:per * e].rearrange("p (t e) -> p t e", e=e),
                                           cum[layer][:, :, tiles].rearrange("p e t -> p t e"), ALU.add)
                L.link(last)
                v.tensor_tensor(ra, hots[0], logit, ALU.mult)
                L.link(v.tensor_tensor(rb, hots[1], logit, ALU.mult))
                v.reduce_sum(few[:, F_P1, :], ra, axis=AX.X)
                L.link(v.reduce_sum(few[:, F_P2, :], rb, axis=AX.X))
                for s in range(2):
                    last = v.tensor_copy(pos_u[:, s, :], few[:, F_P1 + s, :])
                last.then_inc(placed, 1)

                dve.wait_ge(exped, layer + 1)
                L.link(v.reduce_sum(few[:, F_Z, :], exp_e, axis=AX.X))
                L.link(v.reciprocal(few[:, F_P1, :], few[:, F_Z, :]))
                L.link(v.tensor_tensor(few[:, F_P2, :], few[:, F_E2, :], few[:, F_P1, :], ALU.mult))
                L.link(v.tensor_tensor(few[:, F_SUM, :], few[:, F_P1, :], few[:, F_P2, :], ALU.add))
                floor, floor_op = ((1e-20, ALU.add), (1e-10, ALU.max))[layer]
                L.link(v.tensor_scalar(few[:, F_SUM, :], few[:, F_SUM, :], floor, None, floor_op))
                L.link(v.reciprocal(few[:, F_Z, :], few[:, F_SUM, :]))
                for s in range(2):
                    v.tensor_tensor(w_pair[:, s, :], few[:, F_P1 + s, :], few[:, F_Z, :], ALU.mult)

                L.link(v.tensor_tensor(past[layer][0:1, :, :],
                                       sm[0:1, S_IOTA:S_IOTA + BLOCKS].unsqueeze(2).to_broadcast([1, BLOCKS, e]),
                                       ends[0:1, :].unsqueeze(1).to_broadcast([1, BLOCKS, e]), ALU.is_ge))
                L.link(v.reduce_sum(block_at[0:1, :], past[layer][0:1, :, :], axis=AX.X))
                v.tensor_scalar(table[:, :], block_at[0:1, :], float(e - 1), None, ALU.min).then_inc(routed, 1)

            def score_pair(c, u, h, between=None):
                for t in (2 * h, 2 * h + 1):
                    q = qkv[u][:, t, 0:D].rearrange("p (h d) -> p h d", d=DH).unsqueeze(2).to_broadcast([P, H, H, DH])
                    k = qkv[u][:, t, D:2 * D].rearrange("p (g d) -> p g d", d=DH).unsqueeze(1)\
                        .to_broadcast([P, H, H, DH])
                    L.mark(v.tensor_tensor(prod[t % 2], q, k, ALU.mult))
                if between:
                    between()
                for t in (2 * h, 2 * h + 1):
                    dve.wait_ge(dve_step, L.value() - 1 + t % 2)
                    last = v.reduce_sum(score[:, t, :, :], prod[t % 2], axis=AX.X)
                L.link(last)
                s = score[:, 2 * h:2 * h + 2, :, :]
                L.link(v.reduce_max(head_max, s, axis=AX.X))
                v.tensor_tensor(s, s, head_max.unsqueeze(3).to_broadcast([P, 2, H, H]), ALU.subtract)\
                    .then_inc(score_ready, 1)

            def mix_pair(c, u, h):
                dve.wait_ge(prob_ready, c * 2 + h + 1)
                v.reduce_sum(head_sum, score[:, 2 * h:2 * h + 2, :, :], axis=AX.X)
                prod_v = [a.rearrange("p h g d -> p (h g d)").rearrange("p (h d g) -> p h d g", d=DH, g=H)
                          for a in prod]
                for t in (2 * h, 2 * h + 1):
                    p = score[:, t, :, :].unsqueeze(2).to_broadcast([P, H, DH, H])
                    w = qkv[u][:, t, 2 * D:3 * D].rearrange("p (d g) -> p d g", g=H).unsqueeze(1)\
                        .to_broadcast([P, H, DH, H])
                    L.mark(v.tensor_tensor(prod_v[t % 2], p, w, ALU.mult))
                for t in (2 * h, 2 * h + 1):
                    dve.wait_ge(dve_step, L.value() - 1 + t % 2)
                    if t == 2 * h:
                        v.reciprocal(head_rec, head_sum)
                    last = v.reduce_sum(att[:, t, :].rearrange("p (h d) -> p h d", d=DH), prod_v[t % 2], axis=AX.X)
                L.link(last)
                out_t = att[:, 2 * h:2 * h + 2, :].rearrange("p t (h d) -> p t h d", d=DH)
                last = v.tensor_tensor(out_t, out_t, head_rec.unsqueeze(3).to_broadcast([P, 2, H, DH]), ALU.mult)
                if h == 1:
                    last.then_inc(att_done, 1)

            def add_y(c):
                dve.wait_ge(yT_filled, c + 1)
                x_now = x_all[:, bass.ds(c * TILES, TILES), :]
                v.tensor_tensor(x_now, x_now, psQ1[:, :].rearrange("p (t d) -> p t d", d=D), ALU.add)\
                    .then_inc(y_added, 1)

            def shared_hidden(c, f):
                dve.wait_ge(silu_ready, c * HALVES + f + 1)
                dve.wait_ge(up_done, c * HALVES + f + 1)
                v.tensor_tensor(hid[:, f, :], hid[:, f, :], psQ1[:, :], ALU.mult).then_inc(hid_ready, 1)

            def att_chunk(c, u, first=False, last=False, point=lambda n: None):
                dve.wait_ge(qkv_copied, c * TILES + TILES)
                score_pair(c, u, 0)
                point(0)
                score_pair(c, u, 1, between=None if first else lambda: add_y(c - 1))
                point(1)
                mix_pair(c, u, 0)
                point(2)
                if not last:
                    shared_hidden(c + 1, 0)
                mix_pair(c, u, 1)
                if not last:
                    shared_hidden(c + 1, 1)
                point(3)

            def add_experts(layer, c, target):
                uses = layer * (CHUNKS // ROWS_RING + (1 if c % ROWS_RING < CHUNKS % ROWS_RING else 0)) + c // ROWS_RING + 1
                dve.wait_ge(gathered[c % ROWS_RING], uses * 2 * TILES * 16)
                for s in range(2):
                    for j in range(TILES):
                        n = c * TILES + j
                        last = v.scalar_tensor_tensor(target[:, n, :], rings[:, (c % ROWS_RING * TILES + j) * 2 + s, :],
                                                      w_pair[:, s, n:n + 1], target[:, n, :], ALU.mult, ALU.add)
                    if s == 0:
                        L.link(last)
                last.then_inc(mixed, 1)
                dve.wait_ge(mixed, layer * CHUNKS + c + 1)

            def finish(c):
                add_experts(1, c, xn_all)
                now = slice(c * TILES, (c + 1) * TILES)
                L.link(v.tensor_scalar(xn_all[:, now, :], xn_all[:, now, :], -100.0, 100.0, ALU.max, ALU.min))
                v.tensor_tensor(x_all[:, now, :], x_all[:, now, :], xn_all[:, now, :], ALU.add).then_inc(out_ready, 1)

            def chain(pair, point=lambda n: None):
                def chunk(a, u):
                    return a[:, bass.ds((pair * 2 + u) * TILES, TILES), :]

                def statistics(src):
                    for u in range(2):
                        for t in range(TILES):
                            last = v.bn_stats(ch_stats[u][:, t, :], src(u, t))
                    link_alone(last)
                    for u in range(2):
                        for t in range(TILES):
                            last = v.bn_aggr(ch_mv[:, u * TILES + t, :], ch_stats[u][:, t, :])
                    L.link(last)
                    inverse_root(ch_rstd[:, :], ch_mv[:, :, 1], 2 * TILES)

                def apply(src):
                    for u in range(2):
                        for t in range(TILES):
                            n = u * TILES + t
                            last = v.tensor_scalar(z_tok[u][:, t, :], src(u, t), ch_mv[:, n, 0:1],
                                                   ch_rstd[:, n:n + 1], ALU.subtract, ALU.mult)
                        last.then_inc(z_ready[u], 1)

                def running_mean():
                    for u in range(2):
                        if first:
                            dve.wait_ge(q_ready[u], pair + 1)
                        for s in range(SEQS):
                            seq = slice(s * SEQ, (s + 1) * SEQ)
                            last = v.tensor_tensor_scan(scan[u][:, seq], ones_f[:, :], qT[u][:, seq], 0.0,
                                                        ALU.mult, ALU.add)
                    L.link(last)
                    for u in range(2):
                        last = v.tensor_tensor(pooled[u].rearrange("p (s n) -> p s n", n=SEQ),
                                               scan[u].rearrange("p (s n) -> p s n", n=SEQ),
                                               inv_count[:, :].unsqueeze(1).to_broadcast([P, SEQS, SEQ]), ALU.mult)
                    L.link(last)

                def xn_tile(u, t):
                    return tile_of(xn_all, (pair * 2 + u) * TILES + t)

                statistics(xn_tile)
                apply(xn_tile)
                point(0)
                for u in range(2):
                    dve.wait_ge(conv_done[u], pair + 1)
                    last = v.tensor_tensor(x2[u], chunk(xn_all, u), chM[u][:, :].rearrange("p (t d) -> p t d", d=D),
                                           ALU.add)
                link_alone(last)
                statistics(lambda u, t: x2[u][:, t, :])
                apply(lambda u, t: x2[u][:, t, :])
                point(1)
                first = True
                running_mean()
                first = False
                for u in range(2):
                    dve.wait_ge(k_done[u], pair + 1)
                    v.scalar_tensor_tensor(qT[u], chT[u][:, :], cv[:, C_BK:C_BK + 1], pooled[u],
                                           ALU.add, ALU.mult).then_inc(k_read[u], 1)
                for u in range(2):
                    dve.wait_ge(k_read[u], pair + 1)
                running_mean()
                for u in range(2):
                    dve.wait_ge(v_done[u], pair + 1)
                    v.scalar_tensor_tensor(pooled[u], chM[u][:, :], cv[:, C_BV:C_BV + 1], pooled[u],
                                           ALU.add, ALU.mult).then_inc(pkv_ready[u], 1)
                for u in range(2):
                    dve.wait_ge(pkvT_filled[u], pair + 1)
                    v.tensor_tensor(x2[u], x2[u], chT[u][:, :].rearrange("p (t d) -> p t d", d=D), ALU.add)\
                        .then_inc(res_read[u], 1)
                wait_alone((res_read[0], pair * 2 + 1), (res_read[1], pair * 2 + 1))
                statistics(lambda u, t: x2[u][:, t, :])
                apply(lambda u, t: x2[u][:, t, :])
                point(2)
                for u in range(2):
                    dve.wait_ge(mlpT_filled[u], pair + 1)
                    v.tensor_tensor(x2[u], x2[u], chT[u][:, :].rearrange("p (t d) -> p t d", d=D), ALU.add)\
                        .then_inc(res_read[u], 1)
                for u in range(2):
                    dve.wait_ge(res_read[u], pair * 2 + 2)
                    last = v.tensor_tensor(chunk(x_all, u), chunk(x_all, u), x2[u], ALU.add)
                L.link(last)

            norm_all(0)
            route(0)
            for f in range(HALVES):
                shared_hidden(0, f)
            for c in range(BLOCK_CHUNKS[0] + 1):
                att_chunk(c, c % 2, first=(c == 0))
            first_pair = BLOCK_CHUNKS[1] // 2
            with dve.Fori(0, BLOCK_CHUNKS[-1] // 2 + 1 - first_pair) as i:
                L.enter(i, LINKS_ATT)
                for u in range(2):
                    att_chunk(i * 2 + (2 * first_pair + u), u)
            L.leave(BLOCK_CHUNKS[-1] // 2 + 1 - first_pair)
            late = BLOCK_CHUNKS[-1] + 1
            for c in range(late, CHUNKS):
                def point(n):
                    if (c - late) * 4 + n >= 2:
                        add_experts(0, (c - late) * 4 + n - 2, x_all)
                att_chunk(c, c % 2, last=(c == CHUNKS - 1), point=point)
            add_y(CHUNKS - 1)
            dve.wait_ge(y_added, CHUNKS)
            for c in range(4 * (CHUNKS - late) - 2, CHUNKS):
                add_experts(0, c, x_all)
            wait_alone((mixed, CHUNKS))

            norm_all(1)
            route(1)
            for u in range(2):
                v.memset(convT[u][:, :, 0:TAPS - 1], 0.0)
            wait_alone((xn_moved[0], (2 * GROUPS + 1) * 16), (xn_moved[1], (2 * GROUPS + 1) * 16))
            chain(0)
            with dve.Fori(0, BLOCK_PAIRS[-1]) as i:
                L.enter(i, LINKS_CHAIN)
                chain(i + 1)
            L.leave(BLOCK_PAIRS[-1])
            done = 0
            for pair in range(BLOCK_PAIRS[-1] + 1, PAIRS):
                def point(n):
                    nonlocal done
                    upto = LATE_MIXES[(pair - BLOCK_PAIRS[-1] - 1) * 3 + n]
                    for c in range(done, upto):
                        finish(c)
                    done = upto
                chain(pair, point)
            for c in range(done, CHUNKS):
                finish(c)


def _packs(a):
    f32 = np.float32
    g = {k: np.asarray(v) for k, v in a.items()}
    small = np.zeros((P, S_END), f32)

    def put(at, m):
        small[:m.shape[0], at:at + m.shape[1]] = m

    put(S_WQ, g["L0_attn_Wq"])
    put(S_GATE0, g["L0_ffn_gate_w"])
    put(S_WOUT, g["L0_attn_Wout"])
    put(S_GATE1, g["L1_ffn_gate_w"].T)
    conv = g["L1_attn_conv_w"]
    width = conv.shape[1]
    for k in range(TAPS):
        for o in range(D // width):
            small[o * width:(o + 1) * width, S_CONV + k * D + o * width:S_CONV + k * D + (o + 1) * width] = \
                conv[o * width:(o + 1) * width, :, k].T
    put(S_WQ1, g["L1_attn_Wq"].T)
    put(S_WK1, g["L1_attn_Wk"].T)
    put(S_WV1, g["L1_attn_Wv"].T)
    put(S_WB, g["L1_attn_Wb"].T)
    put(S_WU, g["L1_attn_Wu"].T.reshape(BOOM, P, D).transpose(1, 0, 2).reshape(P, BOOM * D))
    put(S_ID, np.eye(P, dtype=f32))
    put(S_IOTA, np.tile(np.arange(BLOCKS, dtype=f32), (P, 1)))
    put(S_COUNT, np.tile(np.arange(1, SEQ + 1, dtype=f32), (P, 1)))

    put(S_BEFORE, np.triu(np.ones((P, P), f32), 1))
    put(S_PAST, (SLOTS + np.arange(E0)[None] * P + np.arange(P)[:, None]).astype(f32))

    narrow = np.zeros((LAT, N_END), f32)

    def kv_order(m):
        m = m.reshape(m.shape[0], H, 2, DH)
        return np.concatenate([m[:, :, 0].reshape(-1, D), m[:, :, 1].transpose(0, 2, 1).reshape(-1, D)], axis=1)

    narrow[:, N_WDOWN:N_WDOWN + D] = g["L0_attn_Wdown"].T
    narrow[:, N_WUP:N_WUP + 2 * D] = kv_order(g["L0_attn_Wup"])
    narrow[:, N_BDOWN] = g["L0_attn_bdown"]
    narrow[0, N_BUP:N_BUP + 2 * D] = kv_order(g["L0_attn_bup"][None])[0]
    narrow[0, N_BQ:N_BQ + D] = g["L0_attn_bq"]
    narrow[0, N_CONVB:N_CONVB + D] = g["L1_attn_conv_b"]
    narrow[0:E1, N_B12:N_B12 + F] = g["L1_ffn_b1"]
    narrow[0:E1, N_B12 + F:N_END] = g["L1_ffn_b2"]

    cols = np.stack(
        [g["L1_attn_" + n] for n in ("ln_conv_g", "ln_conv_b", "ln_attn_g", "ln_attn_b", "ln_boom_g", "ln_boom_b",
                                     "bq", "bk", "bv")]
        + [g["L0_attn_bout"], g["L1_attn_bu"], np.arange(P, dtype=f32)] + list(g["L1_attn_bb"].reshape(BOOM, P)), axis=1)

    def with_shared(e, s):
        return np.concatenate([g[e], g[s][None]], axis=0)

    def halves(m):
        return m.reshape(m.shape[0], HALVES, P, D).transpose(2, 0, 1, 3)

    return {
        "x": g["L0_attn_x"].reshape(-1, D),
        "small": small,
        "narrow": narrow,
        "cols": cols,
        "wgu0": np.concatenate([with_shared("L0_ffn_w_gate", "L0_ffn_ws_gate"),
                                with_shared("L0_ffn_w_up", "L0_ffn_ws_up")], axis=2).transpose(1, 0, 2),
        "wd0": halves(with_shared("L0_ffn_w_down", "L0_ffn_ws_down")),
        "w1": g["L1_ffn_w1"].transpose(1, 0, 2),
        "w2": halves(g["L1_ffn_w2"]),
    }


def kernel(**inputs):
    import concourse.bacc as _bacc
    from concourse.bass_utils import run_bass_kernel_spmd as _run

    shape = np.asarray(inputs["L0_attn_x"]).shape
    arrays = {k: np.ascontiguousarray(v) for k, v in _packs(inputs).items()}
    nc = _bacc.Bacc("TRN2", target_bir_lowering=False, num_devices=1)
    args = {k: nc.dram_tensor(k, a.shape, mybir.dt.from_np(a.dtype), kind="ExternalInput").ap()
            for k, a in arrays.items()}
    out = nc.dram_tensor("out", arrays["x"].shape, FP32, kind="ExternalOutput").ap()
    two_layers(nc, **args, out=out)
    r = _run(nc, [arrays], core_ids=[0])
    return r.results[0]["out"].reshape(shape)
```
